# Optimizing a Trainium2 kernel written in Bass

```python
import numpy as np
import jax
import jax.numpy as jnp

def _softmax(x, axis=-1):
    return jax.nn.softmax(x, axis=axis)

def _gelu(x):
    return jax.nn.gelu(x, approximate=True)

def _silu(x):
    return jax.nn.silu(x)

def _sigmoid(x):
    return jax.nn.sigmoid(x)

def _layernorm(x, axis=-1, eps=1e-05):
    m = jnp.mean(x, axis=axis, keepdims=True)
    v = jnp.var(x, axis=axis, keepdims=True)
    return (x - m) / jnp.sqrt(v + eps)

def _scatter_add(tgt, idx, src, axis=0):
    return tgt.at[idx].add(src)

def _segment_sum(src, seg, n):
    return jax.ops.segment_sum(src, seg, n)
kernel_name = 'mk_perceiver_d1_seqx_r4_7f30c4'

def setup_inputs(seed: int=0):
    np.random.seed(seed)
    _w = jnp.asarray

    def _rec_inputs():
        import jax
        import jax.numpy as jnp
        _rk = jax.random.key(seed)
        x = -0.0005207 + 1.001 * jax.random.normal(jax.random.fold_in(_rk, 1), (16, 64, 256), jnp.float32)
        _lenS = 64 - jax.random.randint(jax.random.fold_in(_rk, 7), (16,), 0, max(1, 64 // 4) + 1, jnp.int32)
        _lenS2 = 1024 - jax.random.randint(jax.random.fold_in(_rk, 8), (16,), 0, max(1, 1024 // 4) + 1, jnp.int32)
        _ctx_1024P = jax.random.normal(jax.random.fold_in(_rk, 11), (16, 16, 256), jnp.float32)
        _ctx_1024c = jax.random.dirichlet(jax.random.fold_in(_rk, 511), 0.3 * jnp.ones((16,), jnp.float32), (16, 1024))
        _ctx_1024t = jnp.einsum('bsk,bkd->bsd', _ctx_1024c, _ctx_1024P)
        _ctx_1024t = _ctx_1024t * jax.lax.rsqrt(jnp.mean(jnp.square(_ctx_1024t)) + 1e-12) * 0.953939
        ctx_1024 = -1.52775e-05 + 0.999936 * (_ctx_1024t + 0.3 * jax.random.normal(jax.random.fold_in(_rk, 611), (16, 1024, 256), jnp.float32))
        return (x, ctx_1024)
    x, ctx_1024 = _rec_inputs()

    def _L0_xattn_setup():
        import jax, jax.numpy as jnp
        import numpy as np
        DIM = 256
        HEADS = 16
        DHEAD = 64
        INNER = HEADS * DHEAD
        EPS = 1e-05

        def layer_norm(x, g, b):
            mu = jnp.mean(x, axis=-1, keepdims=True)
            var = jnp.mean(jnp.square(x - mu), axis=-1, keepdims=True)
            return (x - mu) * jax.lax.rsqrt(var + EPS) * g + b

        def apply_rope(x, cos, sin):
            d2 = x.shape[-1] // 2
            x1, x2 = (x[..., :d2], x[..., d2:])
            return jnp.concatenate([x1 * cos - x2 * sin, x2 * cos + x1 * sin], axis=-1)
        key = jax.random.key(seed)
        ks = jax.random.split(key, 10)
        B, N, S = (8, 64, 1024)
        latents = jax.random.normal(ks[0], (B, N, DIM), dtype=jnp.float32)
        context = jax.random.normal(ks[1], (B, S, DIM), dtype=jnp.float32)
        cos = jax.random.uniform(ks[2], (S, DHEAD // 2), dtype=jnp.float32)
        sin = jax.random.uniform(ks[3], (S, DHEAD // 2), dtype=jnp.float32)
        init = lambda k, shp, fan_in: jax.random.normal(k, shp, dtype=jnp.float32) / np.sqrt(fan_in)
        return {'latents': latents, 'context': context, 'cos': cos, 'sin': sin, 'ln_lat_g': jnp.ones((DIM,), jnp.float32), 'ln_lat_b': jnp.zeros((DIM,), jnp.float32), 'ln_ctx_g': jnp.ones((DIM,), jnp.float32), 'ln_ctx_b': jnp.zeros((DIM,), jnp.float32), 'Wq': init(ks[4], (DIM, INNER), DIM), 'Wkv': init(ks[5], (DIM, 2 * INNER), DIM), 'Wo': init(ks[6], (INNER, DIM), INNER), 'bo': jnp.zeros((DIM,), jnp.float32)}
    _L0_xattn_all = _L0_xattn_setup()
    _L0_xattn_in = {k: v for k, v in _L0_xattn_all.items() if k in ('cos', 'sin', 'ln_lat_g', 'ln_lat_b', 'ln_ctx_g', 'ln_ctx_b', 'Wq', 'Wkv', 'Wo', 'bo')}
    del _L0_xattn_all

    def _L0_attn_setup():
        import jax, jax.numpy as jnp
        import numpy as np
        B, T, C = (2, 512, 256)
        H, M = (16, 64)
        D = C // H
        key = jax.random.key(seed)
        ks = jax.random.split(key, 6)
        x = jax.random.normal(ks[0], (B, T, C), dtype=jnp.float32)
        Wqkv = jax.random.normal(ks[1], (3 * C, C), dtype=jnp.float32) / np.sqrt(C)
        bqkv = jax.random.normal(ks[2], (3 * C,), dtype=jnp.float32) * 0.02
        Wout = jax.random.normal(ks[3], (C, C), dtype=jnp.float32) / np.sqrt(C)
        bout = jax.random.normal(ks[4], (C,), dtype=jnp.float32) * 0.02
        proj = jax.random.normal(ks[5], (H, D, M), dtype=jnp.float32) / np.sqrt(D)
        return {'x': x, 'Wqkv': Wqkv, 'bqkv': bqkv, 'Wout': Wout, 'bout': bout, 'proj': proj}
    _L0_attn_all = _L0_attn_setup()
    _L0_attn_in = {k: v for k, v in _L0_attn_all.items() if k in ('Wqkv', 'bqkv', 'Wout', 'bout', 'proj')}
    del _L0_attn_all

    def _L0_ffn_setup():
        import jax, jax.numpy as jnp
        import numpy as np
        D_MODEL, D_FF, N_EXPERTS, TOP_K = (256, 1024, 8, 2)
        key = jax.random.key(seed)
        k0, k1, k2, k3 = jax.random.split(key, 4)
        x = jax.random.normal(k0, (2, 512, D_MODEL), dtype=jnp.float32)
        Wg = jax.random.normal(k1, (D_MODEL, N_EXPERTS), dtype=jnp.float32) * 0.02
        W1 = jax.random.normal(k2, (N_EXPERTS, D_MODEL, D_FF), dtype=jnp.float32) * 0.02
        b1 = jnp.zeros((N_EXPERTS, D_FF), dtype=jnp.float32)
        W2 = jax.random.normal(k3, (N_EXPERTS, D_FF, D_MODEL), dtype=jnp.float32) * 0.02
        b2 = jnp.zeros((N_EXPERTS, D_MODEL), dtype=jnp.float32)
        return {'x': x, 'Wg': Wg, 'W1': W1, 'b1': b1, 'W2': W2, 'b2': b2}
    _L0_ffn_all = _L0_ffn_setup()
    _L0_ffn_in = {k: v for k, v in _L0_ffn_all.items() if k in ('Wg', 'W1', 'b1', 'W2', 'b2')}
    del _L0_ffn_all
    return {'x': x, 'ctx_1024': ctx_1024, 'L0_xattn_cos': _L0_xattn_in['cos'], 'L0_xattn_sin': _L0_xattn_in['sin'], 'L0_xattn_ln_lat_g': _L0_xattn_in['ln_lat_g'], 'L0_xattn_ln_lat_b': _L0_xattn_in['ln_lat_b'], 'L0_xattn_ln_ctx_g': _L0_xattn_in['ln_ctx_g'], 'L0_xattn_ln_ctx_b': _L0_xattn_in['ln_ctx_b'], 'L0_xattn_Wq': _L0_xattn_in['Wq'], 'L0_xattn_Wkv': _L0_xattn_in['Wkv'], 'L0_xattn_Wo': _L0_xattn_in['Wo'], 'L0_xattn_bo': _L0_xattn_in['bo'], 'L0_attn_Wqkv': _L0_attn_in['Wqkv'], 'L0_attn_bqkv': _L0_attn_in['bqkv'], 'L0_attn_Wout': _L0_attn_in['Wout'], 'L0_attn_bout': _L0_attn_in['bout'], 'L0_attn_proj': _L0_attn_in['proj'], 'L0_ffn_Wg': _L0_ffn_in['Wg'], 'L0_ffn_W1': _L0_ffn_in['W1'], 'L0_ffn_b1': _L0_ffn_in['b1'], 'L0_ffn_W2': _L0_ffn_in['W2'], 'L0_ffn_b2': _L0_ffn_in['b2']}

def reference(x, ctx_1024, L0_xattn_cos, L0_xattn_sin, L0_xattn_ln_lat_g, L0_xattn_ln_lat_b, L0_xattn_ln_ctx_g, L0_xattn_ln_ctx_b, L0_xattn_Wq, L0_xattn_Wkv, L0_xattn_Wo, L0_xattn_bo, L0_attn_Wqkv, L0_attn_bqkv, L0_attn_Wout, L0_attn_bout, L0_attn_proj, L0_ffn_Wg, L0_ffn_W1, L0_ffn_b1, L0_ffn_W2, L0_ffn_b2):
    import jax
    import jax.numpy as jnp

    def _L0_xattn_ref(latents, context, cos, sin, ln_lat_g, ln_lat_b, ln_ctx_g, ln_ctx_b, Wq, Wkv, Wo, bo):
        import jax, jax.numpy as jnp
        import numpy as np
        DIM = 256
        HEADS = 16
        DHEAD = 64
        INNER = HEADS * DHEAD
        EPS = 1e-05

        def layer_norm(x, g, b):
            mu = jnp.mean(x, axis=-1, keepdims=True)
            var = jnp.mean(jnp.square(x - mu), axis=-1, keepdims=True)
            return (x - mu) * jax.lax.rsqrt(var + EPS) * g + b

        def apply_rope(x, cos, sin):
            d2 = x.shape[-1] // 2
            x1, x2 = (x[..., :d2], x[..., d2:])
            return jnp.concatenate([x1 * cos - x2 * sin, x2 * cos + x1 * sin], axis=-1)
        b, n, _ = latents.shape
        s = context.shape[1]
        lat = layer_norm(latents, ln_lat_g, ln_lat_b)
        ctx = layer_norm(context, ln_ctx_g, ln_ctx_b)
        q = (lat @ Wq).reshape(b, n, HEADS, DHEAD).transpose(0, 2, 1, 3)
        kv = ctx @ Wkv
        k, v = jnp.split(kv, 2, axis=-1)
        k = k.reshape(b, s, HEADS, DHEAD).transpose(0, 2, 1, 3)
        v = v.reshape(b, s, HEADS, DHEAD).transpose(0, 2, 1, 3)
        k = apply_rope(k, cos[None, None], sin[None, None])
        scale = DHEAD ** (-0.5)
        attn = jnp.einsum('bhnd,bhsd->bhns', q, k) * scale
        attn = jnp.clip(attn, -11.0, 11.0)
        attn = jax.nn.softmax(attn, axis=-1)
        out = jnp.einsum('bhns,bhsd->bhnd', attn, v)
        out = out.transpose(0, 2, 1, 3).reshape(b, n, INNER)
        return out @ Wo + bo

    def _L0_attn_ref(x, Wqkv, bqkv, Wout, bout, proj):
        import jax, jax.numpy as jnp
        import numpy as np
        B, T, C = (2, 512, 256)
        H, M = (16, 64)
        D = C // H
        b, t, c = x.shape
        h, d, m = proj.shape
        qkv = x @ Wqkv.T + bqkv
        q, k, v = jnp.split(qkv, 3, axis=-1)
        to_heads = lambda z: z.reshape(b, t, h, d).transpose(0, 2, 1, 3)
        q, k, v = (to_heads(q), to_heads(k), to_heads(v))
        qf, kf, vf = (q.astype(jnp.float32), k.astype(jnp.float32), v.astype(jnp.float32))
        pf = proj.astype(jnp.float32)
        q_prime = jax.nn.relu(jnp.einsum('bhtd,hdm->bhtm', qf, pf))
        k_prime = jax.nn.relu(jnp.einsum('bhtd,hdm->bhtm', kf, pf))
        k_cumsum = jnp.cumsum(k_prime, axis=2)
        kv_prod = jnp.einsum('bhtm,bhtd->bhtmd', k_prime, vf)
        kv_cumsum = jnp.cumsum(kv_prod, axis=2)
        context = jnp.einsum('bhtm,bhtmd->bhtd', q_prime, kv_cumsum)
        norm = jnp.einsum('bhtm,bhtm->bht', q_prime, k_cumsum)
        out = context / (norm[..., None] + 1e-06)
        out = out.astype(x.dtype).transpose(0, 2, 1, 3).reshape(b, t, c)
        return out @ Wout.T + bout

    def _L0_ffn_ref(x, Wg, W1, b1, W2, b2):
        import jax, jax.numpy as jnp
        import numpy as np
        D_MODEL, D_FF, N_EXPERTS, TOP_K = (256, 1024, 8, 2)
        B = x.shape[:-1]
        xs = x.reshape(-1, x.shape[-1])
        T = xs.shape[0]
        gate_logits = xs @ Wg
        weights, sel = jax.lax.top_k(gate_logits, TOP_K)
        weights = jax.nn.softmax(weights.astype(jnp.float32), axis=1).astype(x.dtype)
        h = jax.nn.relu(jnp.einsum('td,edf->etf', xs, W1) + b1[:, None, :])
        out_e = jnp.einsum('etf,efd->etd', h, W2) + b2[:, None, :]
        tok = jnp.arange(T)
        picked = out_e[sel, tok[:, None]]
        out = jnp.einsum('tk,tkd->td', weights, picked)
        return out.reshape(*B, x.shape[-1])
    x = x + _L0_xattn_ref(_layernorm(x, axis=-1), ctx_1024, L0_xattn_cos, L0_xattn_sin, L0_xattn_ln_lat_g, L0_xattn_ln_lat_b, L0_xattn_ln_ctx_g, L0_xattn_ln_ctx_b, L0_xattn_Wq, L0_xattn_Wkv, L0_xattn_Wo, L0_xattn_bo)
    x = x + _L0_attn_ref(_layernorm(x, axis=-1), L0_attn_Wqkv, L0_attn_bqkv, L0_attn_Wout, L0_attn_bout, L0_attn_proj)
    x = x + _L0_ffn_ref(_layernorm(x, axis=-1), L0_ffn_Wg, L0_ffn_W1, L0_ffn_b1, L0_ffn_W2, L0_ffn_b2)
    return x

_drawn_inputs = setup_inputs


def setup_inputs(seed=0):
    import zlib

    import numpy as np

    out = dict(_drawn_inputs(seed))
    spreads = {'L0_xattn_ln_lat_g': (1.0, 0.6),
     'L0_xattn_ln_lat_b': (0.0, 0.44),
     'L0_xattn_ln_ctx_g': (1.0, 0.2),
     'L0_xattn_ln_ctx_b': (0.0, 0.1),
     'L0_xattn_bo': (0.0, 0.1),
     'L0_ffn_b1': (0.0, 0.318),
     'L0_ffn_b2': (0.0, 0.1)}
    factors = {'L0_xattn_cos': 4.66, 'L0_xattn_sin': 4.359, 'L0_attn_bout': 3.288}
    for name, (base, spread) in spreads.items():
        noise = np.random.default_rng([zlib.crc32(name.encode()), seed]).standard_normal(out[name].shape)
        drawn = base * np.exp(spread * noise) if base else spread * noise
        out[name] = jnp.asarray(drawn.astype(out[name].dtype))
    for name, factor in factors.items():
        out[name] = (out[name] * factor).astype(out[name].dtype)
    return out
```

```python
from contextlib import ExitStack

import numpy as np
import concourse.bass as bass
from concourse import mybir

F32 = mybir.dt.float32
F32R = mybir.dt.float32r
U32 = mybir.dt.uint32
ALU = mybir.AluOpType
ACT = mybir.ActivationFunctionType

P = 128
B, N, D = 16, 64, 256
S = 1024
H, DH = 16, 64
HALF = DH // 2
INNER = H * DH
KC = D // P
PAIRS = H // 2
ST = S // P
TOK = B * N
TT = TOK // P
STEPS = B * PAIRS
BODY = 2 * PAIRS
TRIPS = STEPS // BODY
TILES = B * ST
EPS = 1e-5
CLIP = 11.0
SCALE = DH ** -0.5
LOW, HIGH = float(np.exp(-CLIP)), float(np.exp(CLIP))


F = 1024
FT = F // P
E = 8
AH, AD, AM = 16, 16, 64
CH = TOK // 2


def build(nc, x, ctx_1024, cos, sin, lat_g, lat_b, ctx_g, ctx_b, Wq, Wkv, Wo, bo, Wqkv, bqkv, Wout, bout, proj,
          Wg, W1, b1, W2, b2, out):
    with ExitStack() as ctx:
        def sem(name):
            return ctx.enter_context(nc.semaphore(name))

        def sb(name, shape, dt=F32, scope=ctx):
            return scope.enter_context(nc.sbuf_tensor(name, shape, dt))

        ident = sb("ident", [P, P])
        consts = sb("consts", [P, 8])
        vecs = sb("vecs", [P, 4, KC])
        bias = sb("bias", [P, 3, PAIRS])
        bst = sb("bst", [P, 2, 6])
        mv = sb("mv", [P, 2, 2])
        ve = sb("ve", [P, 2])
        rstd = sb("rstd", [P, 2])
        rz = sb("rz", [P, 2])
        raw = sb("raw", [P, 2, ST, D])
        wo = sb("wo", [P, PAIRS, D])
        xattn = ctx.enter_context(ExitStack())
        wk_hi = sb("wk_hi", [P, KC, INNER], F32R, xattn)
        wk_lo = sb("wk_lo", [P, KC, INNER], F32R, xattn)
        wv = sb("wv", [P, KC, INNER], F32, xattn)
        ctab = sb("ctab", [P, S], F32, xattn)
        stab = sb("stab", [P, S], F32, xattn)
        qbd = sb("qbd", [P, 2, PAIRS, P], F32, xattn)
        ct_hi = sb("ct_hi", [P, 2, KC, S], F32R, xattn)
        ct_lo = sb("ct_lo", [P, 2, KC, S], F32R, xattn)
        x_hi = sb("x_hi", [P, 2, ST, D + 2], F32R, xattn)
        x_lo = sb("x_lo", [P, 2, ST, D], F32R, xattn)
        with ExitStack() as first:
            vec_rows = sb("vec_rows", [4 * KC, P], F32, first)
            latT = sb("latT", [P, KC, TOK], F32, first)
            wq_raw = sb("wq_raw", [P, KC, INNER], F32, first)
            wq_p = sb("wq_p", [P, KC, INNER], F32, first)
            wk_raw = sb("wk_raw", [P, KC, INNER], F32, first)
            wk_p = sb("wk_p", [P, KC, INNER], F32, first)
            cs_raw = sb("cs_raw", [P, 2, ST, HALF], F32, first)
        ksw = sb("ksw", [P, 2, S], F32, xattn)
        ku = sb("ku", [P, 2, S], F32, xattn)
        kr = sb("kr", [P, 2, S], F32, xattn)
        pr = sb("pr", [P, S], F32, xattn)
        p_hi = sb("p_hi", [P, 2, S], F32R, xattn)
        p_lo = sb("p_lo", [P, 2, S], F32R, xattn)
        zn = sb("zn", [P, D], F32, xattn)
        zts = sb("zts", [P, D], F32, xattn)
        xl = raw[:, 1]
        bo_all = raw[:, 1, 0]
        crep = qbd

        qo = sb("qo", [P, PAIRS, TOK], F32, xattn)
        xattn.close()
        wqkv_raw = raw[:, 1, 1:7]
        lin = ctx.enter_context(ExitStack())
        mask = sb("mask", [P, P], F32, lin)
        st6 = sb("st6", [P, 2, TT, 6], F32, lin)
        mom = sb("mom", [P, 2, TT, 2], F32, lin)
        vpe = sb("vpe", [P, 2, TT], F32, lin)
        rsd = sb("rsd", [P, 2, TT], F32, lin)
        cvec = sb("cvec", [P, 2], F32, lin)
        vec_rows2 = sb("vec_rows2", [E * FT + 4, P], F32, lin)
        vecs2 = sb("vecs2", [P, E * FT + 4], F32, lin)
        b1_now = sb("b1_now", [P, 2, FT], F32, lin)
        v_bias = sb("v_bias", [P, D], F32, lin)
        bout_all = sb("bout_all", [P, D], F32, lin)
        wg = sb("wg", [P, KC, E], F32, lin)
        b2_rows = sb("b2_rows", [E, D], F32, lin)
        iota_e = sb("iota_e", [P, E], F32, lin)
        logit = sb("logit", [P, TT, E], F32, lin)
        top = sb("top", [P, TT, 8], F32, lin)
        top_at = sb("top_at", [P, TT, 8], U32, lin)
        top_f = sb("top_f", [P, TT, 2], F32, lin)
        gate = sb("gate", [P, 4, TT], F32, lin)
        pick = sb("pick", [P, 2, TT, E], F32, lin)
        comb = sb("comb", [P, TT, E], F32, lin)
        combT = sb("combT", [E, TOK], F32, lin)
        x_hiT = sb("x_hiT", [P, KC, TOK], F32R, lin)
        x_loT = sb("x_loT", [P, KC, TOK], F32R, lin)
        w1_raw = sb("w1_raw", [P, KC, F], F32, lin)
        with ExitStack() as attn:
            wqkvT = sb("wqkvT", [P, KC, 3 * D], F32, attn)
            wout_raw = sb("wout_raw", [P, KC, D], F32, attn)
            woutT = sb("woutT", [P, KC, D], F32, attn)
            feat_w = sb("feat_w", [P, AH // 2, P], F32, attn)
            xnT = sb("xnT", [P, KC, TOK], F32, attn)
            qkT = sb("qkT", [P, 4, TOK], F32, attn)
            vaug = sb("vaug", [P, TT, AH, AD + 1], F32, attn)
            am = sb("am", [P, 2, 4, P], F32, attn)
            rec = sb("rec", [P, 2, 2, AH], F32, attn)
            att = sb("att", [P, 2, D], F32, attn)
            attT = sb("attT", [P, 2, D], F32, attn)
            xn = sb("xn", [P, 2, D], F32, attn)
            xfT = sb("xfT", [P, 2, D], F32, attn)
            feat = sb("feat", [P, 2, AH // 2, TOK], F32, attn)
        w2_raw = sb("w2_raw", [P, FT, D], F32, lin)
        w1_hi = sb("w1_hi", [P, 2, KC, F], F32R, lin)
        w1_lo = sb("w1_lo", [P, 2, KC, F], F32R, lin)
        w2_hi = sb("w2_hi", [P, 2, FT, D], F32R, lin)
        w2_lo = sb("w2_lo", [P, 2, FT, D], F32R, lin)
        hid = sb("hid", [P, 4, CH], F32, lin)
        h_hi = sb("h_hi", [P, FT, TOK], F32R, lin)
        h_lo = sb("h_lo", [P, FT, TOK], F32R, lin)

        bank = ctx.enter_context(nc.psum_tensor("bank", [P, 8, 512], F32))
        flat = bank[:].rearrange("p a b -> p (a b)")
        psK, psS = flat[:, 0:1024], flat[:, 1024:2048]
        psZ, psT, psZT, psO = bank[:, 4], bank[:, 5], bank[:, 6], bank[:, 7]

        x_ld, wq_ld, wk_ld, wv_ld, wo_ld, cs_ld, vec_ld = (sem(n) for n in ("x_ld", "wq_ld", "wk_ld", "wv_ld", "wo_ld", "cs_ld", "vec_ld"))
        ctx_ld = [sem(f"ctx_ld{i}") for i in range(2)]
        vec2_ld, lw_ld, misc_ld, proj_ld, w1_ld, w2_ld = (sem(n) for n in ("vec2_ld", "lw_ld", "misc_ld", "proj_ld", "w1_ld", "w2_ld"))
        lin_consts, feat_w_zero, mask_done = sem("lin_consts"), sem("feat_w_zero"), sem("mask_done")
        lw_ps, lw_done, vec2_ps, vec2_done = sem("lw_ps"), sem("lw_done"), sem("vec2_ps"), sem("vec2_done")
        l_bn, l_stats, l_var, l_rstd, xn_done = (sem(n) for n in ("l_bn", "l_stats", "l_var", "l_rstd", "xn_done"))
        xnT_ps, xnT_done, v_ps, v_done, qk_ps, qk_done = (sem(n) for n in ("xnT_ps", "xnT_done", "v_ps", "v_done", "qk_ps", "qk_done"))
        f_ps, f_act, f_dve, am_ps, am_done, c_ps, rec_done, att_done = (sem(n) for n in ("f_ps", "f_act", "f_dve", "am_ps", "am_done", "c_ps", "rec_done", "att_done"))
        cq_ps, b1_done = sem("cq_ps"), sem("b1_done")
        den_done, attT_ps, attT_done, w_ps, x1b_done, x2_done = (sem(n) for n in ("den_done", "attT_ps", "attT_done", "w_ps", "x1b_done", "x2_done"))
        xfT_ps, xfT_done, x_hiT_done, x_loT_done, logit_ps, logit_done = (sem(n) for n in ("xfT_ps", "xfT_done", "x_hiT_done", "x_loT_done", "logit_ps", "logit_done"))
        top_done, gap_done, gap_exp, den2_done, gate_done, top_f_done = (sem(n) for n in ("top_done", "gap_done", "gap_exp", "den2_done", "gate_done", "top_f_done"))
        pick_done, comb_done, combT_ps, combT_done, b2_ps, acc_b2 = (sem(n) for n in ("pick_done", "comb_done", "combT_ps", "combT_done", "b2_ps", "acc_b2"))
        w_hi_done, w_lo_done, h_ps, relu_done, h_hi_done, h_lo_done, e_ps, acc_done = (sem(n) for n in ("w_hi_done", "w_lo_done", "h_ps", "relu_done", "h_hi_done", "h_lo_done", "e_ps", "acc_done"))
        vec_ps, vec_done = sem("vec_ps"), sem("vec_done")
        ident_done, consts_done, ones_done = sem("ident_done"), sem("consts_done"), sem("ones_done")
        xl_stats, xl_var, xl_rstd, xl_norm = sem("xl_stats"), sem("xl_var"), sem("xl_rstd"), sem("xl_norm")
        latT_ps, latT_done = sem("latT_ps"), sem("latT_done")
        wq_perm, wk_perm, wk_hi_done, wk_lo_done, wv_done = sem("wq_perm"), sem("wk_perm"), sem("wk_hi_done"), sem("wk_lo_done"), sem("wv_done")
        crep_done, tab_ps, tab_done = sem("crep_done"), sem("tab_ps"), sem("tab_done")
        bias_ps, bias_done = sem("bias_ps"), sem("bias_done")
        q_ps, q_act, q_dve = sem("q_ps"), sem("q_act"), sem("q_dve")
        bn_done, stats_done, var_done, rstd_done, xhat_done = sem("bn_done"), sem("stats_done"), sem("var_done"), sem("rstd_done"), sem("xhat_done")
        xT_ps, ct_hi_done, ct_lo_done, x_hi_done, x_lo_done = sem("xT_ps"), sem("ct_hi_done"), sem("ct_lo_done"), sem("x_hi_done"), sem("x_lo_done")
        k_ps, k_swapped, ku_done, kv_done, kr_done = sem("k_ps"), sem("k_swapped"), sem("ku_done"), sem("kv_done"), sem("kr_done")
        qbd_done = sem("qbd_done")
        s_ps, exp_done, clamp_done, p_hi_done, p_lo_done = sem("s_ps"), sem("exp_done"), sem("clamp_done"), sem("p_hi_done"), sem("p_lo_done")
        z_ps, rz_done, zn_done, zt_ps, zts_done, o_ps, o_done = (sem(n) for n in ("z_ps", "rz_done", "zn_done", "zt_ps", "zts_done", "o_ps", "o_done"))
        y_ps, y_done, out_st, bo_ld, x2_ld, xbo_done = (sem(n) for n in ("y_ps", "y_done", "out_st", "bo_ld", "x2_ld", "xbo_done"))

        def wait(eng, s, trip, count):
            if isinstance(trip, int):
                if trip * BODY + count > 0:
                    eng.wait_ge(s, trip * BODY + count)
            else:
                eng.wait_ge(s, trip * BODY + count)

        def there(trip, j):
            return not isinstance(trip, int) or 0 <= trip * BODY + j < STEPS

        def trips(eng, step):
            for j in range(0, BODY):
                step(0, j)
            with eng.Fori(1, TRIPS - 1) as trip:
                for j in range(BODY):
                    step(trip, j)
            for j in range(BODY + 2):
                step(TRIPS - 1, j)

        def place(j):
            return (j // PAIRS) % 2, j % PAIRS

        block = ctx.enter_context(nc.Block())

        @block.sync
        def _(sp):
            def ctx_rows(b):
                return ctx_1024[b].rearrange("(p t) d -> p t d", t=ST)

            sp.dma_start(xl, x.rearrange("b n d -> (b n) d").rearrange("(t p) d -> p t d", p=P)).then_inc(x_ld, 16)
            sp.dma_start(raw[:, 0], ctx_rows(0)).then_inc(ctx_ld[0], 16)
            sp.dma_start(cs_raw[:, 0], cos.rearrange("(p t) i -> p t i", t=ST)).then_inc(cs_ld, 16)
            sp.dma_start(cs_raw[:, 1], sin.rearrange("(p t) i -> p t i", t=ST)).then_inc(cs_ld, 16)
            for i, v in enumerate((lat_g, lat_b, ctx_g, ctx_b)):
                sp.dma_start(vec_rows[i * KC:(i + 1) * KC, :], v.rearrange("(k p) -> k p", p=P)).then_inc(vec_ld, 16)
            kv = Wkv.rearrange("(k p) n -> p k n", p=P)
            sp.dma_start(wq_raw[:], Wq.rearrange("(k p) n -> p k n", p=P)).then_inc(wq_ld, 16)
            sp.dma_start(wk_raw[:], kv[:, :, 0:INNER]).then_inc(wk_ld, 16)
            sp.dma_start(wv[:], kv[:, :, INNER:2 * INNER]).then_inc(wv_ld, 16)
            sp.dma_start(wo[:], Wo.rearrange("(g p) n -> p g n", p=P)).then_inc(wo_ld, 16)
            sp.wait_ge(latT_ps, TT)
            sp.dma_start(raw[:, 1], ctx_rows(1)).then_inc(ctx_ld[1], 16)
            with sp.Fori(1, TRIPS) as trip:
                for p in range(2):
                    wait(sp, xT_ps, trip, ST * (p - 1))
                    wait(sp, x_lo_done, trip, ST * (p - 1))
                    sp.dma_start(raw[:, p], ctx_1024[bass.ds(trip * 2 + p, 1)].rearrange("o (p t) d -> p (o t) d", t=ST)).then_inc(ctx_ld[p], 16)
            sp.wait_ge(x_lo_done, TILES)
            sp.wait_ge(xT_ps, TILES)
            sp.dma_start(bo_all, bo.partition_broadcast(P)).then_inc(bo_ld, 16)
            sp.dma_start(raw[:, 0], x.rearrange("b n d -> (b n) d").rearrange("(t p) d -> p t d", p=P)).then_inc(x2_ld, 16)
            sp.dma_start(wqkv_raw, Wqkv.rearrange("(r p) c -> p r c", p=P)).then_inc(lw_ld, 16)
            sp.wait_ge(o_ps, STEPS)
            sp.dma_start(vec_rows2[0:E * FT, :], b1.rearrange("e (f p) -> (e f) p", p=P)).then_inc(vec2_ld, 16)
            sp.dma_start(vec_rows2[E * FT:, :], bqkv[0:2 * D].rearrange("(r p) -> r p", p=P)).then_inc(vec2_ld, 16)
            sp.dma_start(wout_raw[:], Wout.rearrange("(r p) c -> p r c", p=P)).then_inc(lw_ld, 16)
            sp.wait_ge(feat_w_zero, 1)
            for h in range(AH):
                r = h % 8 * AD
                sp.dma_start(feat_w[r:r + AD, h // 2, h % 2 * AM:(h % 2 + 1) * AM], proj[h]).then_inc(proj_ld, 16)
            sp.dma_start(v_bias[:], bqkv[2 * D:3 * D].partition_broadcast(P)).then_inc(misc_ld, 16)
            sp.dma_start(bout_all[:], bout.partition_broadcast(P)).then_inc(misc_ld, 16)
            sp.dma_start(wg[:], Wg.rearrange("(k p) e -> p k e", p=P)).then_inc(misc_ld, 16)
            sp.dma_start(b2_rows[:], b2).then_inc(misc_ld, 16)
            sp.dma_start(w1_raw[:], W1[0].rearrange("(k p) f -> p k f", p=P)).then_inc(w1_ld, 16)
            sp.wait_ge(attT_ps, TT)
            sp.wait_ge(logit_ps, TT)
            sp.dma_start(w2_raw[:], W2[0].rearrange("(f p) d -> p f d", p=P)).then_inc(w2_ld, 16)
            with sp.Fori(1, E) as e:
                sp.wait_ge(w_hi_done, e)
                sp.wait_ge(w_lo_done, e)
                sp.dma_start(w1_raw[:], W1[bass.ds(e, 1)].rearrange("o (k p) f -> p (o k) f", p=P)).then_inc(w1_ld, 16)
                sp.dma_start(w2_raw[:], W2[bass.ds(e, 1)].rearrange("o (f p) d -> p (o f) d", p=P)).then_inc(w2_ld, 16)
            for t in range(TT):
                sp.wait_ge(acc_done, (E - 1) * TT + t + 1)
                sp.dma_start(out.rearrange("b n d -> (b n) d")[t * P:(t + 1) * P, :], raw[:, 0, t]).then_inc(out_st, 16)
            sp.wait_ge(out_st, 16 * TT)

        @block.gpsimd
        def _(pool):
            pool.memset(ident[:], 1.0).then_inc(ident_done, 1)
            pool.wait_ge(ident_done, 1)
            pool.affine_select(out=ident[:], in_=ident[:], compare_op=ALU.is_equal, fill=0.0, base=0,
                               pattern=[[-1, P]], channel_multiplier=1).then_inc(ident_done, 1)

            pool.wait_ge(consts_done, 1)
            for r in range(2 * TT):
                pool.wait_ge(xl_stats, r + 1)
                pool.tensor_tensor(ve[:, r % 2:r % 2 + 1], mv[:, r % 2, 1:2], consts[:, 3:4], ALU.add).then_inc(xl_var, 1)
                pool.wait_ge(xl_var, r + 1)
                pool.tensor_tensor(rstd[:, r % 2:r % 2 + 1], ve[:, r % 2:r % 2 + 1], consts[:, 2:3], ALU.pow).then_inc(xl_rstd, 1)

            def step(trip, j):
                if there(trip, j + 1):
                    i = (j + 1) % 2
                    wait(pool, ku_done, trip, j + 2)
                    wait(pool, kv_done, trip, j + 2)
                    wait(pool, s_ps, trip, j)
                    pool.tensor_tensor(kr[:, i], ku[:, i], ksw[:, i], ALU.add).then_inc(kr_done, 1)
                if there(trip, j + 7):
                    b, t = place(j + 7)
                    wait(pool, x_hi_done, trip, j + 8)
                    pool.tensor_tensor(x_lo[:, b, t], raw[:, b, t], x_hi[:, b, t, 0:D].bitcast(F32), ALU.subtract).then_inc(x_lo_done, 1)
                if there(trip, j + 11):
                    i = (j + 11) % 2
                    wait(pool, stats_done, trip, j + 12)
                    pool.tensor_tensor(ve[:, i:i + 1], mv[:, i, 1:2], consts[:, 3:4], ALU.add).then_inc(var_done, 1)
                    wait(pool, var_done, trip, j + 12)
                    pool.tensor_tensor(rstd[:, i:i + 1], ve[:, i:i + 1], consts[:, 2:3], ALU.pow).then_inc(rstd_done, 1)

            for j in range(-11, 0):
                step(0, j)
            trips(pool, step)

            pool.wait_ge(o_ps, STEPS)
            pool.memset(mask[:], 1.0).then_inc(mask_done, 1)
            pool.memset(feat_w[:], 0.0).then_inc(feat_w_zero, 1)
            pool.memset(vaug[:, :, :, AD:AD + 1], 1.0)
            for e in range(E):
                pool.memset(iota_e[:, e:e + 1], float(e))
            pool.memset(cvec[:, 0:1], -0.5)
            pool.memset(cvec[:, 1:2], EPS).then_inc(lin_consts, 1)
            pool.wait_ge(mask_done, 1)
            pool.affine_select(out=mask[:], in_=mask[:], compare_op=ALU.is_ge, fill=0.0, base=0,
                               pattern=[[1, P]], channel_multiplier=-1).then_inc(mask_done, 1)
            pool.wait_ge(mask_done, 2)
            pool.memset(mask[0:N, N:P], 0.0).then_inc(mask_done, 1)
            pool.wait_ge(lin_consts, 1)
            for r in range(2 * TT):
                c, t = r // TT, r % TT
                pool.wait_ge(l_stats, r + 1)
                pool.tensor_tensor(vpe[:, c, t:t + 1], mom[:, c, t, 1:2], cvec[:, 1:2], ALU.add).then_inc(l_var, 1)
                pool.wait_ge(l_var, r + 1)
                pool.tensor_tensor(rsd[:, c, t:t + 1], vpe[:, c, t:t + 1], cvec[:, 0:1], ALU.pow).then_inc(l_rstd, 1)

            def low_parts(e, b):
                pool.wait_ge(w_hi_done, e + 1)
                pool.tensor_tensor(w1_lo[:, b], w1_raw[:], w1_hi[:, b].bitcast(F32), ALU.subtract)
                pool.tensor_tensor(w2_lo[:, b], w2_raw[:], w2_hi[:, b].bitcast(F32), ALU.subtract).then_inc(w_lo_done, 1)

            pool.wait_ge(x_loT_done, TT)
            with pool.Fori(0, E // 2) as pair:
                for b in range(2):
                    low_parts(pair * 2 + b, b)

        @block.scalar
        def _(act):
            act.wait_ge(vec_ps, 1)
            act.copy(vecs[:].rearrange("p v k -> p (v k)"), psZ[:, 0:4 * KC]).then_inc(vec_done, 1)
            act.wait_ge(vec_done, 1)
            for t in range(TT):
                act.wait_ge(latT_ps, t + 1)
                for k in range(KC):
                    last = act.activation(latT[:, k, t * P:(t + 1) * P], (psZT if t % 2 else psO)[:, k * P:(k + 1) * P], ACT.Identity,
                                          bias=vecs[:, 1, k:k + 1], scale=vecs[:, 0, k:k + 1])
                last.then_inc(latT_done, 1)
            act.wait_ge(wk_perm, 4)
            for k in range(KC):
                act.activation(wk_hi[:, k], wk_p[:, k], ACT.Identity, scale=vecs[:, 2, k:k + 1]).then_inc(wk_hi_done, 1)
            act.wait_ge(wv_ld, 16)
            act.wait_ge(bias_ps, 1)
            for k in range(KC):
                act.activation(wv[:, k], wv[:, k], ACT.Identity, scale=vecs[:, 2, k:k + 1]).then_inc(wv_done, 1)

            def step(trip, j):
                if there(trip, j + 1):
                    i = (j + 1) % 2
                    wait(act, k_ps, trip, j + 2)
                    wait(act, kr_done, trip, j)
                    act.copy(ksw[0:64, i], psK[64:128, :])
                    act.copy(ksw[64:128, i], psK[0:64, :]).then_inc(k_swapped, 1)
                if there(trip, j):
                    wait(act, s_ps, trip, j + 1)
                    wait(act, p_lo_done, trip, j)
                    act.activation(pr[:], psS, ACT.Exp, scale=SCALE).then_inc(exp_done, 1)
                if there(trip, j - 2):
                    wait(act, zt_ps, trip, j - 1)
                    wait(act, o_ps, trip, j - 2)
                    act.copy(zts[:], psZT[:, 0:D]).then_inc(zts_done, 1)
                if there(trip, j + 9):
                    b, t = place(j + 9)
                    wait(act, xT_ps, trip, j + 10)
                    if t == 0:
                        wait(act, k_ps, trip, j + 9 - PAIRS)
                    act.copy(ct_hi[:, b, :, t * P:(t + 1) * P], psT[:, 0:D].rearrange("p (k c) -> p k c", k=KC)).then_inc(ct_hi_done, 1)
                if there(trip, j):
                    i = j % 2
                    wait(act, clamp_done, trip, j + 1)
                    wait(act, z_ps, trip, j - 1)
                    act.copy(p_hi[:, i], pr[:]).then_inc(p_hi_done, 1)
                if there(trip, j - 1):
                    i = (j - 1) % 2
                    wait(act, rz_done, trip, j)
                    wait(act, zt_ps, trip, j - 1)
                    act.activation(zn[:], psZ[:, 0:D], ACT.Identity, scale=rz[:, i:i + 1]).then_inc(zn_done, 1)
                if there(trip, j - 2):
                    g = (j - 2) % PAIRS
                    wait(act, o_ps, trip, j - 1)
                    col = ((j - 2) // PAIRS + trip * 2) * N
                    for h in range(2):
                        rows = slice(h * 64, h * 64 + 64)
                        last = act.activation(qo[rows, g, bass.ds(col, N)], psO[rows, h * N:(h + 1) * N], ACT.Identity, bias=bias[rows, 2, g:g + 1])
                    last.then_inc(o_done, 1)

            for j in range(-11, -1):
                step(0, j)
            for r in range(8):
                act.wait_ge(q_ps, 2 * r + 1)
                act.copy(qo[:, r, 0:512], bank[:, (2 * r) % 4, :]).then_inc(q_act, 1)
            step(0, -1)
            trips(act, step)

            for r in range(8):
                act.wait_ge(lw_ps, r + 1)
                w, c = (wqkvT, r) if r < 6 else (woutT, r - 6)
                act.copy(w[:, :, c * P:(c + 1) * P], bank[:, 6 + r % 2, 0:D].rearrange("p (k c) -> p k c", k=KC)).then_inc(lw_done, 1)
            act.wait_ge(vec2_ps, 1)
            act.copy(vecs2[:], bank[:, 6, 0:E * FT + 4]).then_inc(vec2_done, 1)
            for t in range(TT):
                act.wait_ge(xnT_ps, t + 1)
                act.copy(xnT[:, :, t * P:(t + 1) * P], bank[:, 4 + t % 2, 0:D].rearrange("p (k c) -> p k c", k=KC)).then_inc(xnT_done, 1)
            act.wait_ge(vec2_done, 1)
            for r in range(8):
                act.wait_ge(qk_ps, r + 1)
                act.activation(qkT[:, r // 2, r % 2 * CH:(r % 2 + 1) * CH], bank[:, r % 4], ACT.Identity,
                               bias=vecs2[:, E * FT + r // 2:E * FT + r // 2 + 1]).then_inc(qk_done, 1)
            for r in range(0, 32, 2):
                c, q, p = r // 16, r // 8 % 2, r % 8
                act.wait_ge(f_ps, r + 1)
                act.activation(feat[:, q, p, c * CH:(c + 1) * CH], bank[:, r % 4], ACT.Relu).then_inc(f_act, 1)
            for t in range(TT + 1):
                if t < TT:
                    act.wait_ge(attT_ps, t + 1)
                    act.copy(attT[:, t % 2], bank[:, 0, 0:D]).then_inc(attT_done, 1)
                if t > 0:
                    act.wait_ge(xfT_ps, t)
                    if t > 2:
                        act.wait_ge(logit_ps, t - 2)
                        act.wait_ge(x_loT_done, t - 2)
                    act.copy(xfT[:, (t - 1) % 2], bank[:, 2, 0:D]).then_inc(xfT_done, 1)
            def high_parts(e, b):
                act.wait_ge(w1_ld, (e + 1) * 16)
                act.wait_ge(w2_ld, (e + 1) * 16)
                act.copy(w1_hi[:, b], w1_raw[:])
                act.copy(w2_hi[:, b], w2_raw[:]).then_inc(w_hi_done, 1)
                act.copy(b1_now[:, b], vecs2[:, bass.ds(e * FT, FT)]).then_inc(b1_done, 1)

            act.wait_ge(x_loT_done, TT)
            act.wait_ge(logit_ps, TT)
            high_parts(0, 0)
            act.wait_ge(gap_done, 1)
            act.activation(gate[:, 1], gate[:, 0], ACT.Exp).then_inc(gap_exp, 1)

            def hidden(e, b, first):
                act.wait_ge(b1_done, e + 1)
                for i in range(2 * FT):
                    c, f = i // FT, i % FT
                    act.wait_ge(h_ps, e * 16 + i + 1)
                    if not first or i >= 4:
                        act.wait_ge(h_lo_done, e * 16 + i - 3)
                    act.activation(hid[:, i % 4], bank[:, i % 4], ACT.Relu, bias=b1_now[:, b, f:f + 1]).then_inc(relu_done, 1)

            hidden(0, 0, True)
            high_parts(1, 1)
            hidden(1, 1, False)
            with act.Fori(1, E // 2) as pair:
                for b in range(2):
                    act.wait_ge(e_ps, (pair * 2 + b - 1) * TT)
                    high_parts(pair * 2 + b, b)
                    hidden(pair * 2 + b, b, False)

        @block.vector
        def _(dve):
            for c, v in ((2, -0.5), (3, EPS)):
                dve.memset(consts[:, c:c + 1], v)
            for h in range(2):
                for half in range(2):
                    r = half * 64 + h * 32
                    dve.memset(consts[r:r + 32, h:h + 1], 1.0)
                    dve.memset(consts[r:r + 32, 1 - h:2 - h], 0.0)
            dve.memset(x_hi[:, :, :, D:D + 2].bitcast(F32), 1.0)
            dve.memset(rz[:], 0.0).then_inc(consts_done, 1)

            dve.wait_ge(cs_ld, 32)
            for f in range(2):
                for r in range(4):
                    o = crep[:, f, :, r * HALF:(r + 1) * HALF]
                    last = dve.tensor_scalar(o, cs_raw[:, f], -1.0 if f == 1 and r < 2 else 1.0, None, ALU.mult)
            last.then_inc(crep_done, 1)

            dve.wait_ge(x_ld, 16)
            for rnd in range(2):
                for t in range(TT + 1):
                    r = rnd * TT + t
                    if t < TT:
                        i = r % 2
                        if rnd:
                            dve.wait_ge(xl_norm, t + 1)
                        dve.bn_stats(bst[:, i], xl[:, t]).then_inc(bn_done, 1)
                        dve.wait_ge(bn_done, r + 1)
                        dve.bn_aggr(mv[:, i], bst[:, i]).then_inc(xl_stats, 1)
                    if t > 0:
                        i = (r - 1) % 2
                        dve.wait_ge(xl_stats, r)
                        dve.wait_ge(xl_rstd, r)
                        dve.tensor_scalar(xl[:, t - 1], xl[:, t - 1], mv[:, i, 0:1], rstd[:, i:i + 1], ALU.subtract, ALU.mult).then_inc(xl_norm, 1)

            for f, tab in enumerate((ctab, stab)):
                dve.wait_ge(tab_ps, f + 1)
                dve.tensor_copy(tab[:], (psK, psS)[f]).then_inc(tab_done, 1)

            dve.wait_ge(wk_ld, 16)
            dve.wait_ge(wq_ld, 16)
            for src, dst, s in ((wk_raw, wk_p, wk_perm), (wq_raw, wq_p, wq_perm)):
                for k in range(KC):
                    for half in range(2):
                        o = dst[:, k].rearrange("p (g a hi) -> p g a hi", a=2, hi=64)[:, :, half].rearrange("p g (h i) -> p g h i", h=2)
                        s_ = src[:, k].rearrange("p (g h a i) -> p g h a i", h=2, a=2, i=HALF)[:, :, :, half]
                        dve.tensor_copy(o, s_).then_inc(s, 1)
            dve.wait_ge(wk_perm, 4)
            dve.wait_ge(vec_done, 1)
            for k in range(KC):
                dve.wait_ge(wk_hi_done, k + 1)
                dve.scalar_tensor_tensor(out=wk_lo[:, k], in0=wk_p[:, k], scalar=vecs[:, 2, k:k + 1], in1=wk_hi[:, k].bitcast(F32),
                                         op0=ALU.mult, op1=ALU.subtract).then_inc(wk_lo_done, 1)
            dve.wait_ge(bias_ps, 1)
            dve.tensor_copy(bias[:, 0], psZ[:, 0:8])
            dve.tensor_copy(bias[0:64, 1], psZ[64:128, 0:8])
            dve.tensor_copy(bias[64:128, 1], psZ[0:64, 0:8])
            dve.tensor_copy(bias[:, 2], psZ[:, 8:16]).then_inc(bias_done, 1)

            def queries(trip, b, buf):
                for h in range(2):
                    last = dve.tensor_scalar(qbd[:, buf, :, h * N:(h + 1) * N], qo[:, :, bass.ds((trip * 2 + b) * N, N)], consts[:, h:h + 1], None, ALU.mult)
                last.then_inc(qbd_done, 1)

            def step(trip, j):
                if there(trip, j + 1):
                    i, g = (j + 1) % 2, (j + 1) % PAIRS
                    wait(dve, k_swapped, trip, j + 2)
                    wait(dve, kr_done, trip, j)
                    dve.scalar_tensor_tensor(out=ku[:, i], in0=psK, scalar=bias[:, 0, g:g + 1], in1=ctab[:], op0=ALU.add, op1=ALU.mult).then_inc(ku_done, 1)
                if there(trip, j + 1):
                    dve.scalar_tensor_tensor(out=ksw[:, i], in0=ksw[:, i], scalar=bias[:, 1, g:g + 1], in1=stab[:], op0=ALU.add, op1=ALU.mult).then_inc(kv_done, 1)
                if there(trip, j):
                    wait(dve, exp_done, trip, j + 1)
                    dve.tensor_scalar(pr[:], pr[:], LOW, HIGH, ALU.max, ALU.min).then_inc(clamp_done, 1)
                if there(trip, j + 9):
                    b, t = place(j + 9)
                    cols = slice(t * P, (t + 1) * P)
                    wait(dve, ct_hi_done, trip, j + 10)
                    dve.tensor_tensor(ct_lo[:, b, :, cols], psT[:, 0:D].rearrange("p (k c) -> p k c", k=KC),
                                      ct_hi[:, b, :, cols].bitcast(F32), ALU.subtract).then_inc(ct_lo_done, 1)
                if there(trip, j - 1):
                    i = (j - 1) % 2
                    wait(dve, z_ps, trip, j)
                    dve.reciprocal(rz[:, i:i + 1], psZ[:, D:D + 1]).then_inc(rz_done, 1)
                if there(trip, j):
                    i = j % 2
                    wait(dve, p_hi_done, trip, j + 1)
                    wait(dve, z_ps, trip, j - 1)
                    dve.tensor_tensor(p_lo[:, i], pr[:], p_hi[:, i].bitcast(F32), ALU.subtract).then_inc(p_lo_done, 1)
                if there(trip, j + 7):
                    b, t = place(j + 7)
                    if t == 0:
                        wait(dve, z_ps, trip, j + 7 - PAIRS)
                    wait(dve, xhat_done, trip, j + 8)
                    dve.tensor_copy(x_hi[:, b, t, 0:D], raw[:, b, t]).then_inc(x_hi_done, 1)
                if there(trip, j + 11):
                    b, t = place(j + 11)
                    if t == 0:
                        n = (j + 11) // ST // 2 + 1
                        dve.wait_ge(ctx_ld[b], (trip + n) * 16)
                    dve.bn_stats(bst[:, (j + 11) % 2], raw[:, b, t]).then_inc(bn_done, 1)
                    wait(dve, bn_done, trip, j + 12 + 2 * TT)
                if there(trip, j + 10):
                    b, t = place(j + 10)
                    i = (j + 10) % 2
                    wait(dve, rstd_done, trip, j + 11)
                    dve.tensor_scalar(raw[:, b, t], raw[:, b, t], mv[:, i, 0:1], rstd[:, i:i + 1], ALU.subtract, ALU.mult).then_inc(xhat_done, 1)
                if there(trip, j + 11):
                    i = (j + 11) % 2
                    dve.bn_aggr(mv[:, i], bst[:, i]).then_inc(stats_done, 1)
                if j >= 0 and j % PAIRS == PAIRS - 2 and there(trip, j + 2):
                    queries(trip, j // PAIRS + 1, (j // PAIRS + 1) % 2)

            for j in range(-11, -1):
                step(0, j)
            for r in range(8):
                dve.wait_ge(q_ps, 2 * r + 2)
                dve.tensor_copy(qo[:, r, 512:1024], bank[:, (2 * r + 1) % 4, :]).then_inc(q_dve, 1)
            dve.wait_ge(q_act, 8)
            dve.wait_ge(q_dve, 8)
            dve.wait_ge(tab_ps, 2)
            queries(0, 0, 0)
            step(0, -1)
            trips(dve, step)
            dve.wait_ge(bo_ld, 16)
            dve.wait_ge(x2_ld, 16)
            dve.tensor_tensor(raw[:, 0], raw[:, 0], bo_all.unsqueeze(1).to_broadcast([P, TT, D]), ALU.add).then_inc(xbo_done, 1)
            dve.wait_ge(xbo_done, 1)

            def moments(c, t):
                r = c * TT + t
                dve.bn_stats(st6[:, c, t], raw[:, 0, t]).then_inc(l_bn, 1)
                dve.wait_ge(l_bn, r + 1)
                dve.bn_aggr(mom[:, c, t], st6[:, c, t]).then_inc(l_stats, 1)

            def normalise(c, t):
                r = c * TT + t
                dve.wait_ge(l_rstd, r + 1)
                dve.wait_ge(l_stats, r + 1)
                if r >= 2:
                    dve.wait_ge(xnT_ps if r - 2 < TT else xfT_ps, (r - 2) % TT + 1)
                dve.tensor_scalar(xn[:, r % 2], raw[:, 0, t], mom[:, c, t, 0:1], rsd[:, c, t:t + 1], ALU.subtract, ALU.mult).then_inc(xn_done, 1)

            for t in range(TT + 1):
                if t < TT:
                    dve.wait_ge(y_ps, t + 1)
                    dve.tensor_tensor(raw[:, 0, t], bank[:, t % 4, 0:D], raw[:, 0, t], ALU.add).then_inc(y_done, 1)
                    dve.wait_ge(y_done, t + 1)
                    moments(0, t)
                if t > 0:
                    normalise(0, t - 1)
            dve.wait_ge(misc_ld, 64)
            for t in range(TT):
                dve.wait_ge(v_ps, t + 1)
                dve.tensor_tensor(vaug[:, t, :, 0:AD], bank[:, 6 + t % 2, 0:D].rearrange("p (h d) -> p h d", h=AH),
                                  v_bias[:].rearrange("p (h d) -> p h d", h=AH), ALU.add).then_inc(v_done, 1)
            dve.tensor_tensor(raw[:, 0], raw[:, 0], bout_all[:].unsqueeze(1).to_broadcast([P, TT, D]), ALU.add).then_inc(x1b_done, 1)
            for r in range(1, 32, 2):
                c, q, p = r // 16, r // 8 % 2, r % 8
                dve.wait_ge(f_ps, r + 1)
                dve.tensor_scalar(feat[:, q, p, c * CH:(c + 1) * CH], bank[:, r % 4], 0.0, None, ALU.max).then_inc(f_dve, 1)
            dve.wait_ge(mask_done, 3)

            def result(t):
                i = t % 2
                dve.wait_ge(c_ps, t + 1)
                cv = bank[:, 6 + i, 0:AH * (AD + 1)].rearrange("p (h d) -> p h d", h=AH)
                dve.tensor_scalar(rec[:, i, 0], cv[:, :, AD], 1e-6, None, ALU.add).then_inc(den_done, 1)
                dve.wait_ge(den_done, t + 1)
                dve.reciprocal(rec[:, i, 1], rec[:, i, 0]).then_inc(rec_done, 1)
                dve.wait_ge(rec_done, t + 1)
                if t >= 2:
                    dve.wait_ge(attT_ps, t - 1)
                dve.tensor_tensor(att[:, i].rearrange("p (h d) -> p h d", h=AH), cv[:, :, 0:AD],
                                  rec[:, i, 1].unsqueeze(2).to_broadcast([P, AH, AD]), ALU.mult).then_inc(att_done, 1)

            def residual(t):
                dve.wait_ge(w_ps, t + 1)
                dve.wait_ge(x1b_done, 1)
                dve.tensor_tensor(raw[:, 0, t], bank[:, 1, 0:D], raw[:, 0, t], ALU.add).then_inc(x2_done, 1)
                dve.wait_ge(x2_done, t + 1)
                moments(1, t)
                normalise(1, t)

            def split_input(t):
                cols = slice(t * P, (t + 1) * P)
                v = xfT[:, t % 2].rearrange("p (k c) -> p k c", k=KC)
                dve.wait_ge(xfT_done, t + 1)
                dve.tensor_copy(x_hiT[:, :, cols], v).then_inc(x_hiT_done, 1)
                dve.wait_ge(x_hiT_done, t + 1)
                dve.tensor_tensor(x_loT[:, :, cols], v, x_hiT[:, :, cols].bitcast(F32), ALU.subtract).then_inc(x_loT_done, 1)

            def gating(t):
                dve.wait_ge(logit_ps, t + 1)
                dve.tensor_copy(logit[:, t], bank[:, 3, 0:E]).then_inc(logit_done, 1)

            for t in range(TT + 3):
                if t < TT:
                    for q in range(4):
                        r = 4 * t + q
                        dve.wait_ge(am_ps, r + 1)
                        if r >= 2 and q < 2 and t > 0:
                            dve.wait_ge(c_ps, t)
                        if q >= 2:
                            dve.wait_ge(cq_ps, 2 * t + q - 1)
                        dve.tensor_tensor(am[:, r % 2], bank[:, 4 + r % 2].rearrange("p (h c) -> p h c", h=4),
                                          mask[:].unsqueeze(1).to_broadcast([P, 4, P]), ALU.mult).then_inc(am_done, 1)
                if 1 <= t <= TT:
                    result(t - 1)
                if 2 <= t <= TT + 1:
                    residual(t - 2)
                if t >= 3:
                    split_input(t - 3)
                    gating(t - 3)

            dve.wait_ge(logit_done, TT)
            for t in range(TT):
                dve.max(top[:, t], logit[:, t]).then_inc(top_done, 1)
            dve.wait_ge(top_done, TT)
            for t in range(TT):
                dve.max_index(top_at[:, t], top[:, t], logit[:, t]).then_inc(top_done, 1)
            dve.tensor_tensor(gate[:, 0], top[:, :, 1], top[:, :, 0], ALU.subtract).then_inc(gap_done, 1)
            dve.wait_ge(top_done, 2 * TT)
            dve.tensor_copy(top_f[:], top_at[:, :, 0:2]).then_inc(top_f_done, 1)
            dve.wait_ge(gap_exp, 1)
            dve.tensor_scalar(gate[:, 0], gate[:, 1], 1.0, None, ALU.add).then_inc(den2_done, 1)
            dve.wait_ge(den2_done, 1)
            dve.reciprocal(gate[:, 2], gate[:, 0]).then_inc(gate_done, 1)
            dve.wait_ge(gate_done, 1)
            dve.tensor_tensor(gate[:, 3], gate[:, 1], gate[:, 2], ALU.mult).then_inc(gate_done, 1)
            dve.wait_ge(gate_done, 2)
            dve.wait_ge(top_f_done, 1)
            dve.wait_ge(lin_consts, 1)
            for k in range(2):
                for t in range(TT):
                    dve.tensor_scalar(pick[:, k, t], iota_e[:], top_f[:, t, k:k + 1], gate[:, 2 + k, t:t + 1], ALU.is_equal, ALU.mult).then_inc(pick_done, 1)
            dve.wait_ge(pick_done, 2 * TT)
            dve.tensor_tensor(comb[:], pick[:, 0], pick[:, 1], ALU.add).then_inc(comb_done, 1)
            def parts(e, b):
                for i in range(2 * FT):
                    c, f = i // FT, i % FT
                    cols = slice(c * CH, (c + 1) * CH)
                    dve.wait_ge(relu_done, e * 16 + i + 1)
                    dve.tensor_copy(h_hi[:, f, cols], hid[:, i % 4]).then_inc(h_hi_done, 1)
                    dve.wait_ge(h_hi_done, e * 16 + i + 1)
                    dve.tensor_tensor(h_lo[:, f, cols], hid[:, i % 4], h_hi[:, f, cols].bitcast(F32), ALU.subtract).then_inc(h_lo_done, 1)

            def outputs(e, first):
                for t in range(TT):
                    dve.wait_ge(e_ps, e * TT + t + 1)
                    if not first:
                        dve.wait_ge(acc_done, e * TT + t - (TT - 1))
                    dve.scalar_tensor_tensor(out=raw[:, 0, t], in0=bank[:, 4 + t % 4, 0:D], scalar=comb[:, t, bass.ds(e, 1)],
                                             in1=raw[:, 0, t], op0=ALU.mult, op1=ALU.add).then_inc(acc_done, 1)

            parts(0, 0)
            for t in range(0, TT, 4):
                dve.wait_ge(combT_ps, t // 4 + 1)
                dve.tensor_copy(combT[:, t * P:(t + 4) * P], bank[0:E, 4 + t // 4]).then_inc(combT_done, 1)
            for t in range(TT):
                dve.wait_ge(b2_ps, t + 1)
                dve.tensor_tensor(raw[:, 0, t], bank[:, 4 + t % 4, 0:D], raw[:, 0, t], ALU.add).then_inc(acc_b2, 1)
            dve.wait_ge(acc_b2, TT)
            outputs(0, True)
            with dve.Fori(1, E) as e:
                parts(e, 0)
                outputs(e, False)

        @block.tensor
        def _(pe):
            pe.wait_ge(ident_done, 2)
            pe.wait_ge(vec_ld, 64)
            pe.transpose(psZ[:, 0:4 * KC], vec_rows[:], ident[0:4 * KC, 0:4 * KC]).then_inc(vec_ps, 1)
            pe.wait_ge(crep_done, 1)
            for f in range(2):
                for t in range(ST):
                    last = pe.transpose((psK, psS)[f][:, t * P:(t + 1) * P], crep[:, f, t], ident[:])
                last.then_inc(tab_ps, 1)
            for t in range(TT):
                pe.wait_ge(xl_norm, TT + t + 1)
                if t >= 2:
                    pe.wait_ge(latT_done, t - 1)
                for k in range(KC):
                    last = pe.transpose((psZT if t % 2 else psO)[:, k * P:(k + 1) * P], xl[:, t, k * P:(k + 1) * P], ident[:])
                last.then_inc(latT_ps, 1)
            pe.wait_ge(vec_done, 1)
            pe.wait_ge(wk_perm, 4)
            pe.wait_ge(wv_ld, 16)
            for c in range(2):
                for g in range(PAIRS):
                    for k in range(KC):
                        last = pe.matmul(psZ[:, c * 8 + g:c * 8 + g + 1], (wk_p, wv)[c][:, k, g * P:(g + 1) * P], vecs[:, 3, k:k + 1],
                                         start=(k == 0), stop=(k == KC - 1))
            last.then_inc(bias_ps, 1)

            def step(trip, j):
                if there(trip, j + 1):
                    b, g = place(j + 1)
                    w = slice(g * P, (g + 1) * P)
                    wait(pe, ku_done, trip, j + 1)
                    if g == 0:
                        wait(pe, ct_lo_done, trip, j + 1 + PAIRS)
                    for c in range(2):
                        cols = slice(c * 512, (c + 1) * 512)
                        parts = [(l, r, k) for k in range(KC) for l, r in ((wk_hi, ct_hi), (wk_hi, ct_lo), (wk_lo, ct_hi))]
                        for m, (l, r, k) in enumerate(parts):
                            last = pe.matmul(psK[:, cols], l[:, k, w], r[:, b, k, cols], start=(m == 0), stop=(m == len(parts) - 1))
                    last.then_inc(k_ps, 1)
                if there(trip, j):
                    b, g = place(j)
                    wait(pe, kr_done, trip, j + 1)
                    wait(pe, exp_done, trip, j)
                    if g == 0:
                        pe.wait_ge(qbd_done, trip * 2 + (j // PAIRS + 1))
                    for t in range(ST):
                        last = pe.matmul(psS[:, t * P:(t + 1) * P], kr[:, j % 2, t * P:(t + 1) * P], qbd[:, b, g], start=True, stop=True)
                    last.then_inc(s_ps, 1)
                if there(trip, j + 9):
                    b, t = place(j + 9)
                    wait(pe, xhat_done, trip, j + 10)
                    wait(pe, ct_lo_done, trip, j + 9)
                    for k in range(KC):
                        last = pe.transpose(psT[:, k * P:(k + 1) * P], raw[:, b, t, k * P:(k + 1) * P], ident[:])
                    last.then_inc(xT_ps, 1)
                if there(trip, j - 2):
                    wait(pe, zn_done, trip, j - 1)
                    wait(pe, zts_done, trip, j - 2)
                    for k in range(KC):
                        last = pe.transpose(psZT[:, k * P:(k + 1) * P], zn[:, k * P:(k + 1) * P], ident[:])
                    last.then_inc(zt_ps, 1)
                if there(trip, j - 1):
                    b, g = place(j - 1)
                    i = (j - 1) % 2
                    wait(pe, p_lo_done, trip, j)
                    wait(pe, zn_done, trip, j - 1)
                    if g == 0:
                        wait(pe, x_lo_done, trip, j - 1 + PAIRS)
                    for t in range(ST):
                        c = slice(t * P, (t + 1) * P)
                        pe.matmul(psZ[:, 0:D + 2], p_hi[:, i, c], x_hi[:, b, t], start=(t == 0), stop=False, skip_group_check=True)
                        pe.matmul(psZ[:, 0:D], p_hi[:, i, c], x_lo[:, b, t], start=False, stop=False, skip_group_check=True)
                        last = pe.matmul(psZ[:, 0:D + 2], p_lo[:, i, c], x_hi[:, b, t], start=False, stop=(t == ST - 1), skip_group_check=True)
                    last.then_inc(z_ps, 1)
                if there(trip, j - 2):
                    g = (j - 2) % PAIRS
                    wait(pe, zts_done, trip, j - 1)
                    wait(pe, o_done, trip, j - 2)
                    for k in range(KC):
                        last = pe.matmul(psO[:, 0:P], wv[:, k, g * P:(g + 1) * P], zts[:, k * P:(k + 1) * P], start=(k == 0), stop=(k == KC - 1))
                    last.then_inc(o_ps, 1)

            for j in range(-11, -1):
                step(0, j)
            pe.wait_ge(wq_perm, 4)
            pe.wait_ge(latT_done, TT)
            pe.wait_ge(tab_done, 2)
            for g in range(PAIRS):
                for c in range(2):
                    r = 2 * g + c
                    if r >= 4:
                        pe.wait_ge((q_act, q_dve)[r % 2], (r - 4) // 2 + 1)
                    for k in range(KC):
                        last = pe.matmul(bank[:, r % 4, :], wq_p[:, k, g * P:(g + 1) * P], latT[:, k, c * 512:(c + 1) * 512], start=(k == 0), stop=(k == KC - 1))
                    last.then_inc(q_ps, 1)
            pe.wait_ge(q_act, 8)
            pe.wait_ge(q_dve, 8)
            pe.wait_ge(wk_lo_done, 2)
            pe.wait_ge(bias_done, 1)
            pe.wait_ge(wv_done, 2)
            pe.wait_ge(consts_done, 1)
            step(0, -1)
            trips(pe, step)
            pe.wait_ge(wo_ld, 16)
            pe.wait_ge(o_done, STEPS)

            def turn(t):
                pe.wait_ge(xn_done, t + 1)
                if t >= 2:
                    pe.wait_ge(xnT_done, t - 1)
                for k in range(KC):
                    last = pe.transpose(bank[:, 4 + t % 2, k * P:(k + 1) * P], xn[:, t % 2, k * P:(k + 1) * P], ident[:])
                last.then_inc(xnT_ps, 1)

            for t in range(TT + 2):
                if t < TT:
                    if t >= 4:
                        pe.wait_ge(y_done, t - 3)
                    for g in range(PAIRS):
                        last = pe.matmul(bank[:, t % 4, 0:D], qo[:, g, t * P:(t + 1) * P], wo[:, g], start=(g == 0), stop=(g == PAIRS - 1))
                    last.then_inc(y_ps, 1)
                if t == 1:
                    pe.wait_ge(lw_ld, 32)
                    for r in range(8):
                        if r >= 2:
                            pe.wait_ge(lw_done, r - 1)
                        w, c = (wqkv_raw, r) if r < 6 else (wout_raw, r - 6)
                        for k in range(KC):
                            last = pe.transpose(bank[:, 6 + r % 2, k * P:(k + 1) * P], w[:, c, k * P:(k + 1) * P], ident[:])
                        last.then_inc(lw_ps, 1)
                    pe.wait_ge(vec2_ld, 32)
                    pe.wait_ge(lw_done, 7)
                    pe.transpose(bank[:, 6, 0:E * FT + 4], vec_rows2[:], ident[0:E * FT + 4, 0:E * FT + 4]).then_inc(vec2_ps, 1)
                if t >= 2:
                    turn(t - 2)
            pe.wait_ge(lw_done, 8)
            pe.wait_ge(vec2_done, 1)
            for t in range(TT):
                pe.wait_ge(xnT_done, t + 1)
                if t >= 2:
                    pe.wait_ge(v_done, t - 1)
                for k in range(KC):
                    last = pe.matmul(bank[:, 6 + t % 2, 0:D], xnT[:, k, t * P:(t + 1) * P], wqkvT[:, k, 2 * D:3 * D], start=(k == 0), stop=(k == KC - 1))
                last.then_inc(v_ps, 1)
            pe.wait_ge(y_done, TT)
            for r in range(8):
                if r >= 4:
                    pe.wait_ge(qk_done, r - 3)
                for k in range(KC):
                    last = pe.matmul(bank[:, r % 4], wqkvT[:, k, r // 2 * P:(r // 2 + 1) * P], xnT[:, k, r % 2 * CH:(r % 2 + 1) * CH],
                                     start=(k == 0), stop=(k == KC - 1))
                last.then_inc(qk_ps, 1)
            pe.wait_ge(proj_ld, 16 * AH)
            for r in range(32):
                c, q, p = r // 16, r // 8 % 2, r % 8
                if r < 4:
                    pe.wait_ge(qk_done, 5 + r)
                else:
                    pe.wait_ge((f_act, f_dve)[r % 2], (r - 4) // 2 + 1)
                last = pe.matmul(bank[:, r % 4], feat_w[:, p], qkT[:, q * 2 + p // 4, c * CH:(c + 1) * CH], start=True, stop=True)
                last.then_inc(f_ps, 1)
            pe.wait_ge(f_act, 16)
            pe.wait_ge(f_dve, 16)

            def products(t):
                for q in range(4):
                    r = 4 * t + q
                    if r >= 2:
                        pe.wait_ge(am_done, r - 1)
                    for hh in range(4):
                        h = q // 2 * 8 + 2 * hh + q % 2
                        rows = slice(h % 2 * AM, (h % 2 + 1) * AM)
                        last = pe.matmul(bank[:, 4 + r % 2, hh * P:(hh + 1) * P], feat[rows, 1, h // 2, t * P:(t + 1) * P],
                                         feat[rows, 0, h // 2, t * P:(t + 1) * P], start=True, stop=True)
                    last.then_inc(am_ps, 1)
                    if q >= 1:
                        weighted(t, q - 1)
                weighted(t, 3)

            def weighted(t, q):
                r = 4 * t + q
                pe.wait_ge(am_done, r + 1)
                if q == 0 and t >= 2:
                    pe.wait_ge(att_done, t - 1)
                for hh in range(4):
                    h = q // 2 * 8 + 2 * hh + q % 2
                    last = pe.matmul(bank[:, 6 + t % 2, h * (AD + 1):(h + 1) * (AD + 1)], am[:, r % 2, hh], vaug[:, t, h],
                                     start=(h == 0), stop=(h == AH - 1), skip_group_check=True)
                if q < 3:
                    last.then_inc(cq_ps, 1)
                else:
                    last.then_inc(c_ps, 1)

            def project(t):
                pe.wait_ge(attT_done, t + 1)
                if t >= 1:
                    pe.wait_ge(x2_done, t)
                for k in range(KC):
                    last = pe.matmul(bank[:, 1, 0:D], attT[:, t % 2, k * P:(k + 1) * P], woutT[:, k], start=(k == 0), stop=(k == KC - 1))
                last.then_inc(w_ps, 1)

            def turn_att(t):
                pe.wait_ge(att_done, t + 1)
                if t >= 1:
                    pe.wait_ge(attT_done, t)
                for k in range(KC):
                    last = pe.transpose(bank[:, 0, k * P:(k + 1) * P], att[:, t % 2, k * P:(k + 1) * P], ident[:])
                last.then_inc(attT_ps, 1)

            def turn_input(t):
                pe.wait_ge(xn_done, TT + t + 1)
                if t >= 1:
                    pe.wait_ge(xfT_done, t)
                for k in range(KC):
                    last = pe.transpose(bank[:, 2, k * P:(k + 1) * P], xn[:, t % 2, k * P:(k + 1) * P], ident[:])
                last.then_inc(xfT_ps, 1)

            def logits(t):
                pe.wait_ge(xfT_done, t + 1)
                if t >= 1:
                    pe.wait_ge(logit_done, t)
                for k in range(KC):
                    last = pe.matmul(bank[:, 3, 0:E], xfT[:, t % 2, k * P:(k + 1) * P], wg[:, k], start=(k == 0), stop=(k == KC - 1))
                last.then_inc(logit_ps, 1)

            pe.wait_ge(v_done, TT)
            pe.wait_ge(misc_ld, 64)
            pe.wait_ge(lin_consts, 1)
            for t in range(TT + 4):
                if t < TT:
                    products(t)
                if 1 <= t <= TT:
                    turn_att(t - 1)
                    project(t - 1)
                if 2 <= t <= TT + 1:
                    turn_input(t - 2)
                    logits(t - 2)

            def expert_in(e, b, first):
                pe.wait_ge(w_lo_done, e + 1)
                for i in range(2 * FT):
                    c, f = i // FT, i % FT
                    cols, w = slice(c * CH, (c + 1) * CH), slice(f * P, (f + 1) * P)
                    if not first or i >= 4:
                        pe.wait_ge(relu_done, e * 16 + i - 3)
                    prods = [(l, r, k) for k in range(KC) for l, r in ((w1_hi, x_hiT), (w1_hi, x_loT), (w1_lo, x_hiT))]
                    for m, (l, r, k) in enumerate(prods):
                        last = pe.matmul(bank[:, i % 4], l[:, b, k, w], r[:, k, cols], start=(m == 0), stop=(m == len(prods) - 1))
                    last.then_inc(h_ps, 1)

            def expert_out(e, b, first):
                for t in range(TT):
                    if t % 4 == 0:
                        pe.wait_ge(h_lo_done, e * 16 + (t // 4 + 1) * FT)
                    if not first or t >= 4:
                        pe.wait_ge(acc_done, e * TT + t - 3)
                    rows = slice(t * P, (t + 1) * P)
                    prods = [(l, r, f) for f in range(FT) for l, r in ((h_hi, w2_hi), (h_hi, w2_lo), (h_lo, w2_hi))]
                    for m, (l, r, f) in enumerate(prods):
                        last = pe.matmul(bank[:, 4 + t % 4, 0:D], l[:, f, rows], r[:, b, f], start=(m == 0), stop=(m == len(prods) - 1))
                    last.then_inc(e_ps, 1)

            pe.wait_ge(x_loT_done, TT)
            pe.wait_ge(logit_done, TT)
            expert_in(0, 0, True)
            pe.wait_ge(comb_done, 1)
            for t in range(TT):
                last = pe.transpose(bank[0:E, 4 + t // 4, t % 4 * P:(t % 4 + 1) * P], comb[:, t], ident[:])
                if t % 4 == 3:
                    last.then_inc(combT_ps, 1)
            pe.wait_ge(combT_done, 2)
            for t in range(TT):
                if t >= 4:
                    pe.wait_ge(acc_b2, t - 3)
                pe.matmul(bank[:, 4 + t % 4, 0:D], combT[:, t * P:(t + 1) * P], b2_rows[:], start=True, stop=True).then_inc(b2_ps, 1)
            pe.wait_ge(acc_b2, TT)
            expert_out(0, 0, True)
            expert_in(1, 1, False)
            expert_out(1, 1, False)
            with pe.Fori(1, E // 2) as pair:
                for b in range(2):
                    expert_in(pair * 2 + b, b, False)
                    expert_out(pair * 2 + b, b, False)


_INS = ['x', 'ctx_1024', 'L0_xattn_cos', 'L0_xattn_sin', 'L0_xattn_ln_lat_g', 'L0_xattn_ln_lat_b', 'L0_xattn_ln_ctx_g',
        'L0_xattn_ln_ctx_b', 'L0_xattn_Wq', 'L0_xattn_Wkv', 'L0_xattn_Wo', 'L0_xattn_bo', 'L0_attn_Wqkv', 'L0_attn_bqkv',
        'L0_attn_Wout', 'L0_attn_bout', 'L0_attn_proj', 'L0_ffn_Wg', 'L0_ffn_W1', 'L0_ffn_b1', 'L0_ffn_W2', 'L0_ffn_b2']
_OUTS = [((16, 64, 256), 'float32')]


def kernel(**inputs):
    import numpy as _np
    import concourse.bacc as _bacc
    from concourse import mybir as _mybir
    from concourse.bass_utils import run_bass_kernel_spmd as _run

    nc = _bacc.Bacc("TRN2", target_bir_lowering=False, num_devices=1)
    arrays, args = {}, []
    for name in _INS:
        a = _np.ascontiguousarray(inputs[name])
        arrays[f"in_{name}_dram"] = a
        args.append(nc.dram_tensor(f"in_{name}_dram", a.shape, _mybir.dt.from_np(a.dtype), kind="ExternalInput").ap())
    for i, (shape, dtype) in enumerate(_OUTS):
        dt = _mybir.dt.from_np(_np.dtype(dtype))
        args.append(nc.dram_tensor(f"out_{i}_dram", shape, dt, kind="ExternalOutput").ap())
    build(nc, *args)
    r = _run(nc, [arrays], core_ids=[0])
    got = tuple(r.results[0][f"out_{i}_dram"] for i in range(len(_OUTS)))
    return got[0]
```

```python
from contextlib import ExitStack

import numpy as np
import concourse.bass as bass
from concourse import mybir

F32 = mybir.dt.float32
F32R = mybir.dt.float32r
U32 = mybir.dt.uint32
ALU = mybir.AluOpType
ACT = mybir.ActivationFunctionType

P = 128
B, N, D = 16, 64, 256
S = 1024
H, DH = 16, 64
HALF = DH // 2
INNER = H * DH
KC = D // P
PAIRS = H // 2
ST = S // P
TOK = B * N
TT = TOK // P
STEPS = B * PAIRS
BODY = 2 * PAIRS
TRIPS = STEPS // BODY
TILES = B * ST
EPS = 1e-5
CLIP = 11.0
SCALE = DH ** -0.5
LOW, HIGH = float(np.exp(-CLIP)), float(np.exp(CLIP))


F = 1024
FT = F // P
E = 8
AH, AD, AM = 16, 16, 64
CH = TOK // 2
CHUNK = 2 * P
FEATS = 2 * AH // 2


def build(nc, x, ctx_1024, cos, sin, lat_g, lat_b, ctx_g, ctx_b, Wq, Wkv, Wo, bo, Wqkv, bqkv, Wout, bout, proj,
          Wg, W1, b1, W2, b2, out):
    with ExitStack() as ctx:
        def sem(name):
            return ctx.enter_context(nc.semaphore(name))

        def sb(name, shape, dt=F32, scope=ctx):
            return scope.enter_context(nc.sbuf_tensor(name, shape, dt))

        ident = sb("ident", [P, P])
        consts = sb("consts", [P, 8])
        vecs = sb("vecs", [P, 4, KC])
        bias = sb("bias", [P, 3, PAIRS])
        bst = sb("bst", [P, 2, 6])
        mv = sb("mv", [P, 2, 2])
        ve = sb("ve", [P, 2])
        rstd = sb("rstd", [P, 2])
        rz = sb("rz", [P, 2])
        raw = sb("raw", [P, 2, ST, D])
        wo = sb("wo", [P, PAIRS, D])
        xattn = ctx.enter_context(ExitStack())
        wk_hi = sb("wk_hi", [P, KC, INNER], F32R, xattn)
        wk_lo = sb("wk_lo", [P, KC, INNER], F32R, xattn)
        wv = sb("wv", [P, KC, INNER], F32, xattn)
        ctab = sb("ctab", [P, S], F32, xattn)
        stab = sb("stab", [P, S], F32, xattn)
        qbd = sb("qbd", [P, 2, PAIRS, P], F32, xattn)
        ct_hi = sb("ct_hi", [P, 2, KC, S], F32R, xattn)
        ct_lo = sb("ct_lo", [P, 2, KC, S], F32R, xattn)
        x_hi = sb("x_hi", [P, 2, ST, D + 2], F32R, xattn)
        x_lo = sb("x_lo", [P, 2, ST, D], F32R, xattn)
        with ExitStack() as first:
            vec_rows = sb("vec_rows", [4 * KC, P], F32, first)
            latT = sb("latT", [P, KC, TOK], F32, first)
            wq_raw = sb("wq_raw", [P, KC, INNER], F32, first)
            wq_p = sb("wq_p", [P, KC, INNER], F32, first)
            wk_raw = sb("wk_raw", [P, KC, INNER], F32, first)
            wk_p = sb("wk_p", [P, KC, INNER], F32, first)
            cs_raw = sb("cs_raw", [P, 2, ST, HALF], F32, first)
        ksw = sb("ksw", [P, 2, S], F32, xattn)
        ku = sb("ku", [P, 2, S], F32, xattn)
        kr = sb("kr", [P, 2, S], F32, xattn)
        pr = sb("pr", [P, S], F32, xattn)
        p_hi = sb("p_hi", [P, 2, S], F32R, xattn)
        p_lo = sb("p_lo", [P, 2, S], F32R, xattn)
        zn = sb("zn", [P, D], F32, xattn)
        zts = sb("zts", [P, D], F32, xattn)
        xl = raw[:, 1]
        bo_all = raw[:, 1, 0]
        crep = qbd

        qo = sb("qo", [P, PAIRS, TOK], F32, xattn)
        xattn.close()
        wqkv_raw = raw[:, 1, 1:7]
        lin = ctx.enter_context(ExitStack())
        mask = sb("mask", [P, P], F32, lin)
        st6 = sb("st6", [P, 2, TT, 6], F32, lin)
        mom = sb("mom", [P, 2, TT, 2], F32, lin)
        vpe = sb("vpe", [P, 2, TT], F32, lin)
        rsd = sb("rsd", [P, 2, TT], F32, lin)
        cvec = sb("cvec", [P, 2], F32, lin)
        vec_rows2 = sb("vec_rows2", [E * FT + 4, P], F32, lin)
        vecs2 = sb("vecs2", [P, E * FT + 4], F32, lin)
        b1_now = sb("b1_now", [P, 2, FT], F32, lin)
        v_bias = sb("v_bias", [P, D], F32, lin)
        bout_all = sb("bout_all", [P, D], F32, lin)
        wg = sb("wg", [P, KC, E], F32, lin)
        b2_rows = sb("b2_rows", [E, D], F32, lin)
        iota_e = sb("iota_e", [P, E], F32, lin)
        logit = sb("logit", [P, TT, E], F32, lin)
        top = sb("top", [P, TT, 8], F32, lin)
        top_at = sb("top_at", [P, TT, 8], U32, lin)
        top_f = sb("top_f", [P, TT, 2], F32, lin)
        gate = sb("gate", [P, 4, TT], F32, lin)
        pick = sb("pick", [P, 2, TT, E], F32, lin)
        comb = sb("comb", [P, TT, E], F32, lin)
        combT = sb("combT", [E, TOK], F32, lin)
        x_hiT = sb("x_hiT", [P, KC, TOK], F32R, lin)
        x_loT = sb("x_loT", [P, KC, TOK], F32R, lin)
        w1_raw = sb("w1_raw", [P, KC, F], F32, lin)
        w2_raw = sb("w2_raw", [P, FT, D], F32, lin)

        def expert_parts(b):
            return [sb(f"{n}{b}", sh, F32R, lin) for n, sh in
                    (("w1_hi", [P, KC, F]), ("w1_lo", [P, KC, F]), ("w2_hi", [P, FT, D]), ("w2_lo", [P, FT, D]))]

        parts_even = expert_parts(0)
        with ExitStack() as attn:
            wqkvT = sb("wqkvT", [P, KC, 3 * D], F32, attn)
            wout_raw = sb("wout_raw", [P, KC, D], F32, attn)
            woutT = sb("woutT", [P, KC, D], F32, attn)
            feat_w = sb("feat_w", [P, AH // 2, P], F32, attn)
            att = sb("att", [P, 2, D], F32, attn)
            attT = sb("attT", [P, 2, D], F32, attn)
            xn = sb("xn", [P, 2, D], F32, attn)
            xfT = sb("xfT", [P, 2, D], F32, attn)
            xnT = sb("xnT", [P, KC, TOK], F32, attn)
            qkT = sb("qkT", [P, 4, TOK], F32, attn)
            vaug = sb("vaug", [P, TT, AH, AD + 1], F32, attn)
            rec = sb("rec", [P, 2, 2, AH], F32, attn)
            am = sb("am", [P, 2, 4, 4, P], F32, attn)
            feat = sb("feat", [P, 2, 2, AH // 2, 2 * P], F32, attn)
        w1_hi, w1_lo, w2_hi, w2_lo = zip(parts_even, expert_parts(1))
        hid = sb("hid", [P, 4, CH], F32, lin)
        h_hi = sb("h_hi", [P, FT, TOK], F32R, lin)
        h_lo = sb("h_lo", [P, FT, TOK], F32R, lin)

        bank = ctx.enter_context(nc.psum_tensor("bank", [P, 8, 512], F32))
        flat = bank[:].rearrange("p a b -> p (a b)")
        psK, psS = flat[:, 0:1024], flat[:, 1024:2048]
        psZ, psT, psZT, psO = bank[:, 4], bank[:, 5], bank[:, 6], bank[:, 7]

        x_ld, wq_ld, wk_ld, wv_ld, wo_ld, cs_ld, vec_ld = (sem(n) for n in ("x_ld", "wq_ld", "wk_ld", "wv_ld", "wo_ld", "cs_ld", "vec_ld"))
        ctx_ld = [sem(f"ctx_ld{i}") for i in range(2)]
        vec2_ld, lw_ld, misc_ld, proj_ld, w1_ld, w2_ld = (sem(n) for n in ("vec2_ld", "lw_ld", "misc_ld", "proj_ld", "w1_ld", "w2_ld"))
        lin_consts, feat_w_zero, mask_done = sem("lin_consts"), sem("feat_w_zero"), sem("mask_done")
        lw_ps, lw_done, vec2_ps, vec2_done = sem("lw_ps"), sem("lw_done"), sem("vec2_ps"), sem("vec2_done")
        l_bn, l_stats, l_var, l_rstd, xn_done = (sem(n) for n in ("l_bn", "l_stats", "l_var", "l_rstd", "xn_done"))
        xnT_ps, xnT_done, v_ps, v_done, qk_ps, qk_done = (sem(n) for n in ("xnT_ps", "xnT_done", "v_ps", "v_done", "qk_ps", "qk_done"))
        f_ps, f_done, am_ps, am_done, c_ps, rec_done, att_done = (sem(n) for n in ("f_ps", "f_done", "am_ps", "am_done", "c_ps", "rec_done", "att_done"))
        b1_done = sem("b1_done")
        den_done, attT_ps, attT_done, w_ps, x1b_done, x2_done = (sem(n) for n in ("den_done", "attT_ps", "attT_done", "w_ps", "x1b_done", "x2_done"))
        xfT_ps, xfT_done, x_hiT_done, x_loT_done, logit_ps, logit_done = (sem(n) for n in ("xfT_ps", "xfT_done", "x_hiT_done", "x_loT_done", "logit_ps", "logit_done"))
        top_done, gap_done, gap_exp, den2_done, gate_done, top_f_done = (sem(n) for n in ("top_done", "gap_done", "gap_exp", "den2_done", "gate_done", "top_f_done"))
        pick_done, comb_done, combT_ps, combT_done, b2_ps, acc_b2 = (sem(n) for n in ("pick_done", "comb_done", "combT_ps", "combT_done", "b2_ps", "acc_b2"))
        w_hi_done, w_lo_done, h_ps, relu_done, h_hi_done, h_lo_done, e_ps, acc_done = (sem(n) for n in ("w_hi_done", "w_lo_done", "h_ps", "relu_done", "h_hi_done", "h_lo_done", "e_ps", "acc_done"))
        vec_ps, vec_done = sem("vec_ps"), sem("vec_done")
        ident_done, consts_done, ones_done = sem("ident_done"), sem("consts_done"), sem("ones_done")
        xl_stats, xl_var, xl_rstd, xl_norm = sem("xl_stats"), sem("xl_var"), sem("xl_rstd"), sem("xl_norm")
        latT_ps, latT_done = sem("latT_ps"), sem("latT_done")
        wq_perm, wk_perm, wk_hi_done, wk_lo_done, wv_done = sem("wq_perm"), sem("wk_perm"), sem("wk_hi_done"), sem("wk_lo_done"), sem("wv_done")
        crep_done, tab_ps, tab_done = sem("crep_done"), sem("tab_ps"), sem("tab_done")
        bias_ps, bias_done = sem("bias_ps"), sem("bias_done")
        q_ps, q_act, q_dve = sem("q_ps"), sem("q_act"), sem("q_dve")
        bn_done, stats_done, var_done, rstd_done, xhat_done = sem("bn_done"), sem("stats_done"), sem("var_done"), sem("rstd_done"), sem("xhat_done")
        xT_ps, ct_hi_done, ct_lo_done, x_hi_done, x_lo_done = sem("xT_ps"), sem("ct_hi_done"), sem("ct_lo_done"), sem("x_hi_done"), sem("x_lo_done")
        k_ps, k_swapped, ku_done, kv_done, kr_done = sem("k_ps"), sem("k_swapped"), sem("ku_done"), sem("kv_done"), sem("kr_done")
        qbd_done = sem("qbd_done")
        s_ps, exp_done, clamp_done, p_hi_done, p_lo_done = sem("s_ps"), sem("exp_done"), sem("clamp_done"), sem("p_hi_done"), sem("p_lo_done")
        z_ps, rz_done, zn_done, zt_ps, zts_done, o_ps, o_done = (sem(n) for n in ("z_ps", "rz_done", "zn_done", "zt_ps", "zts_done", "o_ps", "o_done"))
        y_ps, y_done, out_st, bo_ld, x2_ld, xbo_done = (sem(n) for n in ("y_ps", "y_done", "out_st", "bo_ld", "x2_ld", "xbo_done"))

        def wait(eng, s, trip, count):
            if isinstance(trip, int):
                if trip * BODY + count > 0:
                    eng.wait_ge(s, trip * BODY + count)
            else:
                eng.wait_ge(s, trip * BODY + count)

        def there(trip, j):
            return not isinstance(trip, int) or 0 <= trip * BODY + j < STEPS

        def trips(eng, step):
            for j in range(0, BODY):
                step(0, j)
            with eng.Fori(1, TRIPS - 1) as trip:
                for j in range(BODY):
                    step(trip, j)
            for j in range(BODY + 2):
                step(TRIPS - 1, j)

        def place(j):
            return (j // PAIRS) % 2, j % PAIRS

        block = ctx.enter_context(nc.Block())

        @block.sync
        def _(sp):
            def ctx_rows(b):
                return ctx_1024[b].rearrange("(p t) d -> p t d", t=ST)

            sp.dma_start(xl, x.rearrange("b n d -> (b n) d").rearrange("(t p) d -> p t d", p=P)).then_inc(x_ld, 16)
            sp.dma_start(raw[:, 0], ctx_rows(0)).then_inc(ctx_ld[0], 16)
            sp.dma_start(cs_raw[:, 0], cos.rearrange("(p t) i -> p t i", t=ST)).then_inc(cs_ld, 16)
            sp.dma_start(cs_raw[:, 1], sin.rearrange("(p t) i -> p t i", t=ST)).then_inc(cs_ld, 16)
            for i, v in enumerate((lat_g, lat_b, ctx_g, ctx_b)):
                sp.dma_start(vec_rows[i * KC:(i + 1) * KC, :], v.rearrange("(k p) -> k p", p=P)).then_inc(vec_ld, 16)
            kv = Wkv.rearrange("(k p) n -> p k n", p=P)
            sp.dma_start(wq_raw[:], Wq.rearrange("(k p) n -> p k n", p=P)).then_inc(wq_ld, 16)
            sp.dma_start(wk_raw[:], kv[:, :, 0:INNER]).then_inc(wk_ld, 16)
            sp.dma_start(wv[:], kv[:, :, INNER:2 * INNER]).then_inc(wv_ld, 16)
            sp.dma_start(wo[:], Wo.rearrange("(g p) n -> p g n", p=P)).then_inc(wo_ld, 16)
            sp.wait_ge(latT_ps, TT)
            sp.dma_start(raw[:, 1], ctx_rows(1)).then_inc(ctx_ld[1], 16)
            with sp.Fori(1, TRIPS) as trip:
                for p in range(2):
                    wait(sp, xT_ps, trip, ST * (p - 1))
                    wait(sp, x_lo_done, trip, ST * (p - 1))
                    sp.dma_start(raw[:, p], ctx_1024[bass.ds(trip * 2 + p, 1)].rearrange("o (p t) d -> p (o t) d", t=ST)).then_inc(ctx_ld[p], 16)
            sp.wait_ge(x_lo_done, TILES)
            sp.wait_ge(xT_ps, TILES)
            sp.dma_start(bo_all, bo.partition_broadcast(P)).then_inc(bo_ld, 16)
            sp.dma_start(raw[:, 0], x.rearrange("b n d -> (b n) d").rearrange("(t p) d -> p t d", p=P)).then_inc(x2_ld, 16)
            sp.dma_start(wqkv_raw, Wqkv.rearrange("(r p) c -> p r c", p=P)).then_inc(lw_ld, 16)
            sp.wait_ge(o_ps, STEPS)
            sp.dma_start(vec_rows2[0:E * FT, :], b1.rearrange("e (f p) -> (e f) p", p=P)).then_inc(vec2_ld, 16)
            sp.dma_start(vec_rows2[E * FT:, :], bqkv[0:2 * D].rearrange("(r p) -> r p", p=P)).then_inc(vec2_ld, 16)
            sp.dma_start(wout_raw[:], Wout.rearrange("(r p) c -> p r c", p=P)).then_inc(lw_ld, 16)
            sp.wait_ge(feat_w_zero, 1)
            for h in range(AH):
                r = h % 8 * AD
                sp.dma_start(feat_w[r:r + AD, h // 2, h % 2 * AM:(h % 2 + 1) * AM], proj[h]).then_inc(proj_ld, 16)
            sp.dma_start(v_bias[:], bqkv[2 * D:3 * D].partition_broadcast(P)).then_inc(misc_ld, 16)
            sp.dma_start(bout_all[:], bout.partition_broadcast(P)).then_inc(misc_ld, 16)
            sp.dma_start(wg[:], Wg.rearrange("(k p) e -> p k e", p=P)).then_inc(misc_ld, 16)
            sp.dma_start(b2_rows[:], b2).then_inc(misc_ld, 16)
            sp.dma_start(w1_raw[:], W1[0].rearrange("(k p) f -> p k f", p=P)).then_inc(w1_ld, 16)
            sp.dma_start(w2_raw[:], W2[0].rearrange("(f p) d -> p f d", p=P)).then_inc(w2_ld, 16)
            with sp.Fori(1, E) as e:
                sp.wait_ge(w_hi_done, e)
                sp.wait_ge(w_lo_done, e)
                sp.dma_start(w1_raw[:], W1[bass.ds(e, 1)].rearrange("o (k p) f -> p (o k) f", p=P)).then_inc(w1_ld, 16)
                sp.dma_start(w2_raw[:], W2[bass.ds(e, 1)].rearrange("o (f p) d -> p (o f) d", p=P)).then_inc(w2_ld, 16)
            for t in range(TT):
                sp.wait_ge(acc_done, (E - 1) * TT + t + 1)
                sp.dma_start(out.rearrange("b n d -> (b n) d")[t * P:(t + 1) * P, :], raw[:, 0, t]).then_inc(out_st, 16)
            sp.wait_ge(out_st, 16 * TT)

        @block.gpsimd
        def _(pool):
            pool.memset(ident[:], 1.0).then_inc(ident_done, 1)
            pool.wait_ge(ident_done, 1)
            pool.affine_select(out=ident[:], in_=ident[:], compare_op=ALU.is_equal, fill=0.0, base=0,
                               pattern=[[-1, P]], channel_multiplier=1).then_inc(ident_done, 1)

            pool.wait_ge(consts_done, 1)
            for r in range(2 * TT):
                pool.wait_ge(xl_stats, r + 1)
                pool.tensor_tensor(ve[:, r % 2:r % 2 + 1], mv[:, r % 2, 1:2], consts[:, 3:4], ALU.add).then_inc(xl_var, 1)
                pool.wait_ge(xl_var, r + 1)
                pool.tensor_tensor(rstd[:, r % 2:r % 2 + 1], ve[:, r % 2:r % 2 + 1], consts[:, 2:3], ALU.pow).then_inc(xl_rstd, 1)

            def step(trip, j):
                if there(trip, j + 1):
                    i = (j + 1) % 2
                    wait(pool, ku_done, trip, j + 2)
                    wait(pool, kv_done, trip, j + 2)
                    wait(pool, s_ps, trip, j)
                    pool.tensor_tensor(kr[:, i], ku[:, i], ksw[:, i], ALU.add).then_inc(kr_done, 1)
                if there(trip, j + 7):
                    b, t = place(j + 7)
                    wait(pool, x_hi_done, trip, j + 8)
                    pool.tensor_tensor(x_lo[:, b, t], raw[:, b, t], x_hi[:, b, t, 0:D].bitcast(F32), ALU.subtract).then_inc(x_lo_done, 1)
                if there(trip, j + 11):
                    i = (j + 11) % 2
                    wait(pool, stats_done, trip, j + 12)
                    pool.tensor_tensor(ve[:, i:i + 1], mv[:, i, 1:2], consts[:, 3:4], ALU.add).then_inc(var_done, 1)
                    wait(pool, var_done, trip, j + 12)
                    pool.tensor_tensor(rstd[:, i:i + 1], ve[:, i:i + 1], consts[:, 2:3], ALU.pow).then_inc(rstd_done, 1)

            for j in range(-11, 0):
                step(0, j)
            trips(pool, step)

            pool.wait_ge(o_ps, STEPS)
            pool.memset(mask[:], 1.0).then_inc(mask_done, 1)
            pool.memset(feat_w[:], 0.0).then_inc(feat_w_zero, 1)
            pool.memset(vaug[:, :, :, AD:AD + 1], 1.0)
            for e in range(E):
                pool.memset(iota_e[:, e:e + 1], float(e))
            pool.memset(cvec[:, 0:1], -0.5)
            pool.memset(cvec[:, 1:2], EPS).then_inc(lin_consts, 1)
            pool.wait_ge(mask_done, 1)
            pool.affine_select(out=mask[:], in_=mask[:], compare_op=ALU.is_ge, fill=0.0, base=0,
                               pattern=[[1, P]], channel_multiplier=-1).then_inc(mask_done, 1)
            pool.wait_ge(mask_done, 2)
            pool.memset(mask[0:N, N:P], 0.0).then_inc(mask_done, 1)
            pool.wait_ge(lin_consts, 1)

            def moment_scales(c):
                for t in range(TT):
                    r = c * TT + t
                    pool.wait_ge(l_stats, r + 1)
                    pool.tensor_tensor(vpe[:, c, t:t + 1], mom[:, c, t, 1:2], cvec[:, 1:2], ALU.add).then_inc(l_var, 1)
                    pool.wait_ge(l_var, r + 1)
                    pool.tensor_tensor(rsd[:, c, t:t + 1], vpe[:, c, t:t + 1], cvec[:, 0:1], ALU.pow).then_inc(l_rstd, 1)

            moment_scales(0)

            def low_parts(e, b):
                pool.wait_ge(w_hi_done, e + 1)
                pool.tensor_tensor(w1_lo[b][:], w1_raw[:], w1_hi[b][:].bitcast(F32), ALU.subtract)
                pool.tensor_tensor(w2_lo[b][:], w2_raw[:], w2_hi[b][:].bitcast(F32), ALU.subtract).then_inc(w_lo_done, 1)

            low_parts(0, 0)
            moment_scales(1)
            pool.wait_ge(x_loT_done, TT)
            low_parts(1, 1)
            with pool.Fori(1, E // 2) as pair:
                for b in range(2):
                    low_parts(pair * 2 + b, b)

        @block.scalar
        def _(act):
            act.wait_ge(vec_ps, 1)
            act.copy(vecs[:].rearrange("p v k -> p (v k)"), psZ[:, 0:4 * KC]).then_inc(vec_done, 1)
            act.wait_ge(vec_done, 1)
            for t in range(TT):
                act.wait_ge(latT_ps, t + 1)
                for k in range(KC):
                    last = act.activation(latT[:, k, t * P:(t + 1) * P], (psZT if t % 2 else psO)[:, k * P:(k + 1) * P], ACT.Identity,
                                          bias=vecs[:, 1, k:k + 1], scale=vecs[:, 0, k:k + 1])
                last.then_inc(latT_done, 1)
            act.wait_ge(wk_perm, 4)
            for k in range(KC):
                act.activation(wk_hi[:, k], wk_p[:, k], ACT.Identity, scale=vecs[:, 2, k:k + 1]).then_inc(wk_hi_done, 1)
            act.wait_ge(wv_ld, 16)
            act.wait_ge(bias_ps, 1)
            for k in range(KC):
                act.activation(wv[:, k], wv[:, k], ACT.Identity, scale=vecs[:, 2, k:k + 1]).then_inc(wv_done, 1)

            def step(trip, j):
                if there(trip, j + 1):
                    i = (j + 1) % 2
                    wait(act, k_ps, trip, j + 2)
                    wait(act, kr_done, trip, j)
                    act.copy(ksw[0:64, i], psK[64:128, :])
                    act.copy(ksw[64:128, i], psK[0:64, :]).then_inc(k_swapped, 1)
                if there(trip, j):
                    wait(act, s_ps, trip, j + 1)
                    wait(act, p_lo_done, trip, j)
                    act.activation(pr[:], psS, ACT.Exp, scale=SCALE).then_inc(exp_done, 1)
                if there(trip, j - 2):
                    wait(act, zt_ps, trip, j - 1)
                    wait(act, o_ps, trip, j - 2)
                    act.copy(zts[:], psZT[:, 0:D]).then_inc(zts_done, 1)
                if there(trip, j + 9):
                    b, t = place(j + 9)
                    wait(act, xT_ps, trip, j + 10)
                    if t == 0:
                        wait(act, k_ps, trip, j + 9 - PAIRS)
                    act.copy(ct_hi[:, b, :, t * P:(t + 1) * P], psT[:, 0:D].rearrange("p (k c) -> p k c", k=KC)).then_inc(ct_hi_done, 1)
                if there(trip, j):
                    i = j % 2
                    wait(act, clamp_done, trip, j + 1)
                    wait(act, z_ps, trip, j - 1)
                    act.copy(p_hi[:, i], pr[:]).then_inc(p_hi_done, 1)
                if there(trip, j - 1):
                    i = (j - 1) % 2
                    wait(act, rz_done, trip, j)
                    wait(act, zt_ps, trip, j - 1)
                    act.activation(zn[:], psZ[:, 0:D], ACT.Identity, scale=rz[:, i:i + 1]).then_inc(zn_done, 1)
                if there(trip, j - 2):
                    g = (j - 2) % PAIRS
                    wait(act, o_ps, trip, j - 1)
                    col = ((j - 2) // PAIRS + trip * 2) * N
                    for h in range(2):
                        rows = slice(h * 64, h * 64 + 64)
                        last = act.activation(qo[rows, g, bass.ds(col, N)], psO[rows, h * N:(h + 1) * N], ACT.Identity, bias=bias[rows, 2, g:g + 1])
                    last.then_inc(o_done, 1)

            for j in range(-11, -1):
                step(0, j)
            for r in range(8):
                act.wait_ge(q_ps, 2 * r + 1)
                act.copy(qo[:, r, 0:512], bank[:, (2 * r) % 4, :]).then_inc(q_act, 1)
            step(0, -1)
            trips(act, step)

            for r in range(8):
                act.wait_ge(lw_ps, r + 1)
                w, c = (wqkvT, r) if r < 6 else (woutT, r - 6)
                act.copy(w[:, :, c * P:(c + 1) * P], bank[:, 6 + r % 2, 0:D].rearrange("p (k c) -> p k c", k=KC)).then_inc(lw_done, 1)
            act.wait_ge(vec2_ps, 1)
            act.copy(vecs2[:], bank[:, 6, 0:E * FT + 4]).then_inc(vec2_done, 1)
            for t in range(TT):
                act.wait_ge(xnT_ps, t + 1)
                act.copy(xnT[:, :, t * P:(t + 1) * P], bank[:, 4 + t % 2, 0:D].rearrange("p (k c) -> p k c", k=KC)).then_inc(xnT_done, 1)
            act.wait_ge(vec2_done, 1)

            def high_parts(e, b):
                act.wait_ge(w1_ld, (e + 1) * 16)
                act.wait_ge(w2_ld, (e + 1) * 16)
                act.copy(w1_hi[b][:], w1_raw[:])
                act.copy(w2_hi[b][:], w2_raw[:]).then_inc(w_hi_done, 1)
                act.copy(b1_now[:, b], vecs2[:, bass.ds(e * FT, FT)]).then_inc(b1_done, 1)

            high_parts(0, 0)
            for r in range(8):
                act.wait_ge(qk_ps, r + 1)
                act.activation(qkT[:, r // 2, r % 2 * CH:(r % 2 + 1) * CH], bank[:, r % 4], ACT.Identity,
                               bias=vecs2[:, E * FT + r // 2:E * FT + r // 2 + 1]).then_inc(qk_done, 1)

            def feature(n):
                c, q, p = n // FEATS, n // 8 % 2, n % 8
                if c >= 2 and n % FEATS == 0:
                    act.wait_ge(am_ps, 8 * (c - 1))
                act.wait_ge(f_ps, n + 1)
                act.activation(feat[:, c % 2, q, p], bank[:, 5 + n % 2, 0:CHUNK], ACT.Relu).then_inc(f_done, 1)

            def attention_turned(t):
                act.wait_ge(attT_ps, t + 1)
                if t >= 2:
                    act.wait_ge(w_ps, t - 1)
                act.copy(attT[:, t % 2], bank[:, 7, 0:D]).then_inc(attT_done, 1)

            def input_turned(t):
                act.wait_ge(xfT_ps, t + 1)
                if t >= 2:
                    act.wait_ge(logit_ps, t - 1)
                    act.wait_ge(x_loT_done, t - 1)
                act.copy(xfT[:, t % 2], bank[:, 7, 0:D]).then_inc(xfT_done, 1)

            def follow(s, q):
                if q == 3:
                    attention_turned(s - 1)
                if q == 1 and s >= 3:
                    input_turned(s - 3)

            def follow_last(i):
                if i == 1:
                    attention_turned(TT - 1)
                if i in (3, 5):
                    input_turned(TT - 2 + i // 5)

            for n in range(FEATS):
                feature(n)
            for r in range(4 * TT + 2):
                if r < 4 * TT:
                    for n in range(FEATS + 2 * r, FEATS + 2 * r + 2):
                        if n < FEATS * (TT // 2):
                            feature(n)
                if r >= 4:
                    follow(r // 4, r % 4)

            def hidden(e, b, first):
                act.wait_ge(b1_done, e + 1)
                for i in range(2 * FT):
                    c, f = i // FT, i % FT
                    act.wait_ge(h_ps, e * 16 + i + 1)
                    if not first or i >= 4:
                        act.wait_ge(h_lo_done, e * 16 + i - 3)
                    act.activation(hid[:, i % 4], bank[:, i % 4], ACT.Relu, bias=b1_now[:, b, f:f + 1]).then_inc(relu_done, 1)
                    if first:
                        follow_last(i)
                    if first and i == FT + 1:
                        act.wait_ge(gap_done, 1)
                        act.activation(gate[:, 1], gate[:, 0], ACT.Exp).then_inc(gap_exp, 1)

            act.wait_ge(c_ps, TT)
            hidden(0, 0, True)
            high_parts(1, 1)
            hidden(1, 1, False)
            with act.Fori(1, E // 2) as pair:
                for b in range(2):
                    act.wait_ge(e_ps, (pair * 2 + b - 1) * TT)
                    high_parts(pair * 2 + b, b)
                    hidden(pair * 2 + b, b, False)

        @block.vector
        def _(dve):
            for c, v in ((2, -0.5), (3, EPS)):
                dve.memset(consts[:, c:c + 1], v)
            for h in range(2):
                for half in range(2):
                    r = half * 64 + h * 32
                    dve.memset(consts[r:r + 32, h:h + 1], 1.0)
                    dve.memset(consts[r:r + 32, 1 - h:2 - h], 0.0)
            dve.memset(x_hi[:, :, :, D:D + 2].bitcast(F32), 1.0)
            dve.memset(rz[:], 0.0).then_inc(consts_done, 1)

            dve.wait_ge(cs_ld, 32)
            for f in range(2):
                for r in range(4):
                    o = crep[:, f, :, r * HALF:(r + 1) * HALF]
                    last = dve.tensor_scalar(o, cs_raw[:, f], -1.0 if f == 1 and r < 2 else 1.0, None, ALU.mult)
            last.then_inc(crep_done, 1)

            dve.wait_ge(x_ld, 16)
            for rnd in range(2):
                for t in range(TT + 1):
                    r = rnd * TT + t
                    if t < TT:
                        i = r % 2
                        if rnd:
                            dve.wait_ge(xl_norm, t + 1)
                        dve.bn_stats(bst[:, i], xl[:, t]).then_inc(bn_done, 1)
                        dve.wait_ge(bn_done, r + 1)
                        dve.bn_aggr(mv[:, i], bst[:, i]).then_inc(xl_stats, 1)
                    if t > 0:
                        i = (r - 1) % 2
                        dve.wait_ge(xl_stats, r)
                        dve.wait_ge(xl_rstd, r)
                        dve.tensor_scalar(xl[:, t - 1], xl[:, t - 1], mv[:, i, 0:1], rstd[:, i:i + 1], ALU.subtract, ALU.mult).then_inc(xl_norm, 1)

            for f, tab in enumerate((ctab, stab)):
                dve.wait_ge(tab_ps, f + 1)
                dve.tensor_copy(tab[:], (psK, psS)[f]).then_inc(tab_done, 1)

            dve.wait_ge(wk_ld, 16)
            dve.wait_ge(wq_ld, 16)
            for src, dst, s in ((wk_raw, wk_p, wk_perm), (wq_raw, wq_p, wq_perm)):
                for k in range(KC):
                    for half in range(2):
                        o = dst[:, k].rearrange("p (g a hi) -> p g a hi", a=2, hi=64)[:, :, half].rearrange("p g (h i) -> p g h i", h=2)
                        s_ = src[:, k].rearrange("p (g h a i) -> p g h a i", h=2, a=2, i=HALF)[:, :, :, half]
                        dve.tensor_copy(o, s_).then_inc(s, 1)
            dve.wait_ge(wk_perm, 4)
            dve.wait_ge(vec_done, 1)
            for k in range(KC):
                dve.wait_ge(wk_hi_done, k + 1)
                dve.scalar_tensor_tensor(out=wk_lo[:, k], in0=wk_p[:, k], scalar=vecs[:, 2, k:k + 1], in1=wk_hi[:, k].bitcast(F32),
                                         op0=ALU.mult, op1=ALU.subtract).then_inc(wk_lo_done, 1)
            dve.wait_ge(bias_ps, 1)
            dve.tensor_copy(bias[:, 0], psZ[:, 0:8])
            dve.tensor_copy(bias[0:64, 1], psZ[64:128, 0:8])
            dve.tensor_copy(bias[64:128, 1], psZ[0:64, 0:8])
            dve.tensor_copy(bias[:, 2], psZ[:, 8:16]).then_inc(bias_done, 1)

            def queries(trip, b, buf):
                for h in range(2):
                    last = dve.tensor_scalar(qbd[:, buf, :, h * N:(h + 1) * N], qo[:, :, bass.ds((trip * 2 + b) * N, N)], consts[:, h:h + 1], None, ALU.mult)
                last.then_inc(qbd_done, 1)

            def step(trip, j):
                if there(trip, j + 1):
                    i, g = (j + 1) % 2, (j + 1) % PAIRS
                    wait(dve, k_swapped, trip, j + 2)
                    wait(dve, kr_done, trip, j)
                    dve.scalar_tensor_tensor(out=ku[:, i], in0=psK, scalar=bias[:, 0, g:g + 1], in1=ctab[:], op0=ALU.add, op1=ALU.mult).then_inc(ku_done, 1)
                if there(trip, j + 1):
                    dve.scalar_tensor_tensor(out=ksw[:, i], in0=ksw[:, i], scalar=bias[:, 1, g:g + 1], in1=stab[:], op0=ALU.add, op1=ALU.mult).then_inc(kv_done, 1)
                if there(trip, j):
                    wait(dve, exp_done, trip, j + 1)
                    dve.tensor_scalar(pr[:], pr[:], LOW, HIGH, ALU.max, ALU.min).then_inc(clamp_done, 1)
                if there(trip, j + 9):
                    b, t = place(j + 9)
                    cols = slice(t * P, (t + 1) * P)
                    wait(dve, ct_hi_done, trip, j + 10)
                    dve.tensor_tensor(ct_lo[:, b, :, cols], psT[:, 0:D].rearrange("p (k c) -> p k c", k=KC),
                                      ct_hi[:, b, :, cols].bitcast(F32), ALU.subtract).then_inc(ct_lo_done, 1)
                if there(trip, j - 1):
                    i = (j - 1) % 2
                    wait(dve, z_ps, trip, j)
                    dve.reciprocal(rz[:, i:i + 1], psZ[:, D:D + 1]).then_inc(rz_done, 1)
                if there(trip, j):
                    i = j % 2
                    wait(dve, p_hi_done, trip, j + 1)
                    wait(dve, z_ps, trip, j - 1)
                    dve.tensor_tensor(p_lo[:, i], pr[:], p_hi[:, i].bitcast(F32), ALU.subtract).then_inc(p_lo_done, 1)
                if there(trip, j + 7):
                    b, t = place(j + 7)
                    if t == 0:
                        wait(dve, z_ps, trip, j + 7 - PAIRS)
                    wait(dve, xhat_done, trip, j + 8)
                    dve.tensor_copy(x_hi[:, b, t, 0:D], raw[:, b, t]).then_inc(x_hi_done, 1)
                if there(trip, j + 11):
                    b, t = place(j + 11)
                    if t == 0:
                        n = (j + 11) // ST // 2 + 1
                        dve.wait_ge(ctx_ld[b], (trip + n) * 16)
                    dve.bn_stats(bst[:, (j + 11) % 2], raw[:, b, t]).then_inc(bn_done, 1)
                    wait(dve, bn_done, trip, j + 12 + 2 * TT)
                if there(trip, j + 10):
                    b, t = place(j + 10)
                    i = (j + 10) % 2
                    wait(dve, rstd_done, trip, j + 11)
                    dve.tensor_scalar(raw[:, b, t], raw[:, b, t], mv[:, i, 0:1], rstd[:, i:i + 1], ALU.subtract, ALU.mult).then_inc(xhat_done, 1)
                if there(trip, j + 11):
                    i = (j + 11) % 2
                    dve.bn_aggr(mv[:, i], bst[:, i]).then_inc(stats_done, 1)
                if j >= 0 and j % PAIRS == PAIRS - 2 and there(trip, j + 2):
                    queries(trip, j // PAIRS + 1, (j // PAIRS + 1) % 2)

            for j in range(-11, -1):
                step(0, j)
            for r in range(8):
                dve.wait_ge(q_ps, 2 * r + 2)
                dve.tensor_copy(qo[:, r, 512:1024], bank[:, (2 * r + 1) % 4, :]).then_inc(q_dve, 1)
            dve.wait_ge(q_act, 8)
            dve.wait_ge(q_dve, 8)
            dve.wait_ge(tab_ps, 2)
            queries(0, 0, 0)
            step(0, -1)
            trips(dve, step)
            dve.wait_ge(bo_ld, 16)
            dve.wait_ge(x2_ld, 16)
            dve.tensor_tensor(raw[:, 0], raw[:, 0], bo_all.unsqueeze(1).to_broadcast([P, TT, D]), ALU.add).then_inc(xbo_done, 1)
            dve.wait_ge(xbo_done, 1)

            def moments(c, t):
                r = c * TT + t
                dve.bn_stats(st6[:, c, t], raw[:, 0, t]).then_inc(l_bn, 1)
                dve.wait_ge(l_bn, r + 1)
                dve.bn_aggr(mom[:, c, t], st6[:, c, t]).then_inc(l_stats, 1)

            def normalise(c, t):
                r = c * TT + t
                dve.wait_ge(l_rstd, r + 1)
                dve.wait_ge(l_stats, r + 1)
                if r >= 2:
                    dve.wait_ge(xnT_ps if r - 2 < TT else xfT_ps, (r - 2) % TT + 1)
                dve.tensor_scalar(xn[:, r % 2], raw[:, 0, t], mom[:, c, t, 0:1], rsd[:, c, t:t + 1], ALU.subtract, ALU.mult).then_inc(xn_done, 1)

            for t in range(TT + 1):
                if t < TT:
                    dve.wait_ge(y_ps, t + 1)
                    dve.tensor_tensor(raw[:, 0, t], bank[:, t % 4, 0:D], raw[:, 0, t], ALU.add).then_inc(y_done, 1)
                    dve.wait_ge(y_done, t + 1)
                    moments(0, t)
                if t > 0:
                    normalise(0, t - 1)
            dve.wait_ge(misc_ld, 64)
            for t in range(TT):
                dve.wait_ge(v_ps, t + 1)
                dve.tensor_tensor(vaug[:, t, :, 0:AD], bank[:, 6 + t % 2, 0:D].rearrange("p (h d) -> p h d", h=AH),
                                  v_bias[:].rearrange("p (h d) -> p h d", h=AH), ALU.add).then_inc(v_done, 1)
            dve.tensor_tensor(raw[:, 0], raw[:, 0], bout_all[:].unsqueeze(1).to_broadcast([P, TT, D]), ALU.add).then_inc(x1b_done, 1)
            dve.wait_ge(mask_done, 3)

            def masked(t, q):
                r = 4 * t + q
                if t >= 2 and q == 0:
                    dve.wait_ge(c_ps, t - 1)
                dve.wait_ge(am_ps, r + 1)
                dve.tensor_tensor(am[:, t % 2, q], bank[:, r % 3].rearrange("p (h c) -> p h c", h=4),
                                  mask[:].unsqueeze(1).to_broadcast([P, 4, P]), ALU.mult).then_inc(am_done, 1)

            def result(t):
                i = t % 2
                dve.wait_ge(c_ps, t + 1)
                cv = bank[:, 3 + i, 0:AH * (AD + 1)].rearrange("p (h d) -> p h d", h=AH)
                dve.tensor_scalar(rec[:, i, 0], cv[:, :, AD], 1e-6, None, ALU.add).then_inc(den_done, 1)
                dve.wait_ge(den_done, t + 1)
                dve.reciprocal(rec[:, i, 1], rec[:, i, 0]).then_inc(rec_done, 1)
                dve.wait_ge(rec_done, t + 1)
                if t >= 2:
                    dve.wait_ge(attT_ps, t - 1)
                dve.tensor_tensor(att[:, i].rearrange("p (h d) -> p h d", h=AH), cv[:, :, 0:AD],
                                  rec[:, i, 1].unsqueeze(2).to_broadcast([P, AH, AD]), ALU.mult).then_inc(att_done, 1)

            def residual(t):
                dve.wait_ge(w_ps, t + 1)
                dve.wait_ge(x1b_done, 1)
                dve.tensor_tensor(raw[:, 0, t], bank[:, 7, 0:D], raw[:, 0, t], ALU.add).then_inc(x2_done, 1)
                dve.wait_ge(x2_done, t + 1)
                moments(1, t)

            def split_input(t):
                cols = slice(t * P, (t + 1) * P)
                v = xfT[:, t % 2].rearrange("p (k c) -> p k c", k=KC)
                dve.wait_ge(xfT_done, t + 1)
                dve.tensor_copy(x_hiT[:, :, cols], v).then_inc(x_hiT_done, 1)
                dve.wait_ge(x_hiT_done, t + 1)
                dve.tensor_tensor(x_loT[:, :, cols], v, x_hiT[:, :, cols].bitcast(F32), ALU.subtract).then_inc(x_loT_done, 1)

            def gating(t):
                dve.wait_ge(logit_ps, t + 1)
                dve.tensor_copy(logit[:, t], bank[:, 7, 0:E]).then_inc(logit_done, 1)
                dve.wait_ge(logit_done, t + 1)
                dve.max(top[:, t], logit[:, t]).then_inc(top_done, 1)
                dve.wait_ge(top_done, 2 * t + 1)
                dve.max_index(top_at[:, t], top[:, t], logit[:, t]).then_inc(top_done, 1)

            def follow(s, q):
                if q == 1 and s >= 2:
                    residual(s - 2)
                if q == 2:
                    result(s - 1)
                    if s >= 2:
                        normalise(1, s - 2)
                if q == 3 and s >= 3:
                    gating(s - 3)
                    split_input(s - 3)

            def follow_last(i):
                if i == 0:
                    gating(TT - 3)
                    split_input(TT - 3)
                if i == 2:
                    residual(TT - 1)
                if i == 3:
                    normalise(1, TT - 1)
                    split_input(TT - 2)
                if i == 4:
                    gating(TT - 2)
                if i == 5:
                    split_input(TT - 1)
                if i == 6:
                    gating(TT - 1)

            for r in range(4 * TT + 3):
                if r < 4 * TT:
                    masked(r // 4, r % 4)
                if r >= 4:
                    follow(r // 4, r % 4)

            def parts(e, tiles=range(2 * FT)):
                for i in tiles:
                    c, f = i // FT, i % FT
                    cols = slice(c * CH, (c + 1) * CH)
                    dve.wait_ge(relu_done, e * 16 + i + 1)
                    dve.tensor_copy(h_hi[:, f, cols], hid[:, i % 4]).then_inc(h_hi_done, 1)
                    dve.wait_ge(h_hi_done, e * 16 + i + 1)
                    dve.tensor_tensor(h_lo[:, f, cols], hid[:, i % 4], h_hi[:, f, cols].bitcast(F32), ALU.subtract).then_inc(h_lo_done, 1)

            def outputs(e, first):
                for t in range(TT):
                    dve.wait_ge(e_ps, e * TT + t + 1)
                    if not first:
                        dve.wait_ge(acc_done, e * TT + t - (TT - 1))
                    dve.scalar_tensor_tensor(out=raw[:, 0, t], in0=bank[:, 4 + t % 4, 0:D], scalar=comb[:, t, bass.ds(e, 1)],
                                             in1=raw[:, 0, t], op0=ALU.mult, op1=ALU.add).then_inc(acc_done, 1)

            dve.wait_ge(c_ps, TT)
            for i in range(FT):
                parts(0, (i,))
                follow_last(i)
            dve.wait_ge(top_done, 2 * TT)
            dve.tensor_tensor(gate[:, 0], top[:, :, 1], top[:, :, 0], ALU.subtract).then_inc(gap_done, 1)
            parts(0, (FT, FT + 1))
            dve.tensor_copy(top_f[:], top_at[:, :, 0:2]).then_inc(top_f_done, 1)
            dve.wait_ge(gap_exp, 1)
            dve.tensor_scalar(gate[:, 0], gate[:, 1], 1.0, None, ALU.add).then_inc(den2_done, 1)
            dve.wait_ge(den2_done, 1)
            dve.reciprocal(gate[:, 2], gate[:, 0]).then_inc(gate_done, 1)
            dve.wait_ge(gate_done, 1)
            dve.tensor_tensor(gate[:, 3], gate[:, 1], gate[:, 2], ALU.mult).then_inc(gate_done, 1)
            dve.wait_ge(gate_done, 2)
            dve.wait_ge(top_f_done, 1)
            dve.wait_ge(lin_consts, 1)
            for k in range(2):
                dve.tensor_tensor(pick[:, k], iota_e[:].unsqueeze(1).to_broadcast([P, TT, E]), top_f[:, :, k:k + 1].to_broadcast([P, TT, E]), ALU.is_equal).then_inc(pick_done, 1)
            for k in range(2):
                dve.wait_ge(pick_done, k + 1)
                dve.tensor_tensor(pick[:, k], pick[:, k], gate[:, 2 + k].unsqueeze(2).to_broadcast([P, TT, E]), ALU.mult).then_inc(pick_done, 1)
            dve.wait_ge(pick_done, 4)
            dve.tensor_tensor(comb[:], pick[:, 0], pick[:, 1], ALU.add).then_inc(comb_done, 1)
            parts(0, range(FT + 2, 2 * FT))
            outputs(0, True)
            for t in range(0, TT, 4):
                dve.wait_ge(combT_ps, t // 4 + 1)
                dve.tensor_copy(combT[:, t * P:(t + 4) * P], bank[0:E, 4 + t // 4]).then_inc(combT_done, 1)
            parts(1)
            for t in range(TT):
                dve.wait_ge(b2_ps, t + 1)
                dve.wait_ge(acc_done, t + 1)
                dve.tensor_tensor(raw[:, 0, t], bank[:, 4 + t % 4, 0:D], raw[:, 0, t], ALU.add).then_inc(acc_b2, 1)
            dve.wait_ge(acc_b2, TT)
            outputs(1, False)
            with dve.Fori(2, E) as e:
                parts(e)
                outputs(e, False)

        @block.tensor
        def _(pe):
            pe.wait_ge(ident_done, 2)
            pe.wait_ge(vec_ld, 64)
            pe.transpose(psZ[:, 0:4 * KC], vec_rows[:], ident[0:4 * KC, 0:4 * KC]).then_inc(vec_ps, 1)
            pe.wait_ge(crep_done, 1)
            for f in range(2):
                for t in range(ST):
                    last = pe.transpose((psK, psS)[f][:, t * P:(t + 1) * P], crep[:, f, t], ident[:])
                last.then_inc(tab_ps, 1)
            for t in range(TT):
                pe.wait_ge(xl_norm, TT + t + 1)
                if t >= 2:
                    pe.wait_ge(latT_done, t - 1)
                for k in range(KC):
                    last = pe.transpose((psZT if t % 2 else psO)[:, k * P:(k + 1) * P], xl[:, t, k * P:(k + 1) * P], ident[:])
                last.then_inc(latT_ps, 1)
            pe.wait_ge(vec_done, 1)
            pe.wait_ge(wk_perm, 4)
            pe.wait_ge(wv_ld, 16)
            for c in range(2):
                for g in range(PAIRS):
                    for k in range(KC):
                        last = pe.matmul(psZ[:, c * 8 + g:c * 8 + g + 1], (wk_p, wv)[c][:, k, g * P:(g + 1) * P], vecs[:, 3, k:k + 1],
                                         start=(k == 0), stop=(k == KC - 1))
            last.then_inc(bias_ps, 1)

            def step(trip, j):
                if there(trip, j + 1):
                    b, g = place(j + 1)
                    w = slice(g * P, (g + 1) * P)
                    wait(pe, ku_done, trip, j + 1)
                    if g == 0:
                        wait(pe, ct_lo_done, trip, j + 1 + PAIRS)
                    for c in range(2):
                        cols = slice(c * 512, (c + 1) * 512)
                        parts = [(l, r, k) for k in range(KC) for l, r in ((wk_hi, ct_hi), (wk_hi, ct_lo), (wk_lo, ct_hi))]
                        for m, (l, r, k) in enumerate(parts):
                            last = pe.matmul(psK[:, cols], l[:, k, w], r[:, b, k, cols], start=(m == 0), stop=(m == len(parts) - 1))
                    last.then_inc(k_ps, 1)
                if there(trip, j):
                    b, g = place(j)
                    wait(pe, kr_done, trip, j + 1)
                    wait(pe, exp_done, trip, j)
                    if g == 0:
                        pe.wait_ge(qbd_done, trip * 2 + (j // PAIRS + 1))
                    for t in range(ST):
                        last = pe.matmul(psS[:, t * P:(t + 1) * P], kr[:, j % 2, t * P:(t + 1) * P], qbd[:, b, g], start=True, stop=True)
                    last.then_inc(s_ps, 1)
                if there(trip, j + 9):
                    b, t = place(j + 9)
                    wait(pe, xhat_done, trip, j + 10)
                    wait(pe, ct_lo_done, trip, j + 9)
                    for k in range(KC):
                        last = pe.transpose(psT[:, k * P:(k + 1) * P], raw[:, b, t, k * P:(k + 1) * P], ident[:])
                    last.then_inc(xT_ps, 1)
                if there(trip, j - 2):
                    wait(pe, zn_done, trip, j - 1)
                    wait(pe, zts_done, trip, j - 2)
                    for k in range(KC):
                        last = pe.transpose(psZT[:, k * P:(k + 1) * P], zn[:, k * P:(k + 1) * P], ident[:])
                    last.then_inc(zt_ps, 1)
                if there(trip, j - 1):
                    b, g = place(j - 1)
                    i = (j - 1) % 2
                    wait(pe, p_lo_done, trip, j)
                    wait(pe, zn_done, trip, j - 1)
                    if g == 0:
                        wait(pe, x_lo_done, trip, j - 1 + PAIRS)
                    for t in range(ST):
                        c = slice(t * P, (t + 1) * P)
                        pe.matmul(psZ[:, 0:D + 2], p_hi[:, i, c], x_hi[:, b, t], start=(t == 0), stop=False, skip_group_check=True)
                        pe.matmul(psZ[:, 0:D], p_hi[:, i, c], x_lo[:, b, t], start=False, stop=False, skip_group_check=True)
                        last = pe.matmul(psZ[:, 0:D + 2], p_lo[:, i, c], x_hi[:, b, t], start=False, stop=(t == ST - 1), skip_group_check=True)
                    last.then_inc(z_ps, 1)
                if there(trip, j - 2):
                    g = (j - 2) % PAIRS
                    wait(pe, zts_done, trip, j - 1)
                    wait(pe, o_done, trip, j - 2)
                    for k in range(KC):
                        last = pe.matmul(psO[:, 0:P], wv[:, k, g * P:(g + 1) * P], zts[:, k * P:(k + 1) * P], start=(k == 0), stop=(k == KC - 1))
                    last.then_inc(o_ps, 1)

            for j in range(-11, -1):
                step(0, j)
            pe.wait_ge(wq_perm, 4)
            pe.wait_ge(latT_done, TT)
            pe.wait_ge(tab_done, 2)
            for g in range(PAIRS):
                for c in range(2):
                    r = 2 * g + c
                    if r >= 4:
                        pe.wait_ge((q_act, q_dve)[r % 2], (r - 4) // 2 + 1)
                    for k in range(KC):
                        last = pe.matmul(bank[:, r % 4, :], wq_p[:, k, g * P:(g + 1) * P], latT[:, k, c * 512:(c + 1) * 512], start=(k == 0), stop=(k == KC - 1))
                    last.then_inc(q_ps, 1)
            pe.wait_ge(q_act, 8)
            pe.wait_ge(q_dve, 8)
            pe.wait_ge(wk_lo_done, 2)
            pe.wait_ge(bias_done, 1)
            pe.wait_ge(wv_done, 2)
            pe.wait_ge(consts_done, 1)
            step(0, -1)
            trips(pe, step)
            pe.wait_ge(wo_ld, 16)
            pe.wait_ge(o_done, STEPS)

            def turn(t):
                pe.wait_ge(xn_done, t + 1)
                if t >= 2:
                    pe.wait_ge(xnT_done, t - 1)
                for k in range(KC):
                    last = pe.transpose(bank[:, 4 + t % 2, k * P:(k + 1) * P], xn[:, t % 2, k * P:(k + 1) * P], ident[:])
                last.then_inc(xnT_ps, 1)

            for t in range(TT + 2):
                if t < TT:
                    if t >= 4:
                        pe.wait_ge(y_done, t - 3)
                    for g in range(PAIRS):
                        last = pe.matmul(bank[:, t % 4, 0:D], qo[:, g, t * P:(t + 1) * P], wo[:, g], start=(g == 0), stop=(g == PAIRS - 1))
                    last.then_inc(y_ps, 1)
                if t == 1:
                    pe.wait_ge(lw_ld, 32)
                    for r in range(8):
                        if r >= 2:
                            pe.wait_ge(lw_done, r - 1)
                        w, c = (wqkv_raw, r) if r < 6 else (wout_raw, r - 6)
                        for k in range(KC):
                            last = pe.transpose(bank[:, 6 + r % 2, k * P:(k + 1) * P], w[:, c, k * P:(k + 1) * P], ident[:])
                        last.then_inc(lw_ps, 1)
                    pe.wait_ge(vec2_ld, 32)
                    pe.wait_ge(lw_done, 7)
                    pe.transpose(bank[:, 6, 0:E * FT + 4], vec_rows2[:], ident[0:E * FT + 4, 0:E * FT + 4]).then_inc(vec2_ps, 1)
                if t >= 2:
                    turn(t - 2)
            pe.wait_ge(lw_done, 8)
            pe.wait_ge(vec2_done, 1)
            for t in range(TT):
                pe.wait_ge(xnT_done, t + 1)
                if t >= 2:
                    pe.wait_ge(v_done, t - 1)
                for k in range(KC):
                    last = pe.matmul(bank[:, 6 + t % 2, 0:D], xnT[:, k, t * P:(t + 1) * P], wqkvT[:, k, 2 * D:3 * D], start=(k == 0), stop=(k == KC - 1))
                last.then_inc(v_ps, 1)
            pe.wait_ge(y_done, TT)
            for r in range(8):
                if r >= 4:
                    pe.wait_ge(qk_done, r - 3)
                for k in range(KC):
                    last = pe.matmul(bank[:, r % 4], wqkvT[:, k, r // 2 * P:(r // 2 + 1) * P], xnT[:, k, r % 2 * CH:(r % 2 + 1) * CH],
                                     start=(k == 0), stop=(k == KC - 1))
                last.then_inc(qk_ps, 1)
            pe.wait_ge(proj_ld, 16 * AH)

            def feature(n):
                c, q, p = n // FEATS, n // 8 % 2, n % 8
                if c == 0:
                    pe.wait_ge(qk_done, 2 * (q * 2 + p // 4) + 1)
                elif n == FEATS:
                    pe.wait_ge(qk_done, 8)
                if n >= 2:
                    pe.wait_ge(f_done, n - 1)
                pe.matmul(bank[:, 5 + n % 2, 0:CHUNK], feat_w[:, p], qkT[:, q * 2 + p // 4, c * CHUNK:(c + 1) * CHUNK],
                          start=True, stop=True).then_inc(f_ps, 1)

            def products(t, q):
                r = 4 * t + q
                if r >= 3:
                    pe.wait_ge(am_done, r - 2)
                if q == 0:
                    pe.wait_ge(f_done, FEATS * (t // 2 + 1))
                for hh in range(4):
                    h = q // 2 * 8 + 2 * hh + q % 2
                    cols = slice(t % 2 * P, (t % 2 + 1) * P)
                    rows = slice(h % 2 * AM, (h % 2 + 1) * AM)
                    last = pe.matmul(bank[:, r % 3, hh * P:(hh + 1) * P], feat[rows, t // 2 % 2, 1, h // 2, cols],
                                     feat[rows, t // 2 % 2, 0, h // 2, cols], start=True, stop=True)
                last.then_inc(am_ps, 1)

            def weighted(t, q):
                if t >= 2 and q == 0:
                    pe.wait_ge(att_done, t - 1)
                pe.wait_ge(am_done, 4 * t + q + 1)
                for hh in range(4):
                    h = q // 2 * 8 + 2 * hh + q % 2
                    last = pe.matmul(bank[:, 3 + t % 2, h * (AD + 1):(h + 1) * (AD + 1)], am[:, t % 2, q, hh], vaug[:, t, h],
                                     start=(h == 0), stop=(h == AH - 1), skip_group_check=True)
                if q == 3:
                    last.then_inc(c_ps, 1)

            def turn_att(t):
                pe.wait_ge(att_done, t + 1)
                if t >= 2:
                    pe.wait_ge(logit_done, t - 1)
                for k in range(KC):
                    last = pe.transpose(bank[:, 7, k * P:(k + 1) * P], att[:, t % 2, k * P:(k + 1) * P], ident[:])
                last.then_inc(attT_ps, 1)

            def project(t):
                pe.wait_ge(attT_done, t + 1)
                for k in range(KC):
                    last = pe.matmul(bank[:, 7, 0:D], attT[:, t % 2, k * P:(k + 1) * P], woutT[:, k], start=(k == 0), stop=(k == KC - 1))
                last.then_inc(w_ps, 1)

            def turn_input(t):
                pe.wait_ge(xn_done, TT + t + 1)
                if t < TT - 1:
                    pe.wait_ge(x2_done, t + 2)
                else:
                    pe.wait_ge(logit_done, t)
                for k in range(KC):
                    last = pe.transpose(bank[:, 7, k * P:(k + 1) * P], xn[:, t % 2, k * P:(k + 1) * P], ident[:])
                last.then_inc(xfT_ps, 1)

            def logits(t):
                pe.wait_ge(xfT_done, t + 1)
                for k in range(KC):
                    last = pe.matmul(bank[:, 7, 0:E], xfT[:, t % 2, k * P:(k + 1) * P], wg[:, k], start=(k == 0), stop=(k == KC - 1))
                last.then_inc(logit_ps, 1)

            def follow(s, q):
                t, stage = (s - 2, s - 3, s - 3, s - 1)[q], (project, turn_input, logits, turn_att)[q]
                if t >= 0:
                    stage(t)

            def follow_last(i):
                if i < 7:
                    t, stage = ((TT - 3, logits), (TT - 1, turn_att), (TT - 1, project), (TT - 2, turn_input), (TT - 2, logits),
                                (TT - 1, turn_input), (TT - 1, logits))[i]
                    stage(t)

            pe.wait_ge(v_done, TT)
            pe.wait_ge(lin_consts, 1)
            for n in range(FEATS):
                feature(n)
            pe.wait_ge(qk_done, 8)
            pe.wait_ge(misc_ld, 64)
            for r in range(4 * TT + 2):
                if r < 4 * TT:
                    products(r // 4, r % 4)
                    for n in range(FEATS + 2 * r, FEATS + 2 * r + 2):
                        if n < FEATS * (TT // 2):
                            feature(n)
                if r >= 2:
                    weighted((r - 2) // 4, (r - 2) % 4)
                follow(r // 4, r % 4)

            def expert_in(e, b, first):
                pe.wait_ge(w_lo_done, e + 1)
                for i in range(2 * FT):
                    c, f = i // FT, i % FT
                    cols, w = slice(c * CH, (c + 1) * CH), slice(f * P, (f + 1) * P)
                    if not first or i >= 4:
                        pe.wait_ge(relu_done, e * 16 + i - 3)
                    prods = [(l, r, k) for k in range(KC) for l, r in ((w1_hi, x_hiT), (w1_hi, x_loT), (w1_lo, x_hiT))]
                    if first and i == FT:
                        pe.wait_ge(x_loT_done, TT)
                    for m, (l, r, k) in enumerate(prods):
                        last = pe.matmul(bank[:, i % 4], l[b][:, k, w], r[:, k, cols], start=(m == 0), stop=(m == len(prods) - 1))
                    last.then_inc(h_ps, 1)
                    if first:
                        follow_last(i)

            def expert_out(e, b, first):
                for t in range(TT):
                    if t % 4 == 0:
                        pe.wait_ge(h_lo_done, e * 16 + (t // 4 + 1) * FT)
                    if not first or t >= 4:
                        pe.wait_ge(acc_done, e * TT + t - 3)
                    rows = slice(t * P, (t + 1) * P)
                    prods = [(l, r, f) for f in range(FT) for l, r in ((h_hi, w2_hi), (h_hi, w2_lo), (h_lo, w2_hi))]
                    for m, (l, r, f) in enumerate(prods):
                        last = pe.matmul(bank[:, 4 + t % 4, 0:D], l[:, f, rows], r[b][:, f], start=(m == 0), stop=(m == len(prods) - 1))
                    last.then_inc(e_ps, 1)

            pe.wait_ge(x_loT_done, TT // 2)
            expert_in(0, 0, True)
            pe.wait_ge(logit_done, TT)
            expert_out(0, 0, True)
            pe.wait_ge(comb_done, 1)
            for t in range(TT):
                if t % 4 == 0:
                    pe.wait_ge(acc_done, TT - 3 + t // 4)
                last = pe.transpose(bank[0:E, 4 + t // 4, t % 4 * P:(t % 4 + 1) * P], comb[:, t], ident[:])
                if t % 4 == 3:
                    last.then_inc(combT_ps, 1)
            expert_in(1, 1, False)
            pe.wait_ge(combT_done, 2)
            pe.wait_ge(acc_done, TT)
            for t in range(TT):
                if t >= 4:
                    pe.wait_ge(acc_b2, t - 3)
                pe.matmul(bank[:, 4 + t % 4, 0:D], combT[:, t * P:(t + 1) * P], b2_rows[:], start=True, stop=True).then_inc(b2_ps, 1)
            pe.wait_ge(acc_b2, TT)
            expert_out(1, 1, False)
            with pe.Fori(1, E // 2) as pair:
                for b in range(2):
                    expert_in(pair * 2 + b, b, False)
                    expert_out(pair * 2 + b, b, False)


_INS = ['x', 'ctx_1024', 'L0_xattn_cos', 'L0_xattn_sin', 'L0_xattn_ln_lat_g', 'L0_xattn_ln_lat_b', 'L0_xattn_ln_ctx_g',
        'L0_xattn_ln_ctx_b', 'L0_xattn_Wq', 'L0_xattn_Wkv', 'L0_xattn_Wo', 'L0_xattn_bo', 'L0_attn_Wqkv', 'L0_attn_bqkv',
        'L0_attn_Wout', 'L0_attn_bout', 'L0_attn_proj', 'L0_ffn_Wg', 'L0_ffn_W1', 'L0_ffn_b1', 'L0_ffn_W2', 'L0_ffn_b2']
_OUTS = [((16, 64, 256), 'float32')]


def kernel(**inputs):
    import numpy as _np
    import concourse.bacc as _bacc
    from concourse import mybir as _mybir
    from concourse.bass_utils import run_bass_kernel_spmd as _run

    nc = _bacc.Bacc("TRN2", target_bir_lowering=False, num_devices=1)
    arrays, args = {}, []
    for name in _INS:
        a = _np.ascontiguousarray(inputs[name])
        arrays[f"in_{name}_dram"] = a
        args.append(nc.dram_tensor(f"in_{name}_dram", a.shape, _mybir.dt.from_np(a.dtype), kind="ExternalInput").ap())
    for i, (shape, dtype) in enumerate(_OUTS):
        dt = _mybir.dt.from_np(_np.dtype(dtype))
        args.append(nc.dram_tensor(f"out_{i}_dram", shape, dt, kind="ExternalOutput").ap())
    build(nc, *args)
    r = _run(nc, [arrays], core_ids=[0])
    got = tuple(r.results[0][f"out_{i}_dram"] for i in range(len(_OUTS)))
    return got[0]
```

```python
from contextlib import ExitStack

import numpy as np
import concourse.bass as bass
from concourse import mybir

F32 = mybir.dt.float32
F32R = mybir.dt.float32r
U32 = mybir.dt.uint32
I32 = mybir.dt.int32
ALU = mybir.AluOpType
ACT = mybir.ActivationFunctionType

P = 128
B, N, D = 16, 64, 256
S = 1024
H, DH = 16, 64
HALF = DH // 2
INNER = H * DH
KC = D // P
PAIRS = H // 2
ST = S // P
TOK = B * N
TT = TOK // P
STEPS = B * PAIRS
BODY = 2 * PAIRS
TRIPS = STEPS // BODY
TILES = B * ST
EPS = 1e-5
CLIP = 11.0
SCALE = DH ** -0.5
LOW, HIGH = float(np.exp(-CLIP)), float(np.exp(CLIP))

F = 1024
FT = F // P
E = 8
TOPK = 2
ROWS = 2 * P
GROUPS = (TOPK * TOK + E * (ROWS - 1)) // ROWS
AH, AD, AM = 16, 16, 64
CH = TOK // 2
APAIRS = AH // 2
FEATS = 2 * APAIRS // 2


def build(nc, x, ctx_1024, cos, sin, lat_g, lat_b, ctx_g, ctx_b, Wq, Wkv, Wo, bo, Wqkv, bqkv, Wout, bout, proj,
          Wg, W1, b1, W2, b2, out):
    with ExitStack() as ctx:
        def sem(name):
            return ctx.enter_context(nc.semaphore(name))

        def sb(name, shape, dt=F32, scope=ctx):
            return scope.enter_context(nc.sbuf_tensor(name, shape, dt))

        ident = sb("ident", [P, P])
        consts = sb("consts", [P, 8])
        vecs = sb("vecs", [P, 4, KC])
        bias = sb("bias", [P, 3, PAIRS])
        bst = sb("bst", [P, 2, 6])
        mv = sb("mv", [P, 2, 2])
        ve = sb("ve", [P, 2])
        rstd = sb("rstd", [P, 2])
        rz = sb("rz", [P, 2])
        raw = sb("raw", [P, 2, ST, D])
        wo = sb("wo", [P, PAIRS, D])
        xattn = ctx.enter_context(ExitStack())
        wk_hi = sb("wk_hi", [P, KC, INNER], F32R, xattn)
        wk_lo = sb("wk_lo", [P, KC, INNER], F32R, xattn)
        wv = sb("wv", [P, KC, INNER], F32, xattn)
        ctab = sb("ctab", [P, S], F32, xattn)
        stab = sb("stab", [P, S], F32, xattn)
        qbd = sb("qbd", [P, 2, PAIRS, P], F32, xattn)
        ct_hi = sb("ct_hi", [P, 2, KC, S], F32R, xattn)
        ct_lo = sb("ct_lo", [P, 2, KC, S], F32R, xattn)
        x_hi = sb("x_hi", [P, 2, ST, D + 2], F32R, xattn)
        x_lo = sb("x_lo", [P, 2, ST, D], F32R, xattn)
        with ExitStack() as first:
            vec_rows = sb("vec_rows", [4 * KC, P], F32, first)
            wq_raw = sb("wq_raw", [P, KC, INNER], F32, first)
            wk_raw = sb("wk_raw", [P, KC, INNER], F32, first)
            wk_p = sb("wk_p", [P, KC, INNER], F32, first)
            latT = sb("latT", [P, KC, TOK], F32, first)
            wq_p = sb("wq_p", [P, KC, INNER], F32, first)
            cs_raw = sb("cs_raw", [P, 2, ST, HALF], F32, first)
            xl_st6 = sb("xl_st6", [P, TT, 6], F32, first)
            xl_mom = sb("xl_mom", [P, TT, 2], F32, first)
            xl_vpe = sb("xl_vpe", [P, TT], F32, first)
            xl_sum = sb("xl_sum", [P, TT], F32, first)
            xl_rsd = sb("xl_rsd", [P, TT], F32, first)
        ksw = sb("ksw", [P, 2, S], F32, xattn)
        ku = sb("ku", [P, 2, S], F32, xattn)
        kr = sb("kr", [P, 2, S], F32, xattn)
        pr = sb("pr", [P, S], F32, xattn)
        p_hi = sb("p_hi", [P, 2, S], F32R, xattn)
        p_lo = sb("p_lo", [P, 2, S], F32R, xattn)
        zn = sb("zn", [P, D], F32, xattn)
        zts = sb("zts", [P, D], F32, xattn)
        xl = raw[:, 1]
        bo_all = raw[:, 1, 0]
        crep = qbd

        qo = sb("qo", [P, PAIRS, TOK], F32, xattn)
        xattn.close()
        wqkv_raw = raw[:, 1, 1:7]
        lin = ctx.enter_context(ExitStack())
        square = sb("square", [P, P], F32, lin)
        mask = sb("mask", [P, N], F32, lin)
        st6 = sb("st6", [P, 2, TT, 6], F32, lin)
        mom = sb("mom", [P, 2, TT, 2], F32, lin)
        vpe = sb("vpe", [P, 2, TT], F32, lin)
        rsd = sb("rsd", [P, 2, TT], F32, lin)
        cvec = sb("cvec", [P, 2], F32, lin)
        vec_rows2 = sb("vec_rows2", [E * FT + 4, P], F32, lin)
        vecs2 = sb("vecs2", [P, E * FT + 4], F32, lin)
        b1_now = sb("b1_now", [P, 2, FT], F32, lin)
        v_bias = sb("v_bias", [P, D], F32, lin)
        bout_all = sb("bout_all", [P, D], F32, lin)
        wg = sb("wg", [P, KC, E], F32, lin)
        b2_rows = sb("b2_rows", [E, D], F32, lin)
        iota = sb("iota", [P, 16], F32, lin)
        logit = sb("logit", [P, TT, E], F32, lin)
        top = sb("top", [P, TT, 8], F32, lin)
        top_at = sb("top_at", [P, TT, 8], U32, lin)
        top_f = sb("top_f", [P, TT, 2], F32, lin)
        gate = sb("gate", [P, 4, TT], F32, lin)
        pick = sb("pick", [P, 2, TT, E], F32, lin)
        comb = sb("comb", [P, TT, E], F32, lin)
        combT = sb("combT", [E, TOK], F32, lin)
        ones = sb("ones", [P, P], F32, lin)
        picked = sb("picked", [P, TT, E], F32, lin)
        before = sb("before", [P, TT + 1, E], F32, lin)
        n_exp = sb("n_exp", [P, 3, E], F32, lin)
        slot_f = sb("slot_f", [P, TOPK, TT], F32, lin)
        slot = sb("slot", [P, TOPK, TT], I32, lin)
        slot_0 = sb("slot_0", [P, E], F32, lin)
        of_slot = sb("of_slot", [P, TT, E], F32, lin)
        slot_of = sb("slot_of", [P, TT, TOPK, E], F32, lin)
        group_in = sb("group_in", [P, 16, E], F32, lin)
        group_v = sb("group_v", [P, 16, E], F32, lin)
        group_r = sb("group_r", [P, 16], F32, lin)
        group_at = sb("group_at", [P, 16], I32, lin)
        group_cmp = sb("group_cmp", [P, 16, E], F32, lin)
        group_f = sb("group_f", [P, 16], F32, lin)
        group_expert = sb("group_expert", [P, 16], I32, lin)
        fill = sb("fill", [P, 2, D + 1], F32, lin)
        spare = sb("spare", [P, 4], F32, lin)
        numbers = sb("numbers", [P, 2], F32, lin)
        xn_all = sb("xn_all", [P, TOPK, TT, D + 1], F32, lin)
        with ExitStack() as attn:
            wqkvT = sb("wqkvT", [P, KC, 3 * D], F32, attn)
            wout_raw = sb("wout_raw", [P, KC, D], F32, attn)
            woutT = sb("woutT", [P, KC, D], F32, attn)
            feat_w = sb("feat_w", [P, AH // 2, P], F32, attn)
            att = sb("att", [P, 2, D], F32, attn)
            attT = sb("attT", [P, 2, D], F32, attn)
            xn = sb("xn", [P, 2, D], F32, attn)
            xfT = sb("xfT", [P, 2, D], F32, attn)
            xnT = sb("xnT", [P, KC, TOK], F32, attn)
            qkT = sb("qkT", [P, 4, TOK], F32, attn)
            feat_k = sb("feat_k", [P, 2, APAIRS, 2, P], F32, attn)
            vbd = sb("vbd", [P, TT, 2, APAIRS, 2 * (AD + 1)], F32, attn)
            feat_q = sb("feat_q", [P, 2, APAIRS, P], F32, attn)
            am = sb("am", [P, 2, 4, 4, N], F32, attn)
            rec = sb("rec", [P, 2, 2, AH], F32, attn)
        w1_raw = sb("w1_raw", [P, 2, KC, F], F32, lin)
        w2_raw = sb("w2_raw", [P, 2, FT, D], F32, lin)
        w1_hi = sb("w1_hi", [P, 2, KC, F], F32R, lin)
        w1_lo = sb("w1_lo", [P, 2, KC, F], F32R, lin)
        w2_hi = sb("w2_hi", [P, 2, FT, D], F32R, lin)
        w2_lo = sb("w2_lo", [P, 2, FT, D], F32R, lin)
        xs = sb("xs", [P, 2, 2, D + 1], F32, lin)
        result_no = sb("result_no", [P, 2, 2], U32, lin)
        xs_hi = sb("xs_hi", [P, KC, ROWS], F32R, lin)
        xs_lo = sb("xs_lo", [P, KC, ROWS], F32R, lin)
        hid = sb("hid", [P, 4, ROWS], F32, lin)
        h_hi = sb("h_hi", [P, FT, ROWS], F32R, lin)
        h_lo = sb("h_lo", [P, FT, ROWS], F32R, lin)
        ys = sb("ys", [P, 2, 2, D], F32, lin)
        result_of = sb("result_of", [P, TOPK, TT, D], F32, lin)

        x_slots = nc.dram_tensor("x_slots", [E * TOK + ROWS, D + 1], F32, kind="Internal").ap()
        results = nc.dram_tensor("results", [TOPK * TOK + ROWS, D], F32, kind="Internal").ap()

        bank = ctx.enter_context(nc.psum_tensor("bank", [P, 8, 512], F32))
        flat = bank[:].rearrange("p a b -> p (a b)")
        psK, psS = flat[:, 0:1024], flat[:, 1024:2048]
        psZ, psT, psZT, psO = bank[:, 4], bank[:, 5], bank[:, 6], bank[:, 7]

        x_ld, wq_ld, wk_ld, wv_ld, wo_ld, cs_ld, vec_ld = (sem(n) for n in ("x_ld", "wq_ld", "wk_ld", "wv_ld", "wo_ld", "cs_ld", "vec_ld"))
        ctx_ld = [sem(f"ctx_ld{i}") for i in range(2)]
        vec2_ld, lw_ld, misc_ld, proj_ld = (sem(n) for n in ("vec2_ld", "lw_ld", "misc_ld", "proj_ld"))
        w_ld, xs_ld, ys_st = ([sem(f"{n}{i}") for i in range(2)] for n in ("w_ld", "xs_ld", "ys_st"))
        result_ld = [sem(f"result_ld{i}") for i in range(2)]
        fill_done, fill_st, scattered, prefix_done, rank_ps, count_done, slot_done, group_done, chosen = (
            sem(n) for n in ("fill_done", "fill_st", "scattered", "prefix_done", "rank_ps", "count_done", "slot_done", "group_done", "chosen"))
        slot_step, total_ps = sem("slot_step"), sem("total_ps")
        no_done, count_rows, spare_done = sem("no_done"), sem("count_rows"), sem("spare_done")
        lin_consts, feat_w_zero, mask_done = sem("lin_consts"), sem("feat_w_zero"), sem("mask_done")
        vbd_zero, vbd_ones, feat_k_zero = sem("vbd_zero"), sem("vbd_ones"), sem("feat_k_zero")
        lw_ps, lw_done, vec2_ps, vec2_done = sem("lw_ps"), sem("lw_done"), sem("vec2_ps"), sem("vec2_done")
        l_bn, l_stats, l_var, l_rstd, xn_done = (sem(n) for n in ("l_bn", "l_stats", "l_var", "l_rstd", "xn_done"))
        xnT_ps, xnT_done, v_ps, v_done, qk_ps, qk_done = (sem(n) for n in ("xnT_ps", "xnT_done", "v_ps", "v_done", "qk_ps", "qk_done"))
        f_ps, f_done, am_ps, am_done, c_ps, rec_done, att_done = (sem(n) for n in ("f_ps", "f_done", "am_ps", "am_done", "c_ps", "rec_done", "att_done"))
        b1_done = sem("b1_done")
        den_done, attT_ps, attT_done, w_ps, x1b_done, x2_done = (sem(n) for n in ("den_done", "attT_ps", "attT_done", "w_ps", "x1b_done", "x2_done"))
        xfT_ps, xfT_done, logit_ps, logit_done = (sem(n) for n in ("xfT_ps", "xfT_done", "logit_ps", "logit_done"))
        top_done, gap_done, gap_exp, gate_done = (sem(n) for n in ("top_done", "gap_done", "gap_exp", "gate_done"))
        pick_done, comb_done, combT_ps, combT_done, b2_ps, acc_b2 = (sem(n) for n in ("pick_done", "comb_done", "combT_ps", "combT_done", "b2_ps", "acc_b2"))
        w1_hi_done, w2_hi_done, w1_lo_done, w2_lo_done, xs_ps, xs_hi_done, xs_lo_done = (
            sem(n) for n in ("w1_hi_done", "w2_hi_done", "w1_lo_done", "w2_lo_done", "xs_ps", "xs_hi_done", "xs_lo_done"))
        h_ps, relu_done, h_hi_done, h_lo_done, e_ps, ys_done, acc_done = (
            sem(n) for n in ("h_ps", "relu_done", "h_hi_done", "h_lo_done", "e_ps", "ys_done", "acc_done"))
        vec_ps, vec_done = sem("vec_ps"), sem("vec_done")
        ident_done, consts_done = sem("ident_done"), sem("consts_done")
        xl_bn, xl_stats, xl_var, xl_rstd, xl_norm = sem("xl_bn"), sem("xl_stats"), sem("xl_var"), sem("xl_rstd"), sem("xl_norm")
        latT_ps, latT_done = sem("latT_ps"), sem("latT_done")
        wq_perm, wk_perm, wk_hi_done, wk_lo_done, wv_done = sem("wq_perm"), sem("wk_perm"), sem("wk_hi_done"), sem("wk_lo_done"), sem("wv_done")
        crep_done, tab_ps, tab_done = sem("crep_done"), sem("tab_ps"), sem("tab_done")
        bias_ps, bias_done = sem("bias_ps"), sem("bias_done")
        q_ps, q_act, q_dve = sem("q_ps"), sem("q_act"), sem("q_dve")
        bn_done, stats_done, var_done, rstd_done, xhat_done = sem("bn_done"), sem("stats_done"), sem("var_done"), sem("rstd_done"), sem("xhat_done")
        xT_ps, ct_hi_done, ct_lo_done, x_hi_done, x_lo_done = sem("xT_ps"), sem("ct_hi_done"), sem("ct_lo_done"), sem("x_hi_done"), sem("x_lo_done")
        k_ps, k_swapped, ku_done, kv_done, kr_done = sem("k_ps"), sem("k_swapped"), sem("ku_done"), sem("kv_done"), sem("kr_done")
        qbd_done = sem("qbd_done")
        s_ps, exp_done, clamp_done, p_hi_done, p_lo_done = sem("s_ps"), sem("exp_done"), sem("clamp_done"), sem("p_hi_done"), sem("p_lo_done")
        z_ps, rz_done, zn_done, zt_ps, zts_done, o_ps, o_done = (sem(n) for n in ("z_ps", "rz_done", "zn_done", "zt_ps", "zts_done", "o_ps", "o_done"))
        y_ps, y_done, out_st, bo_ld, x2_ld, xbo_done = (sem(n) for n in ("y_ps", "y_done", "out_st", "bo_ld", "x2_ld", "xbo_done"))

        def wait(eng, s, trip, count):
            if isinstance(trip, int):
                if trip * BODY + count > 0:
                    eng.wait_ge(s, trip * BODY + count)
            else:
                eng.wait_ge(s, trip * BODY + count)

        def there(trip, j):
            return not isinstance(trip, int) or 0 <= trip * BODY + j < STEPS

        def trips(eng, step):
            for j in range(0, BODY):
                step(0, j)
            with eng.Fori(1, TRIPS - 1) as trip:
                for j in range(BODY):
                    step(trip, j)
            for j in range(BODY + 2):
                step(TRIPS - 1, j)

        def groups(eng, group):
            group(0, 0)
            with eng.Fori(0, (GROUPS - 3) // 2) as r:
                group(r, 1)
                group(r, 2)
            group((GROUPS - 3) // 2, 1)
            group((GROUPS - 3) // 2, 2)

        def wait_group(eng, s, r, count, per=1, o=0):
            if not isinstance(r, int) or (2 * r + o) * per + count > 0:
                eng.wait_ge(s, r * (2 * per) + (o * per + count))

        def more(r, o, n=1):
            return not isinstance(r, int) or 2 * r + o + n < GROUPS

        def place(j):
            return (j // PAIRS) % 2, j % PAIRS

        def tile_before(g):
            return g - 9 + (g > PAIRS - 3)

        def rank_at(t):
            w = AH * (AD + 1)
            return bank[:, 3 + (t + 3) % 2, w:w + E] if t < TT - 3 else bank[:, t - (TT - 3), 0:E]

        def q_bank(g, c):
            return bank[:, 6 + c if g == PAIRS - 1 else 2 - 2 * (g % 2) + c, :]

        block = ctx.enter_context(nc.Block())

        @block.sync
        def _(sp):
            def ctx_rows(b):
                return ctx_1024[b].rearrange("(p t) d -> p t d", t=ST)

            sp.dma_start(cs_raw[:, 0], cos.rearrange("(p t) i -> p t i", t=ST)).then_inc(cs_ld, 16)
            sp.dma_start(cs_raw[:, 1], sin.rearrange("(p t) i -> p t i", t=ST)).then_inc(cs_ld, 16)
            sp.dma_start(xl, x.rearrange("b n d -> (b n) d").rearrange("(t p) d -> p t d", p=P)).then_inc(x_ld, 16)
            for i, v in enumerate((lat_g, lat_b, ctx_g, ctx_b)):
                sp.dma_start(vec_rows[i * KC:(i + 1) * KC, :], v.rearrange("(k p) -> k p", p=P)).then_inc(vec_ld, 16)
            kv = Wkv.rearrange("(k p) n -> p k n", p=P)
            sp.dma_start(wk_raw[:], kv[:, :, 0:INNER]).then_inc(wk_ld, 16)
            sp.dma_start(raw[:, 0], ctx_rows(0)).then_inc(ctx_ld[0], 16)
            sp.dma_start(wq_raw[:], Wq.rearrange("(k p) n -> p k n", p=P)).then_inc(wq_ld, 16)
            sp.dma_start(wv[:], kv[:, :, INNER:2 * INNER]).then_inc(wv_ld, 16)
            sp.dma_start(wo[:], Wo.rearrange("(g p) n -> p g n", p=P)).then_inc(wo_ld, 16)
            sp.wait_ge(latT_ps, TT)
            sp.dma_start(raw[:, 1], ctx_rows(1)).then_inc(ctx_ld[1], 16)
            with sp.Fori(1, TRIPS) as trip:
                for p in range(2):
                    wait(sp, xT_ps, trip, ST * (p - 1))
                    wait(sp, x_lo_done, trip, ST * (p - 1))
                    sp.dma_start(raw[:, p], ctx_1024[bass.ds(trip * 2 + p, 1)].rearrange("o (p t) d -> p (o t) d", t=ST)).then_inc(ctx_ld[p], 16)
            sp.wait_ge(x_lo_done, TILES)
            sp.wait_ge(xT_ps, TILES)
            sp.dma_start(bo_all, bo.partition_broadcast(P)).then_inc(bo_ld, 16)
            sp.dma_start(raw[:, 0], x.rearrange("b n d -> (b n) d").rearrange("(t p) d -> p t d", p=P)).then_inc(x2_ld, 16)
            sp.dma_start(wqkv_raw, Wqkv.rearrange("(r p) c -> p r c", p=P)).then_inc(lw_ld, 16)
            sp.wait_ge(o_ps, STEPS)
            sp.dma_start(vec_rows2[0:E * FT, :], b1.rearrange("e (f p) -> (e f) p", p=P)).then_inc(vec2_ld, 16)
            sp.dma_start(vec_rows2[E * FT:, :], bqkv[0:2 * D].rearrange("(r p) -> r p", p=P)).then_inc(vec2_ld, 16)
            sp.dma_start(wout_raw[:], Wout.rearrange("(r p) c -> p r c", p=P)).then_inc(lw_ld, 16)
            sp.wait_ge(feat_w_zero, 1)
            for h in range(AH):
                r = h % 8 * AD
                sp.dma_start(feat_w[r:r + AD, h // 2, h % 2 * AM:(h % 2 + 1) * AM], proj[h]).then_inc(proj_ld, 16)
            sp.dma_start(v_bias[:], bqkv[2 * D:3 * D].partition_broadcast(P)).then_inc(misc_ld, 16)
            sp.dma_start(bout_all[:], bout.partition_broadcast(P)).then_inc(misc_ld, 16)
            sp.dma_start(wg[:], Wg.rearrange("(k p) e -> p k e", p=P)).then_inc(misc_ld, 16)
            sp.dma_start(b2_rows[:], b2).then_inc(misc_ld, 16)
            sp.wait_ge(fill_done, 3)
            for g in range(E * TOK // ROWS + 1):
                sp.dma_start(x_slots[g * ROWS:(g + 1) * ROWS, :].rearrange("(s p) d -> p s d", p=P), fill[:]).then_inc(fill_st, 16)

            def number(table, r, o, most):
                return sp.value_load(table[0:1, bass.ds(r * 2 + o, 1)], min_val=0, max_val=most)

            def weights(b, e):
                sp.dma_start(w1_raw[:, b], W1[bass.ds(e, 1)].rearrange("o (k p) f -> p (o k) f", p=P)).then_inc(w_ld[b], 16)
                sp.dma_start(w2_raw[:, b], W2[bass.ds(e, 1)].rearrange("o (f p) d -> p (o f) d", p=P)).then_inc(w_ld[b], 16)

            def rows_in(b, at):
                sp.dma_start(xs[:, b], x_slots[bass.ds(at, ROWS), :].rearrange("(s p) d -> p s d", p=P)).then_inc(xs_ld[b], 16)

            sp.wait_ge(group_done, 1)
            weights(0, number(group_expert, 0, 0, E - 1))
            sp.wait_ge(group_done, 2)
            sp.wait_ge(scattered, 16 * TOPK * TT)
            rows_in(0, number(group_at, 0, 0, E * TOK))
            weights(1, number(group_expert, 0, 1, E - 1))
            rows_in(1, number(group_at, 0, 1, E * TOK))

            def group(r, o):
                if more(r, o, 2):
                    e, at = number(group_expert, r, o + 2, E - 1), number(group_at, r, o + 2, E * TOK)
                    wait_group(sp, w1_lo_done, r, 1, o=o)
                    wait_group(sp, w2_lo_done, r, 1, o=o)
                    weights(o % 2, e)
                    wait_group(sp, xs_ps, r, 1, o=o)
                    wait_group(sp, no_done, r, 1, o=o)
                    rows_in(o % 2, at)

            groups(sp, group)
            sp.wait_ge(ys_st[0], 32 * ((GROUPS + 1) // 2))
            sp.wait_ge(ys_st[1], 32 * (GROUPS // 2))
            for i in range(2):
                t = slice(4 * i, 4 * i + 4)
                for k in range(TOPK):
                    at = k * TOK + i * CH
                    sp.dma_start(result_of[:, k, t], results[at:at + CH, :].rearrange("(t p) d -> p t d", p=P)).then_inc(result_ld[i], 16)
            for t in range(TT):
                sp.wait_ge(acc_done, TOPK * (t + 1))
                sp.dma_start(out.rearrange("b n d -> (b n) d")[t * P:(t + 1) * P, :], raw[:, 0, t]).then_inc(out_st, 16)
            sp.wait_ge(out_st, 16 * TT)

        @block.gpsimd
        def _(pool):
            pool.memset(ident[:], 1.0).then_inc(ident_done, 1)
            pool.wait_ge(ident_done, 1)
            pool.affine_select(out=ident[:], in_=ident[:], compare_op=ALU.is_equal, fill=0.0, base=0,
                               pattern=[[-1, P]], channel_multiplier=1).then_inc(ident_done, 1)

            pool.wait_ge(consts_done, 1)
            for c in range(2):
                t = slice(c * TT // 2, (c + 1) * TT // 2)
                eps = consts[:, 3:4].to_broadcast([P, TT // 2])
                pool.wait_ge(xl_stats, (c + 1) * TT // 2)
                pool.tensor_tensor(xl_vpe[:, t], xl_mom[:, t, 1], eps, ALU.add).then_inc(xl_var, 1)
                pool.wait_ge(xl_var, 3 * c + 1)
                pool.tensor_tensor(xl_sum[:, t], xl_vpe[:, t], eps, ALU.mult).then_inc(xl_var, 1)
                pool.wait_ge(xl_var, 3 * c + 2)
                pool.tensor_tensor(xl_vpe[:, t], xl_sum[:, t], xl_mom[:, t, 1], ALU.add).then_inc(xl_var, 1)
                pool.wait_ge(xl_var, 3 * c + 3)
                pool.tensor_tensor(xl_rsd[:, t], xl_vpe[:, t], consts[:, 2:3].to_broadcast([P, TT // 2]), ALU.pow).then_inc(xl_rstd, 1)

            def step(trip, j):
                if there(trip, j + 1):
                    i = (j + 1) % 2
                    wait(pool, ku_done, trip, j + 2)
                    wait(pool, kv_done, trip, j + 2)
                    wait(pool, s_ps, trip, j)
                    pool.tensor_tensor(kr[:, i], ku[:, i], ksw[:, i], ALU.add).then_inc(kr_done, 1)
                if there(trip, j + 7):
                    b, t = place(j + 7)
                    wait(pool, x_hi_done, trip, j + 8)
                    pool.tensor_tensor(x_lo[:, b, t], raw[:, b, t], x_hi[:, b, t, 0:D].bitcast(F32), ALU.subtract).then_inc(x_lo_done, 1)
                if there(trip, j + 11):
                    i = (j + 11) % 2
                    wait(pool, stats_done, trip, j + 12)
                    pool.tensor_tensor(ve[:, i:i + 1], mv[:, i, 1:2], consts[:, 3:4], ALU.add).then_inc(var_done, 1)
                    wait(pool, var_done, trip, j + 12)
                    pool.tensor_tensor(rstd[:, i:i + 1], ve[:, i:i + 1], consts[:, 2:3], ALU.pow).then_inc(rstd_done, 1)

            for j in range(-11, 0):
                step(0, j)
            trips(pool, step)

            pool.wait_ge(o_ps, STEPS)
            pool.memset(square[:], 1.0).then_inc(mask_done, 1)
            pool.memset(feat_w[:], 0.0).then_inc(feat_w_zero, 1)
            for e in range(16):
                pool.memset(iota[:, e:e + 1], float(e))
            pool.memset(ones[:], 1.0)
            pool.memset(before[:, 0], 0.0)
            pool.memset(fill[:], 0.0).then_inc(fill_done, 1)
            pool.memset(cvec[:, 0:1], -0.5)
            pool.memset(cvec[:, 1:2], EPS).then_inc(lin_consts, 1)
            pool.wait_ge(mask_done, 1)
            pool.affine_select(out=square[:], in_=square[:], compare_op=ALU.is_ge, fill=0.0, base=0,
                               pattern=[[1, P]], channel_multiplier=-1).then_inc(mask_done, 1)
            pool.wait_ge(lin_consts, 1)

            def moment_scale(c, t):
                r = c * TT + t
                pool.wait_ge(l_stats, r + 1)
                pool.tensor_tensor(vpe[:, c, t:t + 1], mom[:, c, t, 1:2], cvec[:, 1:2], ALU.add).then_inc(l_var, 1)
                pool.wait_ge(l_var, r + 1)
                pool.tensor_tensor(rsd[:, c, t:t + 1], vpe[:, c, t:t + 1], cvec[:, 0:1], ALU.pow).then_inc(l_rstd, 1)

            def clear_values():
                pool.memset(vbd[:], 0.0).then_inc(vbd_zero, 1)
                pool.wait_ge(vbd_zero, 1)
                for h in range(2):
                    at = h * (AD + 1) + AD
                    pool.memset(vbd[h * 64:h * 64 + 64, :, :, :, at:at + 1], 1.0).then_inc(vbd_ones, 1)
                    pool.wait_ge(vbd_ones, h + 1)

            for t in range(TT):
                moment_scale(0, t)
                if t == 1:
                    clear_values()
                if t == 4:
                    pool.memset(feat_k[:], 0.0).then_inc(feat_k_zero, 1)

            def scatter(t):
                pool.wait_ge(slot_done, t + 1)
                for k in range(TOPK):
                    pool.indirect_dma_start(x_slots, bass.IndirectOffsetOnAxis(ap=slot[:, k, t:t + 1], axis=0), xn_all[:, k, t], None).then_inc(scattered, 16)

            for t in range(TT):
                moment_scale(1, t)
                if t == 2:
                    pool.wait_ge(fill_st, 16 * (E * TOK // ROWS + 1))
                if t >= 2:
                    scatter(t - 2)
            scatter(TT - 2)
            scatter(TT - 1)

            def group(r, o):
                b = (o + 1) % 2
                if more(r, o):
                    wait_group(pool, w1_hi_done, r, 2, o=o)
                    pool.tensor_tensor(w1_lo[:, b], w1_raw[:, b], w1_hi[:, b].bitcast(F32), ALU.subtract).then_inc(w1_lo_done, 1)
                wait_group(pool, no_done, r, 1, o=o)
                if o:
                    pool.wait_ge(ys_st[(o - 1) % 2], r * 32 + 32)
                for c in range(2):
                    wait_group(pool, ys_done, r, c + 1, 2, o)
                    wait_group(pool, spare_done, r, c, 2, o)
                    pool.tensor_tensor(spare[:, c:c + 1], cvec[:, 0:1], cvec[:, 0:1], ALU.add).then_inc(spare_done, 1)
                    pool.indirect_dma_start(results, bass.IndirectOffsetOnAxis(ap=result_no[:, o % 2, c:c + 1], axis=0), ys[:, o % 2, c], None).then_inc(ys_st[o % 2], 16)

            groups(pool, group)
        @block.scalar
        def _(act):
            act.wait_ge(vec_ps, 1)
            act.copy(vecs[:].rearrange("p v k -> p (v k)"), psZ[:, 0:4 * KC]).then_inc(vec_done, 1)
            for f, tab in enumerate((ctab, stab)):
                act.wait_ge(tab_ps, f + 1)
                act.copy(tab[:], (psK, psS)[f]).then_inc(tab_done, 1)

            def permute(src, dst, k, half):
                return (dst[:, k].rearrange("p (g a hi) -> p g a hi", a=2, hi=64)[:, :, half].rearrange("p g (h i) -> p g h i", h=2),
                        src[:, k].rearrange("p (g h a i) -> p g h a i", h=2, a=2, i=HALF)[:, :, :, half])

            act.wait_ge(wk_ld, 16)
            for k in range(KC):
                for half in range(2):
                    act.copy(*permute(wk_raw, wk_p, k, half)).then_inc(wk_perm, 1)
            act.wait_ge(vec_done, 1)
            for t in range(TT):
                act.wait_ge(latT_ps, t + 1)
                for k in range(KC):
                    last = act.activation(latT[:, k, t * P:(t + 1) * P], (psZT if t % 2 else psO)[:, k * P:(k + 1) * P], ACT.Identity,
                                          bias=vecs[:, 1, k:k + 1], scale=vecs[:, 0, k:k + 1])
                last.then_inc(latT_done, 1)
            act.wait_ge(wk_perm, 4)
            for k in range(KC):
                act.activation(wk_hi[:, k], wk_p[:, k], ACT.Identity, scale=vecs[:, 2, k:k + 1]).then_inc(wk_hi_done, 1)
            def step(trip, j):
                if there(trip, j + 1):
                    i = (j + 1) % 2
                    wait(act, k_ps, trip, j + 2)
                    wait(act, kr_done, trip, j)
                    act.copy(ksw[0:64, i], psK[64:128, :])
                    act.copy(ksw[64:128, i], psK[0:64, :]).then_inc(k_swapped, 1)
                if there(trip, j):
                    wait(act, s_ps, trip, j + 1)
                    wait(act, p_lo_done, trip, j)
                    act.activation(pr[:], psS, ACT.Exp, scale=SCALE).then_inc(exp_done, 1)
                if there(trip, j - 2):
                    wait(act, zt_ps, trip, j - 1)
                    wait(act, o_ps, trip, j - 2)
                    act.copy(zts[:], psZT[:, 0:D]).then_inc(zts_done, 1)
                if there(trip, j + 9):
                    b, t = place(j + 9)
                    wait(act, xT_ps, trip, j + 10)
                    if t == 0:
                        wait(act, k_ps, trip, j + 9 - PAIRS)
                    act.copy(ct_hi[:, b, :, t * P:(t + 1) * P], psT[:, 0:D].rearrange("p (k c) -> p k c", k=KC)).then_inc(ct_hi_done, 1)
                if there(trip, j):
                    i = j % 2
                    wait(act, clamp_done, trip, j + 1)
                    wait(act, z_ps, trip, j - 1)
                    act.copy(p_hi[:, i], pr[:]).then_inc(p_hi_done, 1)
                if there(trip, j - 1):
                    i = (j - 1) % 2
                    wait(act, rz_done, trip, j)
                    wait(act, zt_ps, trip, j - 1)
                    act.activation(zn[:], psZ[:, 0:D], ACT.Identity, scale=rz[:, i:i + 1]).then_inc(zn_done, 1)
                if there(trip, j - 2):
                    g = (j - 2) % PAIRS
                    wait(act, o_ps, trip, j - 1)
                    col = ((j - 2) // PAIRS + trip * 2) * N
                    for h in range(2):
                        rows = slice(h * 64, h * 64 + 64)
                        last = act.activation(qo[rows, g, bass.ds(col, N)], psO[rows, h * N:(h + 1) * N], ACT.Identity, bias=bias[rows, 2, g:g + 1])
                    last.then_inc(o_done, 1)

            def queries(g):
                act.wait_ge(q_ps, 2 * g + 1)
                act.copy(qo[:, g, 0:512], q_bank(g, 0)).then_inc(q_act, 1)

            for g in range(PAIRS - 1):
                step(0, tile_before(g))
                queries(g)
                if g == PAIRS - 3:
                    step(0, -3)
            step(0, -1)
            queries(PAIRS - 1)
            act.wait_ge(bias_ps, 2)
            for k in range(KC):
                act.activation(wv[:, k], wv[:, k], ACT.Identity, scale=vecs[:, 2, k:k + 1]).then_inc(wv_done, 1)
            trips(act, step)

            for r in range(8):
                act.wait_ge(lw_ps, r + 1)
                w, c = (wqkvT, r) if r < 6 else (woutT, r - 6)
                act.copy(w[:, :, c * P:(c + 1) * P], bank[:, 6 + r % 2, 0:D].rearrange("p (k c) -> p k c", k=KC)).then_inc(lw_done, 1)
            act.wait_ge(vec2_ps, 1)
            act.copy(vecs2[:], bank[:, 6, 0:E * FT + 4]).then_inc(vec2_done, 1)
            for t in range(TT):
                act.wait_ge(xnT_ps, t + 1)
                act.copy(xnT[:, :, t * P:(t + 1) * P], bank[:, 4 + t % 2, 0:D].rearrange("p (k c) -> p k c", k=KC)).then_inc(xnT_done, 1)
            act.wait_ge(vec2_done, 1)

            for r in range(8):
                act.wait_ge(qk_ps, r + 1)
                act.activation(qkT[:, r // 2, r % 2 * CH:(r % 2 + 1) * CH], bank[:, r % 4], ACT.Identity,
                               bias=vecs2[:, E * FT + r // 2:E * FT + r // 2 + 1]).then_inc(qk_done, 1)

            def feature(n):
                t, q, p, i = n // FEATS, n // 4 % 2, n % 4 * 2, n // FEATS % 2
                if t >= 2 and n % FEATS == 0:
                    act.wait_ge(am_ps, 4 * (t - 1))
                act.wait_ge(f_ps, n + 1)
                if q == 0:
                    act.activation(feat_q[:, i, p:p + 2], bank[:, 5 + n % 2, 0:2 * P].rearrange("p (g c) -> p g c", g=2), ACT.Relu).then_inc(f_done, 1)
                else:
                    for h in range(2):
                        rows = slice(h * 64, h * 64 + 64)
                        last = act.activation(feat_k[rows, i, p:p + 2, :, h * N:(h + 1) * N],
                                              bank[rows, 5 + n % 2, 0:2 * P].rearrange("p (g b c) -> p g b c", g=2, b=2), ACT.Relu)
                    last.then_inc(f_done, 1)

            def attention_turned(t):
                act.wait_ge(attT_ps, t + 1)
                if t >= 2:
                    act.wait_ge(w_ps, t - 1)
                act.copy(attT[:, t % 2], bank[:, 7, 0:D]).then_inc(attT_done, 1)

            def input_turned(t):
                act.wait_ge(xfT_ps, t + 1)
                if t >= 2:
                    act.wait_ge(logit_ps, t - 1)
                act.copy(xfT[:, t % 2], bank[:, 7, 0:D]).then_inc(xfT_done, 1)

            def follow(s, q):
                if q == 3:
                    attention_turned(s - 1)
                if q == 1 and s >= 3:
                    input_turned(s - 3)

            def follow_last(i):
                if i == 1:
                    attention_turned(TT - 1)
                if i in (3, 5):
                    input_turned(TT - 2 + i // 5)

            act.wait_ge(feat_k_zero, 1)
            for n in range(FEATS):
                feature(n)
            for r in range(4 * TT + 2):
                if r < 4 * TT:
                    for n in range(FEATS + 2 * r, FEATS + 2 * r + 2):
                        if n < FEATS * TT:
                            feature(n)
                if r >= 4:
                    follow(r // 4, r % 4)

            for i in range(7):
                follow_last(i)
            act.wait_ge(gap_done, 1)
            act.activation(gate[:, 1], gate[:, 0], ACT.Exp).then_inc(gap_exp, 1)

            def high_part(r, o, c):
                b = o % 2
                if c == 0:
                    act.wait_ge(w_ld[b], r * 32 + (o // 2 + 1) * 32)
                w, raw_w, s_done, n = (w1_hi, w1_raw, w1_hi_done, KC) if c < 2 else (w2_hi, w2_raw, w2_hi_done, FT)
                at = slice(c % 2 * n // 2, (c % 2 + 1) * n // 2)
                last = act.copy(w[:, b, at], raw_w[:, b, at])
                if c % 2 == 1:
                    last.then_inc(s_done, 1)

            def bias_of(r, o):
                e = act.value_load(group_expert[0:1, bass.ds(r * 2 + o, 1)], min_val=0, max_val=E - 1)
                act.copy(b1_now[:, o % 2], vecs2[:, bass.ds(e * FT, FT)]).then_inc(b1_done, 1)

            def rows_high(r, o):
                wait_group(act, xs_ps, r, 1, o=o)
                act.copy(xs_hi[:].rearrange("p k c -> p (k c)"), bank[:, 6]).then_inc(xs_hi_done, 1)

            act.wait_ge(group_done, 1)
            bias_of(0, 0)
            for t in range(0, TT, 4):
                act.wait_ge(combT_ps, t // 4 + 1)
                act.copy(combT[:, t * P:(t + 4) * P], bank[0:E, 4 + t // 4]).then_inc(combT_done, 1)
            high_part(0, 0, 0)
            high_part(0, 0, 1)
            rows_high(0, 0)
            high_part(0, 0, 2)
            high_part(0, 0, 3)

            def group(r, o):
                wait_group(act, b1_done, r, 1, o=o)
                for f in range(FT):
                    wait_group(act, h_ps, r, f + 1, FT, o)
                    wait_group(act, h_lo_done, r, f - 3, FT, o)
                    act.activation(hid[:, f % 4], bank[:, f % 4, 0:ROWS], ACT.Relu, bias=b1_now[:, o % 2, f:f + 1]).then_inc(relu_done, 1)
                    if f in (1, 3) and more(r, o):
                        high_part(r, o + 1, f // 2)
                if more(r, o):
                    rows_high(r, o + 1)
                    bias_of(r, o + 1)
                    for c in (2, 3):
                        high_part(r, o + 1, c)
                for c in range(2):
                    wait_group(act, e_ps, r, c + 1, 2, o)
                    if c == 0 and not (isinstance(r, int) and r == 0 and o < 2):
                        act.wait_ge(ys_st[o % 2], r * 32 + o // 2 * 32)
                    act.copy(ys[:, o % 2, c], bank[:, 4 + c, 0:D]).then_inc(ys_done, 1)

            groups(act, group)

        @block.vector
        def _(dve):
            for c, v in ((2, -0.5), (3, EPS)):
                dve.memset(consts[:, c:c + 1], v)
            for h in range(2):
                for half in range(2):
                    r = half * 64 + h * 32
                    dve.memset(consts[r:r + 32, h:h + 1], 1.0)
                    dve.memset(consts[r:r + 32, 1 - h:2 - h], 0.0)
            dve.memset(x_hi[:, :, :, D:D + 2].bitcast(F32), 1.0)
            dve.memset(rz[:], 0.0).then_inc(consts_done, 1)

            dve.wait_ge(cs_ld, 32)
            for f in range(2):
                for r in range(4):
                    o = crep[:, f, :, r * HALF:(r + 1) * HALF]
                    last = dve.tensor_scalar(o, cs_raw[:, f], -1.0 if f == 1 and r < 2 else 1.0, None, ALU.mult)
            last.then_inc(crep_done, 1)

            dve.wait_ge(x_ld, 16)
            for t in range(TT + TT // 2):
                if t < TT:
                    dve.bn_stats(xl_st6[:, t], xl[:, t]).then_inc(xl_bn, 1)
                    dve.wait_ge(xl_bn, t + 1)
                    dve.bn_aggr(xl_mom[:, t], xl_st6[:, t]).then_inc(xl_stats, 1)
                if t >= TT // 2:
                    u = t - TT // 2
                    dve.wait_ge(xl_rstd, u // (TT // 2) + 1)
                    dve.tensor_scalar(xl[:, u], xl[:, u], xl_mom[:, u, 0:1], xl_rsd[:, u:u + 1], ALU.subtract, ALU.mult).then_inc(xl_norm, 1)

            dve.wait_ge(wq_ld, 16)
            for k in range(KC):
                for half in range(2):
                    dve.tensor_copy(wq_p[:, k].rearrange("p (g a hi) -> p g a hi", a=2, hi=64)[:, :, half].rearrange("p g (h i) -> p g h i", h=2),
                                    wq_raw[:, k].rearrange("p (g h a i) -> p g h a i", h=2, a=2, i=HALF)[:, :, :, half]).then_inc(wq_perm, 1)

            def key_weights(k):
                dve.wait_ge(wk_perm, 4)
                dve.wait_ge(vec_done, 1)
                dve.wait_ge(wk_hi_done, k + 1)
                dve.scalar_tensor_tensor(out=wk_lo[:, k], in0=wk_p[:, k], scalar=vecs[:, 2, k:k + 1], in1=wk_hi[:, k].bitcast(F32),
                                         op0=ALU.mult, op1=ALU.subtract).then_inc(wk_lo_done, 1)

            def biases(c):
                dve.wait_ge(bias_ps, c + 1)
                if c == 0:
                    dve.tensor_copy(bias[:, 0], psZ[:, 0:8])
                    dve.tensor_copy(bias[0:64, 1], psZ[64:128, 0:8])
                    dve.tensor_copy(bias[64:128, 1], psZ[0:64, 0:8]).then_inc(bias_done, 1)
                else:
                    dve.tensor_copy(bias[:, 2], psZ[:, 0:8]).then_inc(bias_done, 1)

            def queries(trip, b, buf):
                for h in range(2):
                    last = dve.tensor_scalar(qbd[:, buf, :, h * N:(h + 1) * N], qo[:, :, bass.ds((trip * 2 + b) * N, N)], consts[:, h:h + 1], None, ALU.mult)
                last.then_inc(qbd_done, 1)

            def step(trip, j):
                if there(trip, j + 1):
                    i, g = (j + 1) % 2, (j + 1) % PAIRS
                    wait(dve, k_swapped, trip, j + 2)
                    wait(dve, kr_done, trip, j)
                    dve.scalar_tensor_tensor(out=ku[:, i], in0=psK, scalar=bias[:, 0, g:g + 1], in1=ctab[:], op0=ALU.add, op1=ALU.mult).then_inc(ku_done, 1)
                if there(trip, j + 1):
                    dve.scalar_tensor_tensor(out=ksw[:, i], in0=ksw[:, i], scalar=bias[:, 1, g:g + 1], in1=stab[:], op0=ALU.add, op1=ALU.mult).then_inc(kv_done, 1)
                if there(trip, j):
                    wait(dve, exp_done, trip, j + 1)
                    dve.tensor_scalar(pr[:], pr[:], LOW, HIGH, ALU.max, ALU.min).then_inc(clamp_done, 1)
                if there(trip, j + 9):
                    b, t = place(j + 9)
                    cols = slice(t * P, (t + 1) * P)
                    wait(dve, ct_hi_done, trip, j + 10)
                    dve.tensor_tensor(ct_lo[:, b, :, cols], psT[:, 0:D].rearrange("p (k c) -> p k c", k=KC),
                                      ct_hi[:, b, :, cols].bitcast(F32), ALU.subtract).then_inc(ct_lo_done, 1)
                if there(trip, j - 1):
                    i = (j - 1) % 2
                    wait(dve, z_ps, trip, j)
                    dve.reciprocal(rz[:, i:i + 1], psZ[:, D:D + 1]).then_inc(rz_done, 1)
                if there(trip, j):
                    i = j % 2
                    wait(dve, p_hi_done, trip, j + 1)
                    wait(dve, z_ps, trip, j - 1)
                    dve.tensor_tensor(p_lo[:, i], pr[:], p_hi[:, i].bitcast(F32), ALU.subtract).then_inc(p_lo_done, 1)
                if there(trip, j + 7):
                    b, t = place(j + 7)
                    if t == 0:
                        wait(dve, z_ps, trip, j + 7 - PAIRS)
                    wait(dve, xhat_done, trip, j + 8)
                    dve.tensor_copy(x_hi[:, b, t, 0:D], raw[:, b, t]).then_inc(x_hi_done, 1)
                if there(trip, j + 11):
                    b, t = place(j + 11)
                    if t == 0:
                        n = (j + 11) // ST // 2 + 1
                        dve.wait_ge(ctx_ld[b], (trip + n) * 16)
                    dve.bn_stats(bst[:, (j + 11) % 2], raw[:, b, t]).then_inc(bn_done, 1)
                    wait(dve, bn_done, trip, j + 12)
                if there(trip, j + 10):
                    b, t = place(j + 10)
                    i = (j + 10) % 2
                    wait(dve, rstd_done, trip, j + 11)
                    dve.tensor_scalar(raw[:, b, t], raw[:, b, t], mv[:, i, 0:1], rstd[:, i:i + 1], ALU.subtract, ALU.mult).then_inc(xhat_done, 1)
                if there(trip, j + 11):
                    i = (j + 11) % 2
                    dve.bn_aggr(mv[:, i], bst[:, i]).then_inc(stats_done, 1)
                if j >= 0 and j % PAIRS == PAIRS - 2 and there(trip, j + 2):
                    queries(trip, j // PAIRS + 1, (j // PAIRS + 1) % 2)

            step(0, -11)
            step(0, -10)
            def half_queries(g):
                dve.wait_ge(q_ps, 2 * g + 2)
                dve.tensor_copy(qo[:, g, 512:1024], q_bank(g, 1)).then_inc(q_dve, 1)

            for g in range(PAIRS - 1):
                step(0, tile_before(g))
                if g == PAIRS - 3:
                    step(0, -3)
                half_queries(g)
                if g in (1, 2):
                    key_weights(g - 1)
            biases(0)
            dve.wait_ge(bias_done, 1)
            dve.wait_ge(tab_done, 2)
            step(0, -1)
            half_queries(PAIRS - 1)
            dve.wait_ge(q_act, PAIRS)
            dve.wait_ge(q_dve, PAIRS)
            queries(0, 0, 0)
            biases(1)
            trips(dve, step)
            dve.wait_ge(bo_ld, 16)
            dve.wait_ge(x2_ld, 16)
            dve.tensor_tensor(raw[:, 0], raw[:, 0], bo_all.unsqueeze(1).to_broadcast([P, TT, D]), ALU.add).then_inc(xbo_done, 1)
            dve.wait_ge(xbo_done, 1)

            def moments(c, t):
                r = c * TT + t
                dve.bn_stats(st6[:, c, t], raw[:, 0, t]).then_inc(l_bn, 1)
                dve.wait_ge(l_bn, r + 1)
                dve.bn_aggr(mom[:, c, t], st6[:, c, t]).then_inc(l_stats, 1)

            def normalise(c, t):
                r = c * TT + t
                dve.wait_ge(l_rstd, r + 1)
                dve.wait_ge(l_stats, r + 1)
                if c == 0 and t >= 2:
                    dve.wait_ge(xnT_ps, t - 1)
                for to in (xn_all[:, 1, t, 0:D], xn_all[:, 0, t, 0:D]) if c else (xn[:, t % 2],):
                    last = dve.tensor_scalar(to, raw[:, 0, t], mom[:, c, t, 0:1], rsd[:, c, t:t + 1], ALU.subtract, ALU.mult)
                last.then_inc(xn_done, 1)

            for t in range(TT + 1):
                if t < TT:
                    dve.wait_ge(y_ps, t + 1)
                    dve.tensor_tensor(raw[:, 0, t], bank[:, t % 4, 0:D], raw[:, 0, t], ALU.add).then_inc(y_done, 1)
                    dve.wait_ge(y_done, t + 1)
                    moments(0, t)
                if t > 0:
                    normalise(0, t - 1)
            dve.wait_ge(misc_ld, 64)
            for t in range(TT):
                dve.wait_ge(v_ps, t + 1)
                dve.wait_ge(vbd_ones, 2)
                for b in range(2):
                    rows = slice(b * N, (b + 1) * N)
                    for h in range(2):
                        at = h * (AD + 1)
                        last = dve.tensor_tensor(vbd[h * 64:h * 64 + 64, t, b, :, at:at + AD],
                                                 bank[rows, 6 + t % 2, 0:D].rearrange("p (g h d) -> p g h d", g=APAIRS, h=2)[:, :, h],
                                                 v_bias[rows, :].rearrange("p (g h d) -> p g h d", g=APAIRS, h=2)[:, :, h], ALU.add)
                last.then_inc(v_done, 1)
            dve.tensor_tensor(raw[:, 0], raw[:, 0], bout_all[:].unsqueeze(1).to_broadcast([P, TT, D]), ALU.add).then_inc(x1b_done, 1)
            dve.wait_ge(mask_done, 2)
            for h in range(2):
                dve.tensor_copy(mask[h * N:(h + 1) * N, :], square[h * N:(h + 1) * N, h * N:(h + 1) * N]).then_inc(mask_done, 1)
            dve.wait_ge(mask_done, 4)

            dve.tensor_reduce(numbers[:, 0:1], square[:], mybir.AxisListType.X, ALU.add).then_inc(count_rows, 1)
            dve.wait_ge(count_rows, 1)
            dve.tensor_scalar(numbers[:, 1:2], numbers[:, 0:1], -1.0, float(P), ALU.mult, ALU.add).then_inc(count_rows, 1)
            dve.wait_ge(count_rows, 2)
            dve.wait_ge(fill_done, 1)
            dve.tensor_scalar(slot_0[:], iota[:, 0:E], float(TOK), -1.0, ALU.mult, ALU.add)
            for k in range(TOPK):
                dve.scalar_tensor_tensor(out=xn_all[:, k, :, D], in0=iota[:, k * TT:(k + 1) * TT], scalar=float(P), in1=numbers[:, 1:2].to_broadcast([P, TT]),
                                         op0=ALU.mult, op1=ALU.add)
            for c in range(2):
                dve.tensor_scalar(fill[:, c, D:D + 1], numbers[:, 1:2], float(TOPK * TOK + c * P), None, ALU.add).then_inc(fill_done, 1)

            def masked(t, q):
                r = 4 * t + q
                if t >= 2 and q == 0:
                    dve.wait_ge(c_ps, t - 1)
                dve.wait_ge(am_ps, r + 1)
                dve.tensor_tensor(am[:, t % 2, q], bank[:, r % 3, 0:4 * N].rearrange("p (u c) -> p u c", u=4),
                                  mask[:].unsqueeze(1).to_broadcast([P, 4, N]), ALU.mult).then_inc(am_done, 1)

            def result(t):
                i = t % 2
                dve.wait_ge(c_ps, t + 1)
                cv = bank[:, 3 + i, 0:AH * (AD + 1)].rearrange("p (h d) -> p h d", h=AH)
                dve.tensor_scalar(rec[:, i, 0], cv[:, :, AD], 1e-6, None, ALU.add).then_inc(den_done, 1)
                dve.wait_ge(den_done, t + 1)
                dve.reciprocal(rec[:, i, 1], rec[:, i, 0]).then_inc(rec_done, 1)
                dve.wait_ge(rec_done, t + 1)
                if t >= 2:
                    dve.wait_ge(attT_ps, t - 1)
                dve.tensor_tensor(att[:, i].rearrange("p (h d) -> p h d", h=AH), cv[:, :, 0:AD],
                                  rec[:, i, 1].unsqueeze(2).to_broadcast([P, AH, AD]), ALU.mult).then_inc(att_done, 1)

            def residual(t):
                dve.wait_ge(w_ps, t + 1)
                dve.wait_ge(x1b_done, 1)
                dve.tensor_tensor(raw[:, 0, t], bank[:, 7, 0:D], raw[:, 0, t], ALU.add).then_inc(x2_done, 1)
                dve.wait_ge(x2_done, t + 1)
                moments(1, t)

            def gating(t):
                dve.wait_ge(logit_ps, t + 1)
                dve.tensor_copy(logit[:, t], bank[:, 7, 0:E]).then_inc(logit_done, 1)
                dve.wait_ge(logit_done, t + 1)
                dve.max(top[:, t], logit[:, t]).then_inc(top_done, 1)
                dve.wait_ge(top_done, 3 * t + 1)
                dve.max_index(top_at[:, t], top[:, t], logit[:, t]).then_inc(top_done, 1)
                dve.wait_ge(top_done, 3 * t + 2)
                dve.tensor_copy(top_f[:, t], top_at[:, t, 0:2]).then_inc(top_done, 1)
                dve.wait_ge(top_done, 3 * t + 3)
                for k in range(TOPK):
                    dve.tensor_scalar(pick[:, k, t], iota[:, 0:E], top_f[:, t, k:k + 1], None, ALU.is_equal).then_inc(pick_done, 1)
                dve.wait_ge(pick_done, 2 * t + 2)
                dve.tensor_tensor(picked[:, t], pick[:, 0, t], pick[:, 1, t], ALU.add).then_inc(chosen, 1)
                dve.wait_ge(chosen, t + 1)
                if t >= 1:
                    dve.wait_ge(prefix_done, t)
                dve.tensor_tensor(before[:, t + 1], before[:, t], picked[:, t], ALU.add).then_inc(prefix_done, 1)

            def slots(t):
                if t < TT - 3:
                    dve.wait_ge(c_ps, t + 4)
                dve.wait_ge(rank_ps, t + 1)
                dve.tensor_tensor(of_slot[:, t], rank_at(t), slot_0[:], ALU.add).then_inc(slot_step, 1)
                dve.wait_ge(slot_step, 3 * t + 1)
                dve.tensor_tensor(slot_of[:, t], pick[:, :, t], of_slot[:, t].unsqueeze(1).to_broadcast([P, TOPK, E]), ALU.mult).then_inc(slot_step, 1)
                dve.wait_ge(slot_step, 3 * t + 2)
                dve.tensor_reduce(slot_f[:, :, t], slot_of[:, t], mybir.AxisListType.X, ALU.add).then_inc(slot_step, 1)
                dve.wait_ge(slot_step, 3 * t + 3)
                dve.tensor_copy(slot[:, :, t], slot_f[:, :, t]).then_inc(slot_done, 1)

            def follow(s, q):
                if q == 1 and s >= 2:
                    residual(s - 2)
                if q == 2:
                    if s >= 4:
                        slots(s - 4)
                    result(s - 1)
                    if s >= 2:
                        normalise(1, s - 2)
                if q == 3 and s >= 3:
                    gating(s - 3)

            def follow_last(i):
                if i == 0:
                    gating(TT - 3)
                if i == 2:
                    residual(TT - 1)
                if i == 3:
                    normalise(1, TT - 1)
                    slots(TT - 3)
                if i == 4:
                    gating(TT - 2)
                if i == 6:
                    slots(TT - 2)
                    gating(TT - 1)

            for r in range(4 * TT + 3):
                if r < 4 * TT:
                    masked(r // 4, r % 4)
                if r >= 4:
                    follow(r // 4, r % 4)

            for i in range(7):
                follow_last(i)

            dve.wait_ge(top_done, 3 * TT)
            dve.wait_ge(total_ps, 1)
            rows_of = bank[:, 3, 0:E]
            dve.tensor_scalar(n_exp[:, 0], rows_of, 0.0, None, ALU.is_gt).then_inc(count_done, 1)
            for j in range(1, TOK // ROWS):
                dve.wait_ge(count_done, j)
                dve.scalar_tensor_tensor(out=n_exp[:, 0], in0=rows_of, scalar=float(j * ROWS), in1=n_exp[:, 0], op0=ALU.is_gt, op1=ALU.add).then_inc(count_done, 1)
            n = TOK // ROWS
            dve.wait_ge(count_done, n)
            dve.tensor_copy(n_exp[:, 1, 0:1], n_exp[:, 0, 0:1]).then_inc(count_done, 1)
            for e in range(1, E):
                dve.wait_ge(count_done, n + e)
                dve.tensor_tensor(n_exp[:, 1, e:e + 1], n_exp[:, 1, e - 1:e], n_exp[:, 0, e:e + 1], ALU.add).then_inc(count_done, 1)
            n += E
            dve.wait_ge(count_done, n)
            dve.tensor_tensor(group_cmp[:], iota[:].unsqueeze(2).to_broadcast([P, 16, E]), n_exp[:, 1].unsqueeze(1).to_broadcast([P, 16, E]),
                              ALU.is_ge).then_inc(count_done, 1)
            dve.tensor_tensor(n_exp[:, 2], n_exp[:, 1], n_exp[:, 0], ALU.subtract).then_inc(count_done, 1)
            dve.wait_ge(count_done, n + 1)
            dve.tensor_reduce(group_f[:], group_cmp[:], mybir.AxisListType.X, ALU.add).then_inc(count_done, 1)
            dve.wait_ge(count_done, n + 3)
            dve.tensor_scalar(group_expert[:], group_f[:], float(E - 1), None, ALU.min).then_inc(group_done, 1)
            slots(TT - 1)
            dve.tensor_tensor(gate[:, 0], top[:, :, 1], top[:, :, 0], ALU.subtract).then_inc(gap_done, 1)
            n += 3
            dve.tensor_tensor(group_in[:], iota[:].unsqueeze(2).to_broadcast([P, 16, E]), n_exp[:, 2].unsqueeze(1).to_broadcast([P, 16, E]),
                              ALU.is_ge).then_inc(count_done, 1)
            dve.wait_ge(count_done, n + 1)
            dve.tensor_tensor(group_in[:], group_in[:], group_cmp[:], ALU.subtract).then_inc(count_done, 1)
            dve.scalar_tensor_tensor(out=n_exp[:, 2], in0=n_exp[:, 2], scalar=-float(ROWS), in1=slot_0[:], op0=ALU.mult, op1=ALU.add).then_inc(count_done, 1)
            dve.tensor_scalar(group_r[:], iota[:], float(ROWS), 1.0 - E * TOK, ALU.mult, ALU.add).then_inc(count_done, 1)
            dve.wait_ge(count_done, n + 4)
            dve.tensor_tensor(group_v[:], group_r[:].unsqueeze(2).to_broadcast([P, 16, E]), n_exp[:, 2].unsqueeze(1).to_broadcast([P, 16, E]),
                              ALU.add).then_inc(count_done, 1)
            dve.wait_ge(count_done, n + 5)
            dve.tensor_tensor(group_v[:], group_v[:], group_in[:], ALU.mult).then_inc(count_done, 1)
            dve.wait_ge(count_done, n + 6)
            dve.tensor_reduce(group_r[:], group_v[:], mybir.AxisListType.X, ALU.add).then_inc(count_done, 1)
            dve.wait_ge(count_done, n + 7)
            dve.tensor_scalar(group_at[:], group_r[:], float(E * TOK), None, ALU.add).then_inc(group_done, 1)

            dve.wait_ge(gap_exp, 1)
            dve.tensor_scalar(gate[:, 0], gate[:, 1], 1.0, None, ALU.add).then_inc(gate_done, 1)
            dve.wait_ge(gate_done, 1)
            dve.reciprocal(gate[:, 2], gate[:, 0]).then_inc(gate_done, 1)
            dve.wait_ge(gate_done, 2)
            dve.tensor_tensor(gate[:, 3], gate[:, 1], gate[:, 2], ALU.mult).then_inc(gate_done, 1)
            dve.wait_ge(gate_done, 3)
            dve.wait_ge(slot_done, TT)
            for k in range(TOPK):
                dve.tensor_tensor(pick[:, k], pick[:, k], gate[:, 2 + k].unsqueeze(2).to_broadcast([P, TT, E]), ALU.mult).then_inc(pick_done, 1)
            dve.wait_ge(pick_done, 2 * TT + TOPK)
            dve.tensor_tensor(comb[:], pick[:, 0], pick[:, 1], ALU.add).then_inc(comb_done, 1)

            def low_part(r, o, w, s_hi, s_lo):
                lo, hi, rw = ((w1_lo, w1_hi, w1_raw), (w2_lo, w2_hi, w2_raw))[w]
                wait_group(dve, s_hi, r, 1, o=o)
                dve.tensor_tensor(lo[:, o % 2], rw[:, o % 2], hi[:, o % 2].bitcast(F32), ALU.subtract).then_inc(s_lo, 1)

            def rows_low(r, o):
                wait_group(dve, xs_hi_done, r, 1, o=o)
                dve.tensor_tensor(xs_lo[:].rearrange("p k c -> p (k c)"), bank[:, 6], xs_hi[:].rearrange("p k c -> p (k c)").bitcast(F32),
                                  ALU.subtract).then_inc(xs_lo_done, 1)
                if not (isinstance(r, int) and r == 0 and o < 2):
                    dve.wait_ge(ys_st[o % 2], r * 32 + o // 2 * 32)
                dve.tensor_copy(result_no[:, o % 2], xs[:, o % 2, :, D]).then_inc(no_done, 1)

            for t in range(TT):
                dve.wait_ge(b2_ps, t + 1)
                dve.tensor_tensor(raw[:, 0, t], bank[:, (0, 1, 2, 7)[t % 4], 0:D], raw[:, 0, t], ALU.add).then_inc(acc_b2, 1)
            low_part(0, 0, 0, w1_hi_done, w1_lo_done)
            rows_low(0, 0)
            low_part(0, 0, 1, w2_hi_done, w2_lo_done)

            def group(r, o):
                for f in range(FT):
                    wait_group(dve, relu_done, r, f + 1, FT, o)
                    dve.tensor_copy(h_hi[:, f], hid[:, f % 4]).then_inc(h_hi_done, 1)
                    wait_group(dve, h_hi_done, r, f + 1, FT, o)
                    dve.tensor_tensor(h_lo[:, f], hid[:, f % 4], h_hi[:, f].bitcast(F32), ALU.subtract).then_inc(h_lo_done, 1)
                if more(r, o):
                    rows_low(r, o + 1)
                    low_part(r, o + 1, 1, w2_hi_done, w2_lo_done)

            groups(dve, group)
            for t in range(TT):
                dve.wait_ge(result_ld[t // 4], 16 * TOPK)
                dve.wait_ge(acc_b2, t + 1)
                for k in range(TOPK):
                    if k:
                        dve.wait_ge(acc_done, TOPK * t + k)
                    dve.scalar_tensor_tensor(out=raw[:, 0, t], in0=result_of[:, k, t], scalar=gate[:, 2 + k, t:t + 1],
                                             in1=raw[:, 0, t], op0=ALU.mult, op1=ALU.add).then_inc(acc_done, 1)

        @block.tensor
        def _(pe):
            pe.wait_ge(ident_done, 2)
            pe.wait_ge(vec_ld, 64)
            pe.transpose(psZ[:, 0:4 * KC], vec_rows[:], ident[0:4 * KC, 0:4 * KC]).then_inc(vec_ps, 1)
            pe.wait_ge(crep_done, 1)
            for f in range(2):
                for t in range(ST):
                    last = pe.transpose((psK, psS)[f][:, t * P:(t + 1) * P], crep[:, f, t], ident[:])
                last.then_inc(tab_ps, 1)
            for t in range(TT):
                pe.wait_ge(xl_norm, t + 1)
                if t >= 2:
                    pe.wait_ge(latT_done, t - 1)
                for k in range(KC):
                    last = pe.transpose((psZT if t % 2 else psO)[:, k * P:(k + 1) * P], xl[:, t, k * P:(k + 1) * P], ident[:])
                last.then_inc(latT_ps, 1)
            def biases(c, g):
                for k in range(KC):
                    last = pe.matmul(psZ[:, g:g + 1], (wk_p, wv)[c][:, k, g * P:(g + 1) * P], vecs[:, 3, k:k + 1],
                                     start=(k == 0), stop=(k == KC - 1))
                if g == PAIRS - 1:
                    last.then_inc(bias_ps, 1)

            def step(trip, j):
                if there(trip, j + 1):
                    b, g = place(j + 1)
                    w = slice(g * P, (g + 1) * P)
                    wait(pe, ku_done, trip, j + 1)
                    if g == 0:
                        wait(pe, ct_lo_done, trip, j + 1 + PAIRS)
                    for c in range(2):
                        cols = slice(c * 512, (c + 1) * 512)
                        parts = [(l, r, k) for k in range(KC) for l, r in ((wk_hi, ct_hi), (wk_hi, ct_lo), (wk_lo, ct_hi))]
                        for m, (l, r, k) in enumerate(parts):
                            last = pe.matmul(psK[:, cols], l[:, k, w], r[:, b, k, cols], start=(m == 0), stop=(m == len(parts) - 1))
                    last.then_inc(k_ps, 1)
                if there(trip, j):
                    b, g = place(j)
                    wait(pe, kr_done, trip, j + 1)
                    wait(pe, exp_done, trip, j)
                    if g == 0:
                        pe.wait_ge(qbd_done, trip * 2 + (j // PAIRS + 1))
                    for t in range(ST):
                        last = pe.matmul(psS[:, t * P:(t + 1) * P], kr[:, j % 2, t * P:(t + 1) * P], qbd[:, b, g], start=True, stop=True)
                    last.then_inc(s_ps, 1)
                if there(trip, j + 9):
                    b, t = place(j + 9)
                    wait(pe, xhat_done, trip, j + 10)
                    wait(pe, ct_lo_done, trip, j + 9)
                    for k in range(KC):
                        last = pe.transpose(psT[:, k * P:(k + 1) * P], raw[:, b, t, k * P:(k + 1) * P], ident[:])
                    last.then_inc(xT_ps, 1)
                if there(trip, j - 2):
                    wait(pe, zn_done, trip, j - 1)
                    wait(pe, zts_done, trip, j - 2)
                    for k in range(KC):
                        last = pe.transpose(psZT[:, k * P:(k + 1) * P], zn[:, k * P:(k + 1) * P], ident[:])
                    last.then_inc(zt_ps, 1)
                if isinstance(trip, int) and trip * BODY + j == 1:
                    pe.wait_ge(bias_done, 2)
                    pe.wait_ge(q_act, PAIRS)
                    pe.wait_ge(q_dve, PAIRS)
                    pe.wait_ge(wv_done, 2)
                if there(trip, j - 1):
                    b, g = place(j - 1)
                    i = (j - 1) % 2
                    wait(pe, p_lo_done, trip, j)
                    wait(pe, zn_done, trip, j - 1)
                    if g == 0:
                        wait(pe, x_lo_done, trip, j - 1 + PAIRS)
                    for t in range(ST):
                        c = slice(t * P, (t + 1) * P)
                        pe.matmul(psZ[:, 0:D + 2], p_hi[:, i, c], x_hi[:, b, t], start=(t == 0), stop=False, skip_group_check=True)
                        pe.matmul(psZ[:, 0:D], p_hi[:, i, c], x_lo[:, b, t], start=False, stop=False, skip_group_check=True)
                        last = pe.matmul(psZ[:, 0:D + 2], p_lo[:, i, c], x_hi[:, b, t], start=False, stop=(t == ST - 1), skip_group_check=True)
                    last.then_inc(z_ps, 1)
                if there(trip, j - 2):
                    g = (j - 2) % PAIRS
                    wait(pe, zts_done, trip, j - 1)
                    wait(pe, o_done, trip, j - 2)
                    for k in range(KC):
                        last = pe.matmul(psO[:, 0:P], wv[:, k, g * P:(g + 1) * P], zts[:, k * P:(k + 1) * P], start=(k == 0), stop=(k == KC - 1))
                    last.then_inc(o_ps, 1)

            def queries(g):
                for c in range(2):
                    if g >= 2:
                        pe.wait_ge((q_act, q_dve)[c], g - 1)
                    for k in range(KC):
                        last = pe.matmul(q_bank(g, c), wq_p[:, k, g * P:(g + 1) * P], latT[:, k, c * 512:(c + 1) * 512], start=(k == 0), stop=(k == KC - 1))
                    last.then_inc(q_ps, 1)
                    if g == PAIRS - 3 and c == 0:
                        step(0, -3)

            pe.wait_ge(latT_done, TT)
            pe.wait_ge(tab_done, 2)
            pe.wait_ge(wk_perm, 4)
            pe.wait_ge(vec_done, 1)
            for g in range(PAIRS - 1):
                step(0, tile_before(g))
                pe.wait_ge(wq_perm, 4)
                queries(g)
                biases(0, g)
            biases(0, PAIRS - 1)
            pe.wait_ge(q_act, PAIRS - 2)
            pe.wait_ge(q_dve, PAIRS - 2)
            pe.wait_ge(wk_lo_done, 2)
            pe.wait_ge(consts_done, 1)
            step(0, -1)
            queries(PAIRS - 1)
            pe.wait_ge(wv_ld, 16)
            pe.wait_ge(bias_done, 1)
            for g in range(PAIRS):
                biases(1, g)
            trips(pe, step)
            pe.wait_ge(wo_ld, 16)
            pe.wait_ge(o_done, STEPS)

            def turn(t):
                pe.wait_ge(xn_done, t + 1)
                if t >= 2:
                    pe.wait_ge(xnT_done, t - 1)
                for k in range(KC):
                    last = pe.transpose(bank[:, 4 + t % 2, k * P:(k + 1) * P], xn[:, t % 2, k * P:(k + 1) * P], ident[:])
                last.then_inc(xnT_ps, 1)

            for t in range(TT + 2):
                if t < TT:
                    if t >= 4:
                        pe.wait_ge(y_done, t - 3)
                    for g in range(PAIRS):
                        last = pe.matmul(bank[:, t % 4, 0:D], qo[:, g, t * P:(t + 1) * P], wo[:, g], start=(g == 0), stop=(g == PAIRS - 1))
                    last.then_inc(y_ps, 1)
                if t == 1:
                    pe.wait_ge(lw_ld, 32)
                    for r in range(8):
                        if r >= 2:
                            pe.wait_ge(lw_done, r - 1)
                        w, c = (wqkv_raw, r) if r < 6 else (wout_raw, r - 6)
                        for k in range(KC):
                            last = pe.transpose(bank[:, 6 + r % 2, k * P:(k + 1) * P], w[:, c, k * P:(k + 1) * P], ident[:])
                        last.then_inc(lw_ps, 1)
                    pe.wait_ge(vec2_ld, 32)
                    pe.wait_ge(lw_done, 7)
                    pe.transpose(bank[:, 6, 0:E * FT + 4], vec_rows2[:], ident[0:E * FT + 4, 0:E * FT + 4]).then_inc(vec2_ps, 1)
                if t >= 2:
                    turn(t - 2)
            pe.wait_ge(lw_done, 8)
            pe.wait_ge(vec2_done, 1)
            for t in range(TT):
                pe.wait_ge(xnT_done, t + 1)
                if t >= 2:
                    pe.wait_ge(v_done, t - 1)
                for k in range(KC):
                    last = pe.matmul(bank[:, 6 + t % 2, 0:D], xnT[:, k, t * P:(t + 1) * P], wqkvT[:, k, 2 * D:3 * D], start=(k == 0), stop=(k == KC - 1))
                last.then_inc(v_ps, 1)
            pe.wait_ge(y_done, TT)
            for r in range(8):
                if r >= 4:
                    pe.wait_ge(qk_done, r - 3)
                for k in range(KC):
                    last = pe.matmul(bank[:, r % 4], wqkvT[:, k, r // 2 * P:(r // 2 + 1) * P], xnT[:, k, r % 2 * CH:(r % 2 + 1) * CH],
                                     start=(k == 0), stop=(k == KC - 1))
                last.then_inc(qk_ps, 1)
            pe.wait_ge(proj_ld, 16 * AH)

            def feature(n):
                t, q, p = n // FEATS, n // 4 % 2, n % 4 * 2
                if t == 0:
                    pe.wait_ge(qk_done, 2 * (q * 2 + p // 4) + 1)
                elif n == 4 * FEATS:
                    pe.wait_ge(qk_done, 8)
                if n >= 2:
                    pe.wait_ge(f_done, n - 1)
                for g in range(2):
                    last = pe.matmul(bank[:, 5 + n % 2, g * P:(g + 1) * P], feat_w[:, p + g], qkT[:, q * 2 + p // 4, t * P:(t + 1) * P],
                                     start=True, stop=True)
                last.then_inc(f_ps, 1)

            def products(t, q):
                r = 4 * t + q
                if r >= 3:
                    pe.wait_ge(am_done, r - 2)
                if q == 0:
                    pe.wait_ge(f_done, FEATS * (t + 1))
                for u in range(4):
                    p, b = 2 * q + u // 2, u % 2
                    last = pe.matmul(bank[:, r % 3, u * N:(u + 1) * N], feat_k[:, t % 2, p, b], feat_q[:, t % 2, p, b * N:(b + 1) * N],
                                     start=True, stop=True)
                last.then_inc(am_ps, 1)

            def weighted(t, q):
                if t >= 2 and q == 0:
                    pe.wait_ge(att_done, t - 1)
                pe.wait_ge(am_done, 4 * t + q + 1)
                for u in range(4):
                    p, b = 2 * q + u // 2, u % 2
                    w = 2 * (AD + 1)
                    last = pe.matmul(bank[b * N:(b + 1) * N, 3 + t % 2, p * w:(p + 1) * w], am[:, t % 2, q, u], vbd[:, t, b, p],
                                     start=(p == 0), stop=(p == APAIRS - 1), skip_group_check=True)
                if q == 3:
                    last.then_inc(c_ps, 1)

            def turn_att(t):
                pe.wait_ge(att_done, t + 1)
                if t >= 2:
                    pe.wait_ge(logit_done, t - 1)
                for k in range(KC):
                    last = pe.transpose(bank[:, 7, k * P:(k + 1) * P], att[:, t % 2, k * P:(k + 1) * P], ident[:])
                last.then_inc(attT_ps, 1)

            def project(t):
                pe.wait_ge(attT_done, t + 1)
                for k in range(KC):
                    last = pe.matmul(bank[:, 7, 0:D], attT[:, t % 2, k * P:(k + 1) * P], woutT[:, k], start=(k == 0), stop=(k == KC - 1))
                last.then_inc(w_ps, 1)

            def turn_input(t):
                pe.wait_ge(xn_done, TT + t + 1)
                if t < TT - 1:
                    pe.wait_ge(x2_done, t + 2)
                else:
                    pe.wait_ge(logit_done, t)
                for k in range(KC):
                    last = pe.transpose(bank[:, 7, k * P:(k + 1) * P], xn_all[:, 0, t, k * P:(k + 1) * P], ident[:])
                last.then_inc(xfT_ps, 1)

            def logits(t):
                pe.wait_ge(xfT_done, t + 1)
                for k in range(KC):
                    last = pe.matmul(bank[:, 7, 0:E], xfT[:, t % 2, k * P:(k + 1) * P], wg[:, k], start=(k == 0), stop=(k == KC - 1))
                last.then_inc(logit_ps, 1)

            def follow(s, q):
                t, stage = (s - 2, s - 3, s - 3, s - 1)[q], (project, turn_input, logits, turn_att)[q]
                if t >= 0:
                    stage(t)

            def follow_last(i):
                if i < 7:
                    t, stage = ((TT - 3, logits), (TT - 1, turn_att), (TT - 1, project), (TT - 2, turn_input), (TT - 2, logits),
                                (TT - 1, turn_input), (TT - 1, logits))[i]
                    stage(t)

            def rank(t):
                pe.wait_ge(chosen, t + 1)
                pe.matmul(rank_at(t), square[:], picked[:, t], start=True, stop=False, skip_group_check=True)
                if t:
                    pe.wait_ge(prefix_done, t)
                pe.matmul(rank_at(t), ones[:], before[:, t], start=False, stop=True, skip_group_check=True).then_inc(rank_ps, 1)

            pe.wait_ge(v_done, TT)
            pe.wait_ge(lin_consts, 1)
            for n in range(FEATS):
                feature(n)
            pe.wait_ge(qk_done, 8)
            pe.wait_ge(misc_ld, 64)
            for r in range(4 * TT + 2):
                if r < 4 * TT:
                    products(r // 4, r % 4)
                    for n in range(FEATS + 2 * r, FEATS + 2 * r + 2):
                        if n < FEATS * TT:
                            feature(n)
                if r % 4 == 1 and r // 4 >= 4:
                    rank(r // 4 - 4)
                if r >= 2:
                    weighted((r - 2) // 4, (r - 2) % 4)
                follow(r // 4, r % 4)

            for i in range(7):
                follow_last(i)
                if i == 2:
                    rank(TT - 3)
                if i == 5:
                    rank(TT - 2)
            pe.wait_ge(prefix_done, TT)
            pe.matmul(bank[:, 3, 0:E], ones[:], before[:, TT], start=True, stop=True).then_inc(total_ps, 1)
            rank(TT - 1)
            pe.wait_ge(logit_done, TT)
            pe.wait_ge(comb_done, 1)
            for t in range(TT):
                last = pe.transpose(bank[0:E, 4 + t // 4, t % 4 * P:(t % 4 + 1) * P], comb[:, t], ident[:])
                if t % 4 == 3:
                    last.then_inc(combT_ps, 1)
            for t in range(TT):
                pe.wait_ge(combT_done, t // 4 + 1)
                if t >= 4:
                    pe.wait_ge(acc_b2, t - 3)
                pe.matmul(bank[:, (0, 1, 2, 7)[t % 4], 0:D], combT[:, t * P:(t + 1) * P], b2_rows[:], start=True, stop=True).then_inc(b2_ps, 1)

            def rows_turned(r, o):
                pe.wait_ge(xs_ld[o % 2], r * 16 + (o // 2 + 1) * 16)
                for k in range(KC):
                    for c in range(2):
                        last = pe.transpose(bank[:, 6, k * ROWS + c * P:k * ROWS + (c + 1) * P], xs[:, o % 2, c, k * P:(k + 1) * P], ident[:])
                last.then_inc(xs_ps, 1)

            rows_turned(0, 0)
            pe.wait_ge(acc_b2, TT)

            def group(r, o):
                b = o % 2
                wait_group(pe, w1_lo_done, r, 1, o=o)
                wait_group(pe, xs_lo_done, r, 1, o=o)
                for f in range(FT):
                    wait_group(pe, relu_done, r, f - 3, FT, o)
                    prods = [(v, x_, k) for k in range(KC) for v, x_ in ((w1_hi, xs_hi), (w1_hi, xs_lo), (w1_lo, xs_hi))]
                    for m, (v, x_, k) in enumerate(prods):
                        last = pe.matmul(bank[:, f % 4, 0:ROWS], v[:, b, k, f * P:(f + 1) * P], x_[:, k], start=(m == 0), stop=(m == len(prods) - 1))
                    last.then_inc(h_ps, 1)
                if more(r, o):
                    rows_turned(r, o + 1)
                wait_group(pe, w2_lo_done, r, 1, o=o)
                for c in range(2):
                    wait_group(pe, ys_done, r, c - 1, 2, o)
                    for f in range(FT):
                        if c == 0:
                            wait_group(pe, h_lo_done, r, f + 1, FT, o)
                        for m, (v, w) in enumerate(((h_hi, w2_hi), (h_hi, w2_lo), (h_lo, w2_hi))):
                            last = pe.matmul(bank[:, 4 + c, 0:D], v[:, f, c * P:(c + 1) * P], w[:, b, f], start=(f == 0 and m == 0), stop=(f == FT - 1 and m == 2))
                    last.then_inc(e_ps, 1)

            groups(pe, group)


_INS = ['x', 'ctx_1024', 'L0_xattn_cos', 'L0_xattn_sin', 'L0_xattn_ln_lat_g', 'L0_xattn_ln_lat_b', 'L0_xattn_ln_ctx_g',
        'L0_xattn_ln_ctx_b', 'L0_xattn_Wq', 'L0_xattn_Wkv', 'L0_xattn_Wo', 'L0_xattn_bo', 'L0_attn_Wqkv', 'L0_attn_bqkv',
        'L0_attn_Wout', 'L0_attn_bout', 'L0_attn_proj', 'L0_ffn_Wg', 'L0_ffn_W1', 'L0_ffn_b1', 'L0_ffn_W2', 'L0_ffn_b2']
_OUTS = [((16, 64, 256), 'float32')]


def kernel(**inputs):
    import numpy as _np
    import concourse.bacc as _bacc
    from concourse import mybir as _mybir
    from concourse.bass_utils import run_bass_kernel_spmd as _run

    nc = _bacc.Bacc("TRN2", target_bir_lowering=False, num_devices=1)
    arrays, args = {}, []
    for name in _INS:
        a = _np.ascontiguousarray(inputs[name])
        arrays[f"in_{name}_dram"] = a
        args.append(nc.dram_tensor(f"in_{name}_dram", a.shape, _mybir.dt.from_np(a.dtype), kind="ExternalInput").ap())
    for i, (shape, dtype) in enumerate(_OUTS):
        dt = _mybir.dt.from_np(_np.dtype(dtype))
        args.append(nc.dram_tensor(f"out_{i}_dram", shape, dt, kind="ExternalOutput").ap())
    build(nc, *args)
    r = _run(nc, [arrays], core_ids=[0])
    got = tuple(r.results[0][f"out_{i}_dram"] for i in range(len(_OUTS)))
    return got[0]
```
